# Optimizing a Trainium2 kernel written in Bass

```python
import numpy as np
import jax
import jax.numpy as jnp

def _softmax(x, axis=-1):
    return jax.nn.softmax(x, axis=axis)

def _gelu(x):
    return jax.nn.gelu(x, approximate=True)

def _silu(x):
    return jax.nn.silu(x)

def _sigmoid(x):
    return jax.nn.sigmoid(x)

def _layernorm(x, axis=-1, eps=1e-05):
    m = jnp.mean(x, axis=axis, keepdims=True)
    v = jnp.var(x, axis=axis, keepdims=True)
    return (x - m) / jnp.sqrt(v + eps)

def _scatter_add(tgt, idx, src, axis=0):
    return tgt.at[idx].add(src)

def _segment_sum(src, seg, n):
    return jax.ops.segment_sum(src, seg, n)
kernel_name = 'mk_decoder_postln_d2_seqx_r4_4a8cdb'

def setup_inputs(seed: int=0):
    np.random.seed(seed)
    _w = jnp.asarray

    def _rec_inputs():
        import jax
        import jax.numpy as jnp
        _rk = jax.random.key(seed)
        x = -0.0005207 + 1.001 * jax.random.normal(jax.random.fold_in(_rk, 1), (8, 100, 256), jnp.float32)
        _lenS = 100 - jax.random.randint(jax.random.fold_in(_rk, 7), (8,), 0, max(1, 100 // 4) + 1, jnp.int32)
        _lenS2 = 361 - jax.random.randint(jax.random.fold_in(_rk, 8), (8,), 0, max(1, 361 // 4) + 1, jnp.int32)
        _ctx_1024P = jax.random.normal(jax.random.fold_in(_rk, 11), (8, 16, 256), jnp.float32)
        _ctx_1024c = jax.random.dirichlet(jax.random.fold_in(_rk, 511), 0.3 * jnp.ones((16,), jnp.float32), (8, 361))
        _ctx_1024t = jnp.einsum('bsk,bkd->bsd', _ctx_1024c, _ctx_1024P)
        _ctx_1024t = _ctx_1024t * jax.lax.rsqrt(jnp.mean(jnp.square(_ctx_1024t)) + 1e-12) * 0.953939
        ctx_1024 = -0.000514642 + 1.00011 * (_ctx_1024t + 0.3 * jax.random.normal(jax.random.fold_in(_rk, 611), (8, 361, 256), jnp.float32))
        return (x, ctx_1024)
    x, ctx_1024 = _rec_inputs()

    def _L0_attn_setup():
        import jax, jax.numpy as jnp
        import numpy as np
        NUM_HEADS = 1
        LN_EPS = 1e-05
        key = jax.random.key(seed)
        ks = jax.random.split(key, 4)
        B, L, D = (8, 1024, 256)
        x = jax.random.normal(ks[0], (B, L, D), dtype=jnp.float32)
        qkv_w = jax.random.normal(ks[1], (3 * D, D), dtype=jnp.float32) * np.float32(np.sqrt(1.0 / D))
        qkv_b = jnp.zeros((3 * D,), dtype=jnp.float32)
        proj_w = jax.random.normal(ks[2], (D, D), dtype=jnp.float32) * np.float32(np.sqrt(1.0 / D))
        proj_b = jnp.zeros((D,), dtype=jnp.float32)
        return {'x': x, 'norm_w': jnp.ones((D,), dtype=jnp.float32), 'norm_b': jnp.zeros((D,), dtype=jnp.float32), 'qkv_w': qkv_w, 'qkv_b': qkv_b, 'proj_w': proj_w, 'proj_b': proj_b}
    _L0_attn_all = _L0_attn_setup()
    _L0_attn_in = {k: v for k, v in _L0_attn_all.items() if k in ('norm_w', 'norm_b', 'qkv_w', 'qkv_b', 'proj_w', 'proj_b')}
    del _L0_attn_all

    def _L0_xattn_setup():
        import jax, jax.numpy as jnp
        import numpy as np
        EMBED_DIM = 256
        NUM_HEADS = 16
        HEAD_DIM = EMBED_DIM // NUM_HEADS
        WINDOW = 64

        def apply_rope(x):
            B, H, S, d = x.shape
            half = d // 2
            pos = jnp.arange(S, dtype=x.dtype)
            freqs = 1.0 / 10000.0 ** (jnp.arange(half, dtype=x.dtype) / half)
            ang = pos[:, None] * freqs[None, :]
            cos, sin = (jnp.cos(ang), jnp.sin(ang))
            x1, x2 = (x[..., :half], x[..., half:])
            return jnp.concatenate([x1 * cos - x2 * sin, x1 * sin + x2 * cos], axis=-1)

        def _forward(query, key, value, q_w, q_b, k_w, k_b, v_w, v_b, o_w, o_b):
            B, S_q, D = query.shape
            S_k = key.shape[1]
            H, d, W = (NUM_HEADS, HEAD_DIM, WINDOW)
            q = (query @ q_w.T + q_b).reshape(B, S_q, H, d).transpose(0, 2, 1, 3)
            k = (key @ k_w.T + k_b).reshape(B, S_k, H, d).transpose(0, 2, 1, 3)
            v = (value @ v_w.T + v_b).reshape(B, S_k, H, d).transpose(0, 2, 1, 3)
            q = apply_rope(q) * d ** (-0.5)
            k = apply_rope(k)
            q_pos = jnp.arange(S_q)[:, None]
            offsets = jnp.arange(-W, 1)[None, :]
            idx = q_pos + offsets
            local_mask = (idx < 0) | (idx >= S_k)
            gidx = jnp.clip(idx, 0, S_k - 1)
            k_win = k[:, :, gidx, :]
            v_win = v[:, :, gidx, :]
            scores = jnp.einsum('bhqd,bhqwd->bhqw', q, k_win)
            mask = local_mask[None, None, :, :]
            scores = jnp.where(mask, -jnp.inf, scores)
            m = jnp.max(scores, axis=-1, keepdims=True)
            m = jnp.where(jnp.isfinite(m), m, 0.0)
            e = jnp.exp(scores - m)
            denom = jnp.sum(e, axis=-1, keepdims=True)
            probs = jnp.where(denom > 0, e / jnp.where(denom > 0, denom, 1.0), 0.0)
            ctx = jnp.einsum('bhqw,bhqwd->bhqd', probs, v_win)
            ctx = ctx.transpose(0, 2, 1, 3).reshape(B, S_q, D)
            return ctx @ o_w.T + o_b
        key = jax.random.key(seed)
        ks = jax.random.split(key, 12)
        B, S, D = (1, 512, EMBED_DIM)
        scale = 1.0 / np.sqrt(D)
        inp = {'query': jax.random.normal(ks[0], (B, S, D), jnp.float32), 'key': jax.random.normal(ks[1], (B, S, D), jnp.float32), 'value': jax.random.normal(ks[2], (B, S, D), jnp.float32), 'q_w': jax.random.normal(ks[3], (D, D), jnp.float32) * scale, 'q_b': jax.random.normal(ks[4], (D,), jnp.float32) * 0.01, 'k_w': jax.random.normal(ks[5], (D, D), jnp.float32) * scale, 'k_b': jax.random.normal(ks[6], (D,), jnp.float32) * 0.01, 'v_w': jax.random.normal(ks[7], (D, D), jnp.float32) * scale, 'v_b': jax.random.normal(ks[8], (D,), jnp.float32) * 0.01, 'o_w': jax.random.normal(ks[9], (D, D), jnp.float32) * scale, 'o_b': jax.random.normal(ks[10], (D,), jnp.float32) * 0.01}
        return inp
    _L0_xattn_all = _L0_xattn_setup()
    _L0_xattn_in = {k: v for k, v in _L0_xattn_all.items() if k in ('q_w', 'q_b', 'k_w', 'k_b', 'v_w', 'v_b', 'o_w', 'o_b')}
    del _L0_xattn_all

    def _L0_ffn_setup():
        import jax, jax.numpy as jnp
        import numpy as np
        HIDDEN_SIZE = 256
        NUM_EXPERTS = 8
        MOE_INTERMEDIATE_SIZE = 352
        NUM_EXPERTS_PER_TOK = 2
        SHARED_EXPERT_INTERMEDIATE_SIZE = 704
        B, T = (2, 256)
        W_SCALE = 0.02
        key = jax.random.key(seed)
        ks = jax.random.split(key, 8)
        H, E, I, SI = (HIDDEN_SIZE, NUM_EXPERTS, MOE_INTERMEDIATE_SIZE, SHARED_EXPERT_INTERMEDIATE_SIZE)
        return {'x': jax.random.normal(ks[0], (B, T, H), jnp.float32), 'gate_w': jax.random.normal(ks[1], (E, H), jnp.float32) * W_SCALE, 'experts_gate_up': jax.random.normal(ks[2], (E, 2 * I, H), jnp.float32) * W_SCALE, 'experts_down': jax.random.normal(ks[3], (E, H, I), jnp.float32) * W_SCALE, 'shared_gate_w': jax.random.normal(ks[4], (SI, H), jnp.float32) * W_SCALE, 'shared_up_w': jax.random.normal(ks[5], (SI, H), jnp.float32) * W_SCALE, 'shared_down_w': jax.random.normal(ks[6], (H, SI), jnp.float32) * W_SCALE, 'shared_expert_gate_w': jax.random.normal(ks[7], (1, H), jnp.float32) * W_SCALE}
    _L0_ffn_all = _L0_ffn_setup()
    _L0_ffn_in = {k: v for k, v in _L0_ffn_all.items() if k in ('gate_w', 'experts_gate_up', 'experts_down', 'shared_gate_w', 'shared_up_w', 'shared_down_w', 'shared_expert_gate_w')}
    del _L0_ffn_all

    def _L1_attn_setup():
        import jax, jax.numpy as jnp
        import numpy as np
        B, T = (4, 512)
        D_MODEL = 256
        N_HEADS = 8
        HEAD_DIM = 64
        KV_LRANK = 64

        def _orthogonalize_per_head(w):
            chunks = w.reshape(N_HEADS, HEAD_DIM, D_MODEL)

            def ns(m):
                A = m @ m.T
                Bm = 1.5 * jnp.eye(HEAD_DIM, dtype=m.dtype) - 0.5 * A
                return Bm @ m
            return jax.vmap(ns)(chunks).reshape(w.shape)
        key = jax.random.key(seed)
        ks = jax.random.split(key, 6)

        def lin(k, out_dim, in_dim):
            bound = 1.0 / np.sqrt(in_dim)
            return jax.random.uniform(k, (out_dim, in_dim), jnp.float32, -bound, bound)
        Wq = _orthogonalize_per_head(lin(ks[0], N_HEADS * HEAD_DIM, D_MODEL))
        return {'x': jax.random.normal(ks[1], (B, T, D_MODEL), jnp.float32), 'Wq': Wq, 'Wkv_down': lin(ks[2], KV_LRANK, D_MODEL), 'Wk_up': lin(ks[3], N_HEADS * HEAD_DIM, KV_LRANK), 'Wv_up': lin(ks[4], N_HEADS * HEAD_DIM, KV_LRANK), 'Wo': lin(ks[5], D_MODEL, N_HEADS * HEAD_DIM)}
    _L1_attn_all = _L1_attn_setup()
    _L1_attn_in = {k: v for k, v in _L1_attn_all.items() if k in ('Wq', 'Wkv_down', 'Wk_up', 'Wv_up', 'Wo')}
    del _L1_attn_all

    def _L1_xattn_setup():
        import jax, jax.numpy as jnp
        import numpy as np
        E, T, H, F = (8, 512, 256, 1024)
        key = jax.random.key(seed)
        k1, k2, k3 = jax.random.split(key, 3)
        x = jax.random.normal(k1, (E, T, H), dtype=jnp.float32)
        w1 = jax.random.normal(k2, (E, F, H), dtype=jnp.float32) * 0.02
        w2 = jax.random.normal(k3, (E, F, H), dtype=jnp.float32) * 0.02
        return {'x': x, 'w1': w1, 'w2': w2}
    _L1_xattn_all = _L1_xattn_setup()
    _L1_xattn_in = {k: v for k, v in _L1_xattn_all.items() if k in ()}
    del _L1_xattn_all

    def _L1_ffn_setup():
        import jax, jax.numpy as jnp
        import numpy as np
        DIM = 256

        def _reference_tuple_inner(x, W_r, W_k, W_v, mu_r, mu_k):
            B, T, C = x.shape
            x_prev = jnp.concatenate([jnp.zeros((B, 1, C), x.dtype), x[:, :-1, :]], axis=1)
            xr = mu_r * x + (1.0 - mu_r) * x_prev
            xk = mu_k * x + (1.0 - mu_k) * x_prev
            r = jax.nn.sigmoid(jnp.einsum('btc,dc->btd', xr, W_r))
            k = jnp.einsum('btc,dc->btd', xk, W_k)
            k_act = jnp.square(jax.nn.relu(k))
            out = r * jnp.einsum('btc,dc->btd', k_act, W_v)
            new_state = x[:, -1, :]
            return (out, new_state)
        key = jax.random.key(seed)
        ks = jax.random.split(key, 6)
        B, T, C = (8, 512, DIM)
        x = jax.random.normal(ks[0], (B, T, C), dtype=jnp.float32)
        s = 1.0 / np.sqrt(C)
        W_r = jax.random.uniform(ks[1], (C, C), jnp.float32, -s, s)
        W_k = jax.random.uniform(ks[2], (C, C), jnp.float32, -s, s)
        W_v = jax.random.uniform(ks[3], (C, C), jnp.float32, -s, s)
        mu_r = jax.random.uniform(ks[4], (C,), jnp.float32)
        mu_k = jax.random.uniform(ks[5], (C,), jnp.float32)
        return {'x': x, 'W_r': W_r, 'W_k': W_k, 'W_v': W_v, 'mu_r': mu_r, 'mu_k': mu_k}
    _L1_ffn_all = _L1_ffn_setup()
    _L1_ffn_in = {k: v for k, v in _L1_ffn_all.items() if k in ('W_r', 'W_k', 'W_v', 'mu_r', 'mu_k')}
    del _L1_ffn_all
    return {'x': x, 'ctx_1024': ctx_1024, 'L0_attn_norm_w': _L0_attn_in['norm_w'], 'L0_attn_norm_b': _L0_attn_in['norm_b'], 'L0_attn_qkv_w': _L0_attn_in['qkv_w'], 'L0_attn_qkv_b': _L0_attn_in['qkv_b'], 'L0_attn_proj_w': _L0_attn_in['proj_w'], 'L0_attn_proj_b': _L0_attn_in['proj_b'], 'L0_xattn_q_w': _L0_xattn_in['q_w'], 'L0_xattn_q_b': _L0_xattn_in['q_b'], 'L0_xattn_k_w': _L0_xattn_in['k_w'], 'L0_xattn_k_b': _L0_xattn_in['k_b'], 'L0_xattn_v_w': _L0_xattn_in['v_w'], 'L0_xattn_v_b': _L0_xattn_in['v_b'], 'L0_xattn_o_w': _L0_xattn_in['o_w'], 'L0_xattn_o_b': _L0_xattn_in['o_b'], 'L0_ffn_gate_w': _L0_ffn_in['gate_w'], 'L0_ffn_experts_gate_up': _L0_ffn_in['experts_gate_up'], 'L0_ffn_experts_down': _L0_ffn_in['experts_down'], 'L0_ffn_shared_gate_w': _L0_ffn_in['shared_gate_w'], 'L0_ffn_shared_up_w': _L0_ffn_in['shared_up_w'], 'L0_ffn_shared_down_w': _L0_ffn_in['shared_down_w'], 'L0_ffn_shared_expert_gate_w': _L0_ffn_in['shared_expert_gate_w'], 'L1_attn_Wq': _L1_attn_in['Wq'], 'L1_attn_Wkv_down': _L1_attn_in['Wkv_down'], 'L1_attn_Wk_up': _L1_attn_in['Wk_up'], 'L1_attn_Wv_up': _L1_attn_in['Wv_up'], 'L1_attn_Wo': _L1_attn_in['Wo'], 'L1_ffn_W_r': _L1_ffn_in['W_r'], 'L1_ffn_W_k': _L1_ffn_in['W_k'], 'L1_ffn_W_v': _L1_ffn_in['W_v'], 'L1_ffn_mu_r': _L1_ffn_in['mu_r'], 'L1_ffn_mu_k': _L1_ffn_in['mu_k']}

def reference(x, ctx_1024, L0_attn_norm_w, L0_attn_norm_b, L0_attn_qkv_w, L0_attn_qkv_b, L0_attn_proj_w, L0_attn_proj_b, L0_xattn_q_w, L0_xattn_q_b, L0_xattn_k_w, L0_xattn_k_b, L0_xattn_v_w, L0_xattn_v_b, L0_xattn_o_w, L0_xattn_o_b, L0_ffn_gate_w, L0_ffn_experts_gate_up, L0_ffn_experts_down, L0_ffn_shared_gate_w, L0_ffn_shared_up_w, L0_ffn_shared_down_w, L0_ffn_shared_expert_gate_w, L1_attn_Wq, L1_attn_Wkv_down, L1_attn_Wk_up, L1_attn_Wv_up, L1_attn_Wo, L1_ffn_W_r, L1_ffn_W_k, L1_ffn_W_v, L1_ffn_mu_r, L1_ffn_mu_k):
    import jax
    import jax.numpy as jnp

    def _L0_attn_ref(x, norm_w, norm_b, qkv_w, qkv_b, proj_w, proj_b):
        import jax, jax.numpy as jnp
        import numpy as np
        NUM_HEADS = 1
        LN_EPS = 1e-05
        B, L, D = x.shape
        H = NUM_HEADS
        mu = jnp.mean(x, axis=-1, keepdims=True)
        var = jnp.mean(jnp.square(x - mu), axis=-1, keepdims=True)
        h = (x - mu) / jnp.sqrt(var + LN_EPS) * norm_w + norm_b
        qkv = h @ qkv_w.T + qkv_b
        qkv = qkv.reshape(B * H, L // H, 3, D)
        q, k, v = (qkv[..., 0, :], qkv[..., 1, :], qkv[..., 2, :])
        scale = np.float32(1.0 / np.sqrt(L // H))
        w = jax.nn.softmax(jnp.einsum('ncq,nck->nqk', q, k * scale), axis=2)
        a = jnp.einsum('nqk,nck->ncq', w, v)
        a = a.reshape(B, L, D)
        return a @ proj_w.T + proj_b + x

    def _L0_xattn_ref(query, key, value, q_w, q_b, k_w, k_b, v_w, v_b, o_w, o_b):
        import jax, jax.numpy as jnp
        import numpy as np
        EMBED_DIM = 256
        NUM_HEADS = 16
        HEAD_DIM = EMBED_DIM // NUM_HEADS
        WINDOW = 64

        def apply_rope(x):
            B, H, S, d = x.shape
            half = d // 2
            pos = jnp.arange(S, dtype=x.dtype)
            freqs = 1.0 / 10000.0 ** (jnp.arange(half, dtype=x.dtype) / half)
            ang = pos[:, None] * freqs[None, :]
            cos, sin = (jnp.cos(ang), jnp.sin(ang))
            x1, x2 = (x[..., :half], x[..., half:])
            return jnp.concatenate([x1 * cos - x2 * sin, x1 * sin + x2 * cos], axis=-1)

        def _forward(query, key, value, q_w, q_b, k_w, k_b, v_w, v_b, o_w, o_b):
            B, S_q, D = query.shape
            S_k = key.shape[1]
            H, d, W = (NUM_HEADS, HEAD_DIM, WINDOW)
            q = (query @ q_w.T + q_b).reshape(B, S_q, H, d).transpose(0, 2, 1, 3)
            k = (key @ k_w.T + k_b).reshape(B, S_k, H, d).transpose(0, 2, 1, 3)
            v = (value @ v_w.T + v_b).reshape(B, S_k, H, d).transpose(0, 2, 1, 3)
            q = apply_rope(q) * d ** (-0.5)
            k = apply_rope(k)
            q_pos = jnp.arange(S_q)[:, None]
            offsets = jnp.arange(-W, 1)[None, :]
            idx = q_pos + offsets
            local_mask = (idx < 0) | (idx >= S_k)
            gidx = jnp.clip(idx, 0, S_k - 1)
            k_win = k[:, :, gidx, :]
            v_win = v[:, :, gidx, :]
            scores = jnp.einsum('bhqd,bhqwd->bhqw', q, k_win)
            mask = local_mask[None, None, :, :]
            scores = jnp.where(mask, -jnp.inf, scores)
            m = jnp.max(scores, axis=-1, keepdims=True)
            m = jnp.where(jnp.isfinite(m), m, 0.0)
            e = jnp.exp(scores - m)
            denom = jnp.sum(e, axis=-1, keepdims=True)
            probs = jnp.where(denom > 0, e / jnp.where(denom > 0, denom, 1.0), 0.0)
            ctx = jnp.einsum('bhqw,bhqwd->bhqd', probs, v_win)
            ctx = ctx.transpose(0, 2, 1, 3).reshape(B, S_q, D)
            return ctx @ o_w.T + o_b
        return _forward(query, key, value, q_w, q_b, k_w, k_b, v_w, v_b, o_w, o_b)

    def _L0_ffn_ref(x, gate_w, experts_gate_up, experts_down, shared_gate_w, shared_up_w, shared_down_w, shared_expert_gate_w):
        import jax, jax.numpy as jnp
        import numpy as np
        HIDDEN_SIZE = 256
        NUM_EXPERTS = 8
        MOE_INTERMEDIATE_SIZE = 352
        NUM_EXPERTS_PER_TOK = 2
        SHARED_EXPERT_INTERMEDIATE_SIZE = 704
        B, T = (2, 256)
        W_SCALE = 0.02
        Bx, Tx, H = x.shape
        E = gate_w.shape[0]
        I = experts_down.shape[2]
        x_flat = x.reshape(Bx * Tx, H)
        logits = x_flat @ gate_w.T
        scores = jax.nn.softmax(logits, axis=-1)
        _, topk_ids = jax.lax.top_k(scores, NUM_EXPERTS_PER_TOK)
        in_topk = jax.nn.one_hot(topk_ids, E, dtype=x.dtype).sum(axis=1)
        w = scores * in_topk
        gu = jnp.einsum('nh,eih->nei', x_flat, experts_gate_up)
        g, u = (gu[..., :I], gu[..., I:])
        h = jax.nn.silu(g) * u
        expert_out = jnp.einsum('nei,ehi->neh', h, experts_down)
        out = jnp.einsum('neh,ne->nh', expert_out, w)
        shared = jax.nn.silu(x_flat @ shared_gate_w.T) * (x_flat @ shared_up_w.T) @ shared_down_w.T
        shared_weight = jax.nn.sigmoid(x_flat @ shared_expert_gate_w.T)
        out = out + shared_weight * shared
        return out.reshape(Bx, Tx, H)

    def _L1_attn_ref(x, Wq, Wkv_down, Wk_up, Wv_up, Wo):
        import jax, jax.numpy as jnp
        import numpy as np
        B, T = (4, 512)
        D_MODEL = 256
        N_HEADS = 8
        HEAD_DIM = 64
        KV_LRANK = 64

        def _orthogonalize_per_head(w):
            chunks = w.reshape(N_HEADS, HEAD_DIM, D_MODEL)

            def ns(m):
                A = m @ m.T
                Bm = 1.5 * jnp.eye(HEAD_DIM, dtype=m.dtype) - 0.5 * A
                return Bm @ m
            return jax.vmap(ns)(chunks).reshape(w.shape)
        b, t, _ = x.shape
        q = (x @ Wq.T).reshape(b, t, N_HEADS, HEAD_DIM)
        kv_latent = x @ Wkv_down.T
        k = (kv_latent @ Wk_up.T).reshape(b, t, N_HEADS, HEAD_DIM)
        v = (kv_latent @ Wv_up.T).reshape(b, t, N_HEADS, HEAD_DIM)
        scale = HEAD_DIM ** (-0.5)
        scores = jnp.einsum('bqhd,bkhd->bhqk', q, k) * scale
        attn = jax.nn.softmax(scores, axis=-1)
        out = jnp.einsum('bhqk,bkhd->bqhd', attn, v)
        out = out.reshape(b, t, N_HEADS * HEAD_DIM)
        return out @ Wo.T

    def _L1_xattn_ref(x, w1, w2):
        import jax, jax.numpy as jnp
        import numpy as np
        E, T, H, F = (8, 512, 256, 1024)
        h = jnp.einsum('eth,efh->etf', x, w1)
        a = jax.nn.gelu(h, approximate=True)
        return jnp.einsum('etf,efh->eth', a, w2)

    def _L1_ffn_ref(x, W_r, W_k, W_v, mu_r, mu_k):
        import jax, jax.numpy as jnp
        import numpy as np
        DIM = 256

        def _reference_tuple_inner(x, W_r, W_k, W_v, mu_r, mu_k):
            B, T, C = x.shape
            x_prev = jnp.concatenate([jnp.zeros((B, 1, C), x.dtype), x[:, :-1, :]], axis=1)
            xr = mu_r * x + (1.0 - mu_r) * x_prev
            xk = mu_k * x + (1.0 - mu_k) * x_prev
            r = jax.nn.sigmoid(jnp.einsum('btc,dc->btd', xr, W_r))
            k = jnp.einsum('btc,dc->btd', xk, W_k)
            k_act = jnp.square(jax.nn.relu(k))
            out = r * jnp.einsum('btc,dc->btd', k_act, W_v)
            new_state = x[:, -1, :]
            return (out, new_state)
        return _reference_tuple_inner(x, W_r, W_k, W_v, mu_r, mu_k)[0]
    x = _layernorm(x + _L0_attn_ref(x, L0_attn_norm_w, L0_attn_norm_b, L0_attn_qkv_w, L0_attn_qkv_b, L0_attn_proj_w, L0_attn_proj_b), axis=-1)
    x = _layernorm(x + _L0_xattn_ref(x, ctx_1024, ctx_1024, L0_xattn_q_w, L0_xattn_q_b, L0_xattn_k_w, L0_xattn_k_b, L0_xattn_v_w, L0_xattn_v_b, L0_xattn_o_w, L0_xattn_o_b), axis=-1)
    x = _layernorm(x + _L0_ffn_ref(x, L0_ffn_gate_w, L0_ffn_experts_gate_up, L0_ffn_experts_down, L0_ffn_shared_gate_w, L0_ffn_shared_up_w, L0_ffn_shared_down_w, L0_ffn_shared_expert_gate_w), axis=-1)
    x = _layernorm(x + _L1_attn_ref(x, L1_attn_Wq, L1_attn_Wkv_down, L1_attn_Wk_up, L1_attn_Wv_up, L1_attn_Wo), axis=-1)
    x = _layernorm(x + _L1_xattn_ref(x, ctx_1024, ctx_1024), axis=-1)
    x = _layernorm(x + _L1_ffn_ref(x, L1_ffn_W_r, L1_ffn_W_k, L1_ffn_W_v, L1_ffn_mu_r, L1_ffn_mu_k), axis=-1)
    return x

_drawn_inputs = setup_inputs


def setup_inputs(seed=0):
    import zlib

    import numpy as np

    out = dict(_drawn_inputs(seed))
    spreads = {'L0_attn_norm_w': (1.0, 0.2),
     'L0_attn_norm_b': (0.0, 0.404),
     'L0_attn_qkv_b': (0.0, 0.455),
     'L0_attn_proj_b': (0.0, 0.1)}
    factors = {'L0_xattn_q_b': 8.0,
     'L0_xattn_k_b': 8.0,
     'L0_xattn_v_b': 8.0,
     'L0_xattn_o_b': 8.0,
     'L0_ffn_gate_w': 8.0,
     'L0_ffn_experts_gate_up': 8.0,
     'L0_ffn_experts_down': 8.0,
     'L0_ffn_shared_gate_w': 5.78,
     'L0_ffn_shared_up_w': 5.957,
     'L0_ffn_shared_down_w': 5.749,
     'L0_ffn_shared_expert_gate_w': 8.0,
     'L1_attn_Wq': 8.0,
     'L1_attn_Wk_up': 8.0,
     'L1_ffn_mu_r': 8.0}
    for name, (base, spread) in spreads.items():
        noise = np.random.default_rng([zlib.crc32(name.encode()), seed]).standard_normal(out[name].shape)
        drawn = base * np.exp(spread * noise) if base else spread * noise
        out[name] = jnp.asarray(drawn.astype(out[name].dtype))
    for name, factor in factors.items():
        out[name] = (out[name] * factor).astype(out[name].dtype)
    return out
```

```python
from contextlib import ExitStack

import numpy as np

import concourse.bass as bass
from concourse import mybir

F32, F32R, BF16 = mybir.dt.float32, mybir.dt.float32r, mybir.dt.bfloat16
ACT = mybir.ActivationFunctionType
ALU = mybir.AluOpType
X_AXIS = mybir.AxisListType.X

B, S, D = 8, 100, 256
SK = 361
P = 128
KC = D // P
N = B * S
HB = B // 2
HN = HB * S
H0, D0, WINDOW = 16, 16, 64
HC = P // D0
QH = 4
E, I, TOPK = 8, 352, 2
SI = 704
GROUPS = E + SI // I
MC = -(-I // P)
ROWS = [min(P, I - m * P) for m in range(MC)]
UNITS = MC * 2
PAIR = 2 * UNITS
NU = GROUPS * UNITS
H1, D1, R1 = 8, 64, 64
QC = H1 * D1 // P
FC = -(-SK // P)
FROWS = [min(P, SK - f * P) for f in range(FC)]
EPS = 1e-5
MASKED = -3e38
SCALE0 = float(np.float32(1.0 / np.sqrt(S)))


def build(nc, I_, out):
    ctx = ExitStack()
    with ctx:
        def sb(name, shape, dt=F32, where=ctx):
            return where.enter_context(nc.sbuf_tensor(name, shape, dt))

        def sem(name):
            return ctx.enter_context(nc.semaphore(name))

        X = sb("X", [P, B, D])
        XN = sb("XN", [P, B, D])
        RES = sb("RES", [P, B, D])
        T0 = sb("T0", [P, KC, N])
        T1 = sb("T1", [P, KC, N])
        ident = sb("ident", [P, P])
        stats = sb("stats", [P, B, 6])
        mv = sb("mv", [P, B, 2])
        lnv = sb("lnv", [P, B])
        rstd = sb("rstd", [P, B])
        epsb = sb("epsb", [P, 1])
        zero16 = sb("zero16", [P, HN], BF16)

        work = ExitStack()
        w_gu = sb("w_gu", [P, KC, 2 * I], F32, work)
        w_dn = sb("w_dn", [P, MC, D], F32, work)
        gu_hi = [sb(f"gu_hi{s}", [P, KC, 2 * I], F32R, work) for s in range(2)]
        gu_lo = [sb(f"gu_lo{s}", [P, KC, 2 * I], F32R, work) for s in range(2)]
        dn_hi = [sb(f"dn_hi{s}", [P, MC, D], F32R, work) for s in range(2)]
        dn_lo = [sb(f"dn_lo{s}", [P, MC, D], F32R, work) for s in range(2)]

        with ExitStack() as r:
            qk = sb("qk", [P, B, 2 * D], F32, r)
            vT = sb("vT", [P, KC, N], F32, r)
            e0 = sb("e0", [P, 4, KC, D], F32, r)
            eT0 = sb("eT0", [P, 4, KC, D], F32, r)
            aT = sb("aT", [P, B, KC, S], F32, r)
        with ExitStack() as r:
            kblk = sb("kblk", [P, 4, HC, S], F32, r)
            e1 = sb("e1", [P, 4, QH, S], F32, r)
            eT1 = sb("eT1", [P, 4, QH, S], F32, r)
            ctxn = sb("ctxn", [P, B, D], F32, r)
            ctxnT = sb("ctxnT", [P, KC, N], F32, r)
        with ExitStack() as r:
            wb = sb("wb", [P, GROUPS, N], F32, r)
            x_hi = sb("x_hi", [P, KC, N], F32R, r)
            x_lo = sb("x_lo", [P, KC, N], F32R, r)
        sb("place1", [P, B * 2 * D + 2 * KC * N + 8 * KC * D], F32, work)

        with ExitStack() as r:
            kr = sb("kr", [P, KC, N], F32, r)
            qr = sb("qr", [P, KC, N], F32, r)
            rot = sb("rot", [P, 2, 2, HN], F32, r)
            cA = sb("cA", [P, KC, N], F32, r)
            vaug = sb("vaug", [P, B, H0, D0 + 1], F32, r)
            qkvT = sb("qkvT", [P, KC, 3 * D], F32, r)
            projT = sb("projT", [P, KC, D], F32, r)
            xqT = sb("xqT", [P, KC, 2 * D], F32, r)
            xkT = sb("xkT", [P, KC, 2 * D], F32, r)
            xvT = sb("xvT", [P, KC, D], F32, r)
            xoT = sb("xoT", [P, KC, D], F32, r)
            qk_b = sb("qk_b", [P, 2 * D], F32, r)
            proj_b = sb("proj_b", [P, D], F32, r)
            xv_b = sb("xv_b", [P, D], F32, r)
            xo_b = sb("xo_b", [P, D], F32, r)
            colb = sb("colb", [P, 14], F32, r)
            rope = sb("rope", [P, 2, S], F32, r)
            hmask = sb("hmask", [P, HC], F32, r)
            identb = sb("identb", [P, P], BF16, r)
            maskb = sb("maskb", [P, QH * S], BF16, r)
            gateT = sb("gateT", [P, KC, E + 1], F32, r)
            max0 = sb("max0", [P, B, KC], F32, r)
            nb0 = sb("nb0", [P, B, KC], F32, r)
            sum0 = sb("sum0", [P, B, KC], F32, r)
            rs0 = sb("rs0", [P, B, KC], F32, r)
            max1 = sb("max1", [P, 8 * B * H0 // 8], F32, r)
            rs1 = sb("rs1", [P, B, H0], F32, r)
            gmax = sb("gmax", [P, B], F32, r)
            gexp = sb("gexp", [P, B, E + 1], F32, r)
            gsum = sb("gsum", [P, B], F32, r)
            grs = sb("grs", [P, B], F32, r)
            score = sb("score", [P, B, 2 * E], F32, r)
            top = sb("top", [P, B, 8], F32, r)
            picked = sb("picked", [P, B, 2 * E], F32, r)
            wtm = sb("wtm", [P, B, GROUPS], F32, r)
            sig1 = sb("sig1", [P, B], F32, r)
        with ExitStack() as r:
            sg = sb("sg", [P, 2, HN], F32, r)
            hu = sb("hu", [P, 2, HN], F32, r)
            hw = sb("hw", [P, 2, HN], F32, r)
            h_hi = [sb(f"h_hi{s}", [P, HN], F32R, r) for s in range(3)]
            h_lo = [sb(f"h_lo{s}", [P, HN], F32R, r) for s in range(3)]
        sb("rings", [P, 12 * HN], F32, work)
        with ExitStack() as r:
            wqT = sb("wqT", [P, KC, H1 * D1], F32, r)
            wkdT = sb("wkdT", [P, KC, R1], F32, r)
            wkuT = sb("wkuT", [R1, H1 * D1], F32, r)
            wvuT = sb("wvuT", [R1, H1 * D1], F32, r)
            woT = sb("woT", [P, QC, D], F32, r)
            wrT = sb("wrT", [P, KC, D], F32, r)
            wkT = sb("wkT", [P, KC, D], F32, r)
            wvT = sb("wvT", [P, KC, D], F32, r)
            mu = sb("mu", [P, 2, KC], F32, r)
            omm = sb("omm", [P, 2, KC], F32, r)
            cN = sb("cN", [P, B, FC, D], F32, r)
            max2 = sb("max2", [P, B * H1], F32, r)
            rs2 = sb("rs2", [P, B * H1], F32, r)
        work.close()

        with ExitStack() as r:
            q1T = sb("q1T", [P, QC, N], F32, r)
            k1T = sb("k1T", [P, QC, N], F32, r)
            latT = sb("latT", [R1, N], F32, r)
            e2 = sb("e2", [P, 4, QH, S], F32, r)
            eT2 = sb("eT2", [P, 4, QH, S], F32, r)
            v1 = sb("v1", [P, B, H1, D1 + 1], F32, r)
            a1 = sb("a1", [P, B, H1 * D1], F32, r)
            a1T = sb("a1T", [P, 4, QC, S], F32, r)
            cT = sb("cT", [P, KC, B, SK], F32, r)
        with ExitStack() as r:
            fT = sb("fT", [P, KC, N], F32, r)
        with ExitStack() as r:
            gT = sb("gT", [P, B, FC, S], F32, r)
            pad = sb("pad", [P, KC, B, S + 1], F32, r)
            mix = sb("mix", [P, 2, KC, N], F32, r)
            mixt = sb("mixt", [P, 2, HN], F32, r)
            kpos = sb("kpos", [P, 2, HN], F32, r)
            ksq = sb("ksq", [P, KC, N], F32, r)
            rec = sb("rec", [P, 2, 2, D], F32, r)

        PB = [ctx.enter_context(nc.psum_tensor(f"PB{i}", [P, 512], F32)) for i in range(8)]

        ld_x, ld_a, ld_k, ld_b, ld_w, ld_c, ld_ct = [
            sem("ld_" + n) for n in ("x", "a", "k", "b", "w", "c", "ct")]
        ones_set, zero_set, sent_set = sem("ones_set"), sem("zero_set"), sem("sent_set")
        ln_st, ln_mv, ln_lg, ln_rs, ln_out = [sem("ln_" + n) for n in ("st", "mv", "lg", "rs", "out")]
        twice = sem("twice")
        summed = sem("summed")
        resid = sem("resid")
        hT_ps, hT_ready = sem("hT_ps"), sem("hT_ready")
        qk_ps, qk_ready = sem("qk_ps"), sem("qk_ready")
        vT_ps, vT_ready = sem("vT_ps"), sem("vT_ready")
        kp_ps, k_rot, kr_ready = sem("kp_ps"), sem("k_rot"), sem("kr_ready")
        v_ps, v_ready = sem("v_ps"), sem("v_ready")
        s0_ps, s0_max, s0_nb, s0_exp, s0_rs = [sem("s0_" + n) for n in ("ps", "max", "nb", "exp", "rs")]
        eT0_ps, eT0_ready = sem("eT0_ps"), sem("eT0_ready")
        aT_ps, aT_ready = sem("aT_ps"), sem("aT_ready")
        y1_ps = sem("y1_ps")
        x1T_ps, x1T_ready = sem("x1T_ps"), sem("x1T_ready")
        qp_ps, q_rot, qr_ready = sem("qp_ps"), sem("q_rot"), sem("qr_ready")
        kblk_ready = sem("kblk_ready")
        s1_ps, s1_max, s1_sub, s1_exp = [sem("s1_" + n) for n in ("ps", "max", "sub", "exp")]
        eT1_ps, eT1_ready = sem("eT1_ps"), sem("eT1_ready")
        c1_ps, c1_rs, c1_ready = sem("c1_ps"), sem("c1_rs"), sem("c1_ready")
        cT1_ps, cT1_ready = sem("cT1_ps"), sem("cT1_ready")
        y2_ps = sem("y2_ps")
        x2T_ps, x2T_ready = sem("x2T_ps"), sem("x2T_ready")
        xhi_ready, xlo_ready = sem("xhi_ready"), sem("xlo_ready")
        g_ps, g_step, g_exp, wtm_ready = sem("g_ps"), sem("g_step"), sem("g_exp"), sem("wtm_ready")
        wb_ps, wb_ready = sem("wb_ps"), sem("wb_ready")
        gu_hi_ready, gu_lo_ready = sem("gu_hi_ready"), sem("gu_lo_ready")
        dn_hi_ready, dn_lo_ready = sem("dn_hi_ready"), sem("dn_lo_ready")
        gu_ps, silu_ready, hu_ready, hw_ready = sem("gu_ps"), sem("silu_ready"), sem("hu_ready"), sem("hw_ready")
        hhi_ready, hlo_ready, down_done = sem("hhi_ready"), sem("hlo_ready"), sem("down_done")
        load_turn, weigh_turn = sem("load_turn"), sem("weigh_turn")
        fT_ready = sem("fT_ready")
        y3_ps = sem("y3_ps")
        x3T_ps, x3T_ready = sem("x3T_ps"), sem("x3T_ready")
        lat_ps, lat_ready = sem("lat_ps"), sem("lat_ready")
        q1_ps, q1_ready = sem("q1_ps"), sem("q1_ready")
        v1_ps, v1_ready, one1_set = sem("v1_ps"), sem("v1_ready"), sem("one1_set")
        s2_ps, s2_max, s2_sub, s2_exp = [sem("s2_" + n) for n in ("ps", "max", "sub", "exp")]
        eT2_ps, eT2_ready = sem("eT2_ps"), sem("eT2_ready")
        c2_ps, c2_rs, c2_ready = sem("c2_ps"), sem("c2_rs"), sem("c2_ready")
        a1T_ps, a1T_ready = sem("a1T_ps"), sem("a1T_ready")
        y4_ps = sem("y4_ps")
        x4T_ps, x4T_ready = sem("x4T_ps"), sem("x4T_ready")
        g4_ps, gelu_ready = sem("g4_ps"), sem("gelu_ready")
        y5_ps = sem("y5_ps")
        x5T_ps, pad_ready, pad_zero = sem("x5T_ps"), sem("pad_ready"), sem("pad_zero")
        omm_ready, mixt_ready, mix_ready = sem("omm_ready"), sem("mixt_ready"), sem("mix_ready")
        kk_ps, kpos_ready, ksq_ready = sem("kk_ps"), sem("kpos_ready"), sem("ksq_ready")
        gated = sem("gated")
        r_ps, rexp_ready, r_step, y6_ps = sem("r_ps"), sem("rexp_ready"), sem("r_step"), sem("y6_ps")
        stored = sem("stored")

        def tok(b):
            return slice(b * S, (b + 1) * S)

        def half(h):
            return slice(h * HN, (h + 1) * HN)

        def heads(ap):
            return ap.rearrange("p (j s) -> p j s", s=S)

        def tripled(a, b):
            return [(a[0], b[0]), (a[0], b[1]), (a[1], b[0])]

        block = ctx.enter_context(nc.Block())

        @block.sync
        def _(sp):
            def rows(name):
                return I_[name].rearrange("(k p) n -> p k n", p=P)

            def all_rows(name, width):
                return I_[name].rearrange("(o n) -> o n", o=1).broadcast_to([S, width])

            sp.dma_start(X[0:S], I_["x"].rearrange("b s d -> s b d")).then_inc(ld_x, 16)
            sp.dma_start(ident[:], I_["ident"]).then_inc(ld_a, 16)
            sp.dma_start(colb[:], I_["colb"]).then_inc(ld_a, 16)
            sp.dma_start(qkvT[:], rows("qkvT")).then_inc(ld_a, 16)
            sp.dma_start(qk_b[0:S], all_rows("qk_b", 2 * D)).then_inc(ld_a, 16)
            sp.dma_start(cA[:], rows("cA")).then_inc(ld_k, 16)
            sp.dma_start(xkT[:], rows("xkT")).then_inc(ld_k, 16)
            sp.dma_start(xvT[:], rows("xvT")).then_inc(ld_k, 16)
            sp.dma_start(xv_b[0:S], all_rows("xv_b", D)).then_inc(ld_k, 16)
            sp.dma_start(rope[:], I_["rope"]).then_inc(ld_k, 16)
            sp.dma_start(proj_b[0:S], all_rows("proj_b", D)).then_inc(ld_b, 16)
            sp.dma_start(projT[:], rows("projT")).then_inc(ld_b, 16)
            sp.dma_start(xqT[:], rows("xqT")).then_inc(ld_b, 16)
            sp.dma_start(hmask[:], I_["hmask"]).then_inc(ld_b, 16)
            sp.dma_start(identb[:], I_["identb"]).then_inc(ld_b, 16)
            sp.dma_start(maskb[0:S], I_["maskb"]).then_inc(ld_b, 16)
            sp.dma_start(xoT[:], rows("xoT")).then_inc(ld_b, 16)
            sp.dma_start(xo_b[0:S], all_rows("xo_b", D)).then_inc(ld_b, 16)
            sp.dma_start(gateT[:], rows("gateT")).then_inc(ld_b, 16)

            def load_group(g):
                gu = I_["guT"].rearrange("g (k p) n -> p g k n", p=P)
                sp.dma_start(w_gu[:], gu[:, bass.ds(g, 1)].rearrange("p g k n -> p (g k) n")).then_inc(ld_w, 16)
                full = (MC - 1) * P
                dn = I_["dnT"][:, 0:full, :].rearrange("g (m p) n -> p g m n", p=P)
                sp.dma_start(w_dn[:, 0:MC - 1], dn[:, bass.ds(g, 1)].rearrange("p g m n -> p (g m) n")).then_inc(ld_w, 16)
                tail = I_["dnT"][:, full:I, :].rearrange("g p n -> p g n")
                sp.dma_start(w_dn[0:I - full, MC - 1:MC], tail[:, bass.ds(g, 1)]).then_inc(ld_w, 16)

            load_group(0)
            sp.wait_ge(gu_hi_ready, 1)
            sp.wait_ge(gu_lo_ready, 2)
            sp.wait_ge(dn_hi_ready, 1)
            sp.wait_ge(dn_lo_ready, 2)
            load_group(1)
            sp.wait_ge(wb_ready, 3 * B)
            sp.wait_ge(xlo_ready, B)
            sp.dma_start(wqT[:], rows("wqT")).then_inc(ld_c, 16)
            sp.dma_start(wkdT[:], rows("wkdT")).then_inc(ld_c, 16)
            sp.dma_start(wkuT[:], I_["wkuT"]).then_inc(ld_c, 16)
            sp.dma_start(wvuT[:], I_["wvuT"]).then_inc(ld_c, 16)
            sp.dma_start(woT[:], rows("woT")).then_inc(ld_c, 16)
            sp.dma_start(wrT[:], rows("wrT")).then_inc(ld_c, 16)
            sp.dma_start(wkT[:], rows("wkT")).then_inc(ld_c, 16)
            sp.dma_start(wvT[:], rows("wvT")).then_inc(ld_c, 16)
            sp.dma_start(mu[:], I_["mu"].rearrange("p (a k) -> p a k", a=2)).then_inc(ld_c, 16)
            with sp.Fori(2, GROUPS) as g:
                parts = sp.snap(g * 2)
                sp.wait_ge(gu_lo_ready, parts)
                sp.wait_ge(dn_lo_ready, parts)
                sp.wait_ge(gu_hi_ready, g)
                sp.wait_ge(dn_hi_ready, g)
                sp.sem_inc(load_turn, 1)
                load_group(g)
            cf = (FC - 1) * P
            for b in range(B):
                sp.dma_start(cN[:, b, 0:FC - 1], I_["cN"][b, 0:cf].rearrange("(f p) d -> p f d", p=P)).then_inc(ld_c, 16)
            sp.dma_start(cN[0:SK - cf, :, FC - 1], I_["cN"][:, cf:SK].rearrange("b p d -> p b d")).then_inc(ld_c, 16)
            sp.wait_ge(fT_ready, 4)
            sp.dma_start(cT[:], I_["cT"].rearrange("(k p) b n -> p k b n", p=P)).then_inc(ld_ct, 16)
            for b in range(B):
                sp.wait_ge(ln_out, 6 * B + b + 1)
                sp.dma_start(out[b], X[0:S, b]).then_inc(stored, 16)
            sp.wait_ge(stored, 16 * B)
        LD_A, LD_K, LD_B, LD_W, LD_C = 4 * 16, 5 * 16, 9 * 16, 3 * 16, (9 + B + 1) * 16

        @block.tensor
        def _(pe):
            mm = nc.tensor.matmul

            def to_cm(src, bank, b):
                for k in range(KC):
                    last = nc.tensor.transpose(bank[:, k * S:(k + 1) * S], src[0:S, b, k * P:(k + 1) * P], ident[0:S, 0:S])
                return last

            def product(out_, pairs):
                for n, (a, m) in enumerate(pairs):
                    last = mm(out_, a, m, start=(n == 0), stop=(n == len(pairs) - 1))
                return last

            pe.wait_ge(ld_a, LD_A)
            for b in range(B):
                pe.wait_ge(ln_out, b + 1)
                if b >= 2:
                    pe.wait_ge(hT_ready, b - 1)
                to_cm(XN, PB[b % 2], b).then_inc(hT_ps, 1)
            for b in range(B):
                pe.wait_ge(hT_ready, b + 1)
                if b >= 2:
                    pe.wait_ge(qk_ready, b - 1)
                product(PB[2 + b % 2][0:S, :], [(T0[:, k, tok(b)], qkvT[:, k, 0:2 * D]) for k in range(KC)]).then_inc(qk_ps, 1)
            for h in range(2):
                for m in range(KC):
                    if h:
                        pe.wait_ge(vT_ready, m + 1)
                    product(PB[4 + m][:, 0:HN], [(qkvT[:, k, 2 * D + m * P:2 * D + (m + 1) * P], T0[:, k, half(h)])
                                                 for k in range(KC)]).then_inc(vT_ps, 1)
            pe.wait_ge(ld_k, LD_K)
            for n, (h, m) in enumerate([(h, m) for h in range(2) for m in range(KC)]):
                if n:
                    pe.wait_ge(k_rot, 2 * n)
                for sw in range(2):
                    last = product(PB[6 + sw][:, 0:HN], [(xkT[:, k, sw * D + m * P:sw * D + (m + 1) * P], cA[:, k, half(h)])
                                                         for k in range(KC)])
                last.then_inc(kp_ps, 1)
            for b in range(B):
                if b < 2:
                    pe.wait_ge(vT_ready, 4)
                else:
                    pe.wait_ge(v_ready, b - 1)
                product(PB[4 + b % 2][0:S, 0:D], [(cA[:, k, tok(b)], xvT[:, k, :]) for k in range(KC)]).then_inc(v_ps, 1)
            def scores0(b):
                if b < 2:
                    pe.wait_ge(k_rot, 8)
                else:
                    pe.wait_ge(s0_exp, b - 1)
                pe.wait_ge(qk_ready, b + 1)
                for q in range(KC):
                    last = product(PB[6 + b % 2][:, q * D:(q + 1) * D], [(qk[0:S, b, q * P:(q + 1) * P], qk[0:S, b, D:2 * D])])
                last.then_inc(s0_ps, 1)

            def transposes0(b):
                if b < 2:
                    pe.wait_ge(hT_ready, B)
                else:
                    pe.wait_ge(eT0_ready, b - 1)
                pe.wait_ge(s0_exp, b + 1)
                for k in range(KC):
                    for q in range(KC):
                        last = nc.tensor.transpose(PB[b % 2][:, k * D + q * P:k * D + (q + 1) * P],
                                                   e0[:, b % 4, q, k * P:(k + 1) * P], ident[:])
                last.then_inc(eT0_ps, 1)

            def values0(b):
                if b < 2:
                    pe.wait_ge(qk_ready, B)
                else:
                    pe.wait_ge(aT_ready, b - 1)
                pe.wait_ge(eT0_ready, b + 1)
                pe.wait_ge(vT_ready, 2 * (b // HB) + 2)
                for q in range(KC):
                    last = product(PB[2 + b % 2][:, q * S:(q + 1) * S],
                                   [(eT0[:, b % 4, k, q * P:(q + 1) * P], vT[:, k, tok(b)]) for k in range(KC)])
                last.then_inc(aT_ps, 1)

            for b in range(B + 4):
                if b < B:
                    scores0(b)
                if 2 <= b < B + 2:
                    transposes0(b - 2)
                if b >= 4:
                    values0(b - 4)
            pe.wait_ge(ld_b, LD_B)
            for b in range(B):
                if b < 2:
                    pe.wait_ge(v_ready, B)
                else:
                    pe.wait_ge(summed, b - 1)
                pe.wait_ge(aT_ready, b + 1)
                product(PB[4 + b % 2][0:S, 0:D], [(aT[:, b, q, :], projT[:, q, :]) for q in range(KC)]).then_inc(y1_ps, 1)
            for b in range(B):
                if b < 2:
                    pe.wait_ge(eT0_ready, B)
                else:
                    pe.wait_ge(x1T_ready, b - 1)
                pe.wait_ge(ln_out, B + b + 1)
                to_cm(XN, PB[b % 2], b).then_inc(x1T_ps, 1)
            for n, (h, m) in enumerate([(h, m) for h in range(2) for m in range(KC)]):
                if n:
                    pe.wait_ge(q_rot, 2 * n)
                else:
                    pe.wait_ge(aT_ready, B)
                pe.wait_ge(x1T_ready, HB * (h + 1))
                for sw in range(2):
                    last = product(PB[2 + sw][:, 0:HN], [(xqT[:, k, sw * D + m * P:sw * D + (m + 1) * P], T1[:, k, half(h)])
                                                         for k in range(KC)])
                last.then_inc(qp_ps, 1)

            def scores1(u):
                b, c, j = u // 4, u // 2 % 2, u % 2
                bank = PB[4 + u % 2][0:S, 0:QH * S]
                if u < 2:
                    pe.wait_ge(summed, B)
                else:
                    pe.wait_ge(s1_sub, u - 1)
                pe.wait_ge(qr_ready, 2 * (b // HB) + c + 1)
                pe.wait_ge(kblk_ready, u // 2 + 1)
                product(bank, [(qr[:, c, tok(b)], kblk[:, u // 2 % 4, QH * j:QH * (j + 1), :]),
                               (identb[0:S, 0:S], maskb[0:S, :])]).then_inc(s1_ps, 1)

            def transposes1(u):
                if u < 2:
                    pe.wait_ge(s0_exp, B)
                else:
                    pe.wait_ge(eT1_ready, u - 1)
                pe.wait_ge(s1_exp, u + 1)
                for h in range(QH):
                    last = nc.tensor.transpose(PB[6 + u % 2][0:S, h * S:(h + 1) * S], e1[0:S, u % 4, h, :], ident[0:S, 0:S])
                last.then_inc(eT1_ps, 1)

            def values1(u):
                b, w = u // 4, D0 + 1
                if u % 4 == 0:
                    if b < 2:
                        pe.wait_ge(x1T_ready, B)
                    else:
                        pe.wait_ge(c1_ready, b - 1)
                pe.wait_ge(eT1_ready, u + 1)
                for h in range(QH):
                    hh = QH * (u % 4) + h
                    last = product(PB[b % 2][0:S, hh * w:(hh + 1) * w], [(eT1[0:S, u % 4, h, :], vaug[0:S, b, hh, :])])
                if u % 4 == 3:
                    last.then_inc(c1_ps, 1)

            UN = B * H0 // QH
            for u in range(UN + 4):
                if u < UN:
                    scores1(u)
                if 2 <= u < UN + 2:
                    transposes1(u - 2)
                if u >= 4:
                    values1(u - 4)
            for b in range(B):
                if b < 2:
                    pe.wait_ge(q_rot, 8)
                else:
                    pe.wait_ge(cT1_ready, b - 1)
                pe.wait_ge(c1_ready, b + 1)
                to_cm(ctxn, PB[2 + b % 2], b).then_inc(cT1_ps, 1)
            for b in range(B):
                if b < 2:
                    pe.wait_ge(s1_sub, UN)
                else:
                    pe.wait_ge(summed, B + b - 1)
                pe.wait_ge(cT1_ready, b + 1)
                product(PB[4 + b % 2][0:S, 0:D], [(ctxnT[:, k, tok(b)], xoT[:, k, :]) for k in range(KC)]).then_inc(y2_ps, 1)
            for b in range(B):
                if b < 2:
                    pe.wait_ge(c1_ready, B)
                else:
                    pe.wait_ge(x2T_ready, b - 1)
                pe.wait_ge(ln_out, 2 * B + b + 1)
                to_cm(X, PB[b % 2], b).then_inc(x2T_ps, 1)
            pe.wait_ge(cT1_ready, B)
            for b in range(B):
                pe.wait_ge(x2T_ready, b + 1)
                product(PB[2][0:S, b * (E + 1):(b + 1) * (E + 1)], [(T0[:, k, tok(b)], gateT[:, k, :]) for k in range(KC)]).then_inc(g_ps, 1)
            pe.wait_ge(wtm_ready, 1)
            for n, (b, c) in enumerate([(b, c) for b in range(B) for c in range(3)]):
                if n < 2:
                    pe.wait_ge(summed, 2 * B)
                elif n < 4:
                    pe.wait_ge(eT1_ready, UN)
                else:
                    pe.wait_ge(wb_ready, n - 3)
                for j, g in enumerate(range(4 * c, min(4 * c + 4, GROUPS))):
                    last = nc.tensor.transpose(PB[4 + n % 4][:, j * S:(j + 1) * S],
                                               wtm[0:S, b, g:g + 1].broadcast_to([S, P]), ident[0:S, 0:S])
                last.then_inc(wb_ps, 1)

            acc = [[PB[2 * hc + t][:, 0:HN] for t in range(2)] for hc in range(KC)]
            pe.wait_ge(zero_set, 1)
            pe.wait_ge(x2T_ready, B)
            pe.wait_ge(g_exp, 2)
            for hc in range(KC):
                for t in range(2):
                    last = mm(acc[hc][t], zero16[:, 0:P], zero16[:], start=True, stop=False)
                    if 2 * hc + t < 3:
                        last.then_inc(down_done, 1)
            pe.wait_ge(xlo_ready, B)
            pe.wait_ge(wb_ready, 3 * B)

            def gate_up(j, n):
                slot, m, t = j // UNITS % 2, j % UNITS // 2, j % 2
                r = ROWS[m]
                pe.wait_ge(hu_ready, n + 1)
                for up in range(2):
                    c0 = up * I + m * P
                    pairs = []
                    for k in range(KC):
                        pairs += tripled((gu_hi[slot][:, k, c0:c0 + r], gu_lo[slot][:, k, c0:c0 + r]),
                                         (x_hi[:, k, half(t)], x_lo[:, k, half(t)]))
                    last = product(PB[4 + 2 * (j % 2) + up][0:r, 0:HN], pairs)
                last.then_inc(gu_ps, 1)

            def group_split(g):
                pe.wait_ge(gu_hi_ready, g + 1)
                pe.wait_ge(gu_lo_ready, g * 2 + 2)

            def down(j, n, last_turn):
                slot, m, t = j // UNITS % 2, j % UNITS // 2, j % 2
                r = ROWS[m]
                pe.wait_ge(hlo_ready, n + 1 + 2)
                for hc in range(KC):
                    cols = slice(hc * P, (hc + 1) * P)
                    pairs = tripled((dn_hi[slot][0:r, m, cols], dn_lo[slot][0:r, m, cols]),
                                    (h_hi[j % 3][0:r, :], h_lo[j % 3][0:r, :]))
                    for i, (a, v) in enumerate(pairs):
                        last = mm(acc[hc][t], a, v, start=False, stop=last_turn and j >= PAIR - 2 and i == 2)
                last.then_inc(down_done, 1)

            group_split(0)
            gate_up(0, 0)
            gate_up(1, 1)

            def turn(i, last_turn):
                for j in range(PAIR):
                    if not (last_turn and j + 2 >= PAIR):
                        if (j + 2) % UNITS == 0:
                            group_split(i * 2 + (j + 2) // UNITS)
                        gate_up(j + 2, i * PAIR + (j + 2))
                    if j % UNITS == 0:
                        pe.wait_ge(dn_hi_ready, i * 2 + (j // UNITS + 1))
                        pe.wait_ge(dn_lo_ready, i * 4 + 2 * (j // UNITS + 1))
                    down(j, i * PAIR + j, last_turn)

            with pe.Fori(0, GROUPS // 2 - 1) as i:
                turn(i, False)
            turn(GROUPS // 2 - 1, True)

            for b in range(B):
                if b < 2:
                    pe.wait_ge(hu_ready, NU + 2)
                else:
                    pe.wait_ge(summed, 2 * B + b - 1)
                pe.wait_ge(fT_ready, 2 * (b // HB) + 2)
                for k in range(KC):
                    last = nc.tensor.transpose(PB[4 + b % 2][0:S, k * P:(k + 1) * P], fT[:, k, tok(b)], ident[:])
                last.then_inc(y3_ps, 1)
            for b in range(B):
                if b >= 2:
                    pe.wait_ge(x3T_ready, b - 1)
                pe.wait_ge(ln_out, 3 * B + b + 1)
                to_cm(XN, PB[6 + b % 2], b).then_inc(x3T_ps, 1)
            pe.wait_ge(ld_c, LD_C)
            pe.wait_ge(fT_ready, 4)
            n = 0
            for h in range(2):
                pe.wait_ge(x3T_ready, HB * (h + 1))
                product(PB[2 + h][0:R1, 0:HN], [(wkdT[:, k, :], T1[:, k, half(h)]) for k in range(KC)]).then_inc(lat_ps, 1)
                for kind in range(2):
                    for m in range(QC):
                        if n >= 2:
                            pe.wait_ge(q1_ready, n - 1)
                        cols = slice(m * P, (m + 1) * P)
                        if kind == 0:
                            pairs = [(wqT[:, k, cols], T1[:, k, half(h)]) for k in range(KC)]
                        else:
                            pe.wait_ge(lat_ready, h + 1)
                            pairs = [(wkuT[:, cols], latT[:, half(h)])]
                        product(PB[n % 2][:, 0:HN], pairs).then_inc(q1_ps, 1)
                        n += 1
            for b in range(B):
                if b < 2:
                    pe.wait_ge(x3T_ready, B)
                else:
                    pe.wait_ge(v1_ready, b - 1)
                product(PB[6 + b % 2][0:S, :], [(latT[:, tok(b)], wvuT[:])]).then_inc(v1_ps, 1)

            def scores2(u):
                b, j = u // 2, u % 2
                if u < 2:
                    pe.wait_ge(summed, 3 * B)
                else:
                    pe.wait_ge(s2_sub, u - 1)
                for h in range(QH):
                    c, lo = h, j * D1
                    last = product(PB[4 + u % 2][0:S, h * S:(h + 1) * S],
                                   [(q1T[lo:lo + D1, c, tok(b)], k1T[lo:lo + D1, c, tok(b)])])
                last.then_inc(s2_ps, 1)

            def transposes2(u):
                if u < 2:
                    pe.wait_ge(v1_ready, B)
                else:
                    pe.wait_ge(eT2_ready, u - 1)
                pe.wait_ge(s2_exp, u + 1)
                for h in range(QH):
                    last = nc.tensor.transpose(PB[6 + u % 2][0:S, h * S:(h + 1) * S], e2[0:S, u % 4, h, :], ident[0:S, 0:S])
                last.then_inc(eT2_ps, 1)

            def values2(u):
                w = D1 + 1
                if u >= 2:
                    pe.wait_ge(c2_ready, u - 1)
                pe.wait_ge(eT2_ready, u + 1)
                for h in range(QH):
                    last = product(PB[2 + u % 2][0:S, h * w:(h + 1) * w],
                                   [(eT2[0:S, u % 4, h, :], v1[0:S, u // 2, 2 * h + u % 2, :])])
                last.then_inc(c2_ps, 1)

            U2 = B * H1 // QH
            pe.wait_ge(q1_ready, 2 * 2 * QC)
            for u in range(U2 + 4):
                if u < U2:
                    scores2(u)
                if 2 <= u < U2 + 2:
                    transposes2(u - 2)
                if u >= 4:
                    values2(u - 4)

            def project(b):
                product(PB[4 + b % 2][0:S, 0:D], [(a1T[:, b % 4, c, :], woT[:, c, :]) for c in range(QC)]).then_inc(y4_ps, 1)

            for b in range(B):
                if b >= 2:
                    pe.wait_ge(a1T_ready, b - 1)
                pe.wait_ge(c2_ready, 2 * b + 2)
                for c in range(QC):
                    last = nc.tensor.transpose(PB[b % 2][:, c * S:(c + 1) * S], a1[0:S, b, c * P:(c + 1) * P], ident[0:S, 0:S])
                last.then_inc(a1T_ps, 1)
                if b >= 1:
                    pe.wait_ge(a1T_ready, b)
                if b >= 3:
                    pe.wait_ge(summed, 3 * B + b - 2)
                if b >= 1:
                    project(b - 1)
            pe.wait_ge(a1T_ready, B)
            pe.wait_ge(summed, 3 * B + B - 2)
            project(B - 1)
            for b in range(B):
                if b < 2:
                    pe.wait_ge(eT2_ready, U2)
                else:
                    pe.wait_ge(x4T_ready, b - 1)
                pe.wait_ge(ln_out, 4 * B + b + 1)
                to_cm(X, PB[6 + b % 2], b).then_inc(x4T_ps, 1)
            pe.wait_ge(ld_ct, 16)
            for b in range(B):
                if b < 2:
                    pe.wait_ge(a1T_ready, B)
                else:
                    pe.wait_ge(gelu_ready, b - 1)
                pe.wait_ge(x4T_ready, b + 1)
                for f, r in enumerate(FROWS):
                    last = product(PB[b % 2][0:r, f * S:(f + 1) * S],
                                   [(cT[:, k, b, f * P:f * P + r], T0[:, k, tok(b)]) for k in range(KC)])
                last.then_inc(g4_ps, 1)
            for b in range(B):
                if b < 2:
                    pe.wait_ge(c2_ready, U2)
                else:
                    pe.wait_ge(summed, 4 * B + b - 1)
                pe.wait_ge(gelu_ready, b + 1)
                product(PB[2 + b % 2][0:S, 0:D], [(gT[0:r, b, f, :], cN[0:r, b, f, :]) for f, r in enumerate(FROWS)]).then_inc(y5_ps, 1)
            for b in range(B):
                if b < 2:
                    pe.wait_ge(summed, 4 * B)
                else:
                    pe.wait_ge(pad_ready, b - 1)
                pe.wait_ge(ln_out, 5 * B + b + 1)
                to_cm(XN, PB[4 + b % 2], b).then_inc(x5T_ps, 1)
            for n, (h, m) in enumerate([(h, m) for h in range(2) for m in range(KC)]):
                if n < 2:
                    pe.wait_ge(x4T_ready, B)
                else:
                    pe.wait_ge(kpos_ready, n - 1)
                pe.wait_ge(mix_ready, 4 * h + 4)
                product(PB[6 + n % 2][:, 0:HN], [(wkT[:, k, m * P:(m + 1) * P], mix[:, 1, k, half(h)]) for k in range(KC)]).then_inc(kk_ps, 1)
            for b in range(B):
                if b < 2:
                    pe.wait_ge(gelu_ready, B)
                    pe.wait_ge(summed, 5 * B)
                else:
                    pe.wait_ge(rexp_ready, b - 1)
                    pe.wait_ge(gated, b - 1)
                product(PB[b % 2][0:S, 0:D], [(mix[:, 0, k, tok(b)], wrT[:, k, :]) for k in range(KC)]).then_inc(r_ps, 1)
                pe.wait_ge(ksq_ready, 2 * (b // HB) + 2)
                product(PB[2 + b % 2][0:S, 0:D], [(ksq[:, k, tok(b)], wvT[:, k, :]) for k in range(KC)]).then_inc(y6_ps, 1)

        @block.gpsimd
        def _(pool):
            TT = nc.gpsimd.tensor_tensor
            nc.gpsimd.memset(epsb[:], EPS).then_inc(ones_set, 1)
            nc.gpsimd.memset(vaug[0:S, :, :, D0:D0 + 1], 1.0).then_inc(ones_set, 1)
            nc.gpsimd.memset(zero16[:], 0.0).then_inc(zero_set, 1)
            nc.gpsimd.memset(score[0:S, :, E:2 * E], -1.0).then_inc(sent_set, 1)
            pool.wait_ge(ld_x, 16)
            pool.wait_ge(ld_b, LD_B)
            for b in range(B):
                TT(RES[0:S, b], X[0:S, b], proj_b[0:S], ALU.add).then_inc(twice, 1)
            for b in range(B):
                pool.wait_ge(twice, b + 1)
                TT(RES[0:S, b], RES[0:S, b], X[0:S, b], ALU.add).then_inc(resid, 1)
            for n, (h, m) in enumerate([(h, m) for h in range(2) for m in range(KC)]):
                pool.wait_ge(k_rot, 2 * n + 2)
                TT(kr[:, m, half(h)], rot[:, n % 2, 0], rot[:, n % 2, 1], ALU.add).then_inc(kr_ready, 1)
            for b in range(B):
                pool.wait_ge(s0_max, b + 1)
                nc.gpsimd.tensor_scalar_mul(nb0[:, b], max0[:, b], SCALE0).then_inc(s0_nb, 1)

            def lo_gu(slot, k):
                TT(gu_lo[slot][:, k], w_gu[:, k], gu_hi[slot][:, k].bitcast(F32), ALU.subtract).then_inc(gu_lo_ready, 1)

            def lo_dn(slot, part):
                q = (slice(0, P), slice(0, MC - 1)) if part == 0 else (slice(0, ROWS[-1]), slice(MC - 1, MC))
                TT(dn_lo[slot][q], w_dn[q], dn_hi[slot][q].bitcast(F32), ALU.subtract).then_inc(dn_lo_ready, 1)

            pool.wait_ge(gu_hi_ready, 1)
            lo_gu(0, 0)
            lo_gu(0, 1)
            pool.wait_ge(dn_hi_ready, 1)
            lo_dn(0, 0)
            lo_dn(0, 1)

            def key_blocks(n):
                b, c = n // 2, n % 2
                if n >= 4:
                    pool.wait_ge(s1_ps, 2 * (n - 4) + 2)
                pool.wait_ge(kr_ready, 2 * (b // HB) + c + 1)
                TT(kblk[:, n % 4], kr[:, c, tok(b)].unsqueeze(1).broadcast_to([P, HC, S]),
                   hmask[:].unsqueeze(2).broadcast_to([P, HC, S]), ALU.mult).then_inc(kblk_ready, 1)

            pool.wait_ge(s0_ps, B)
            for n in range(4):
                key_blocks(n)
            for b in range(B):
                pool.wait_ge(ln_out, B + b + 1)
                TT(RES[0:S, b], XN[0:S, b], xo_b[0:S], ALU.add).then_inc(resid, 1)
            for n, (h, m) in enumerate([(h, m) for h in range(2) for m in range(KC)]):
                pool.wait_ge(q_rot, 2 * n + 2)
                TT(qr[:, m, half(h)], rot[:, n % 2, 0], rot[:, n % 2, 1], ALU.add).then_inc(qr_ready, 1)
            for n in range(4, 2 * B):
                key_blocks(n)
            for b in range(B):
                pool.wait_ge(x2T_ready, b + 1)
                nc.gpsimd.tensor_copy(x_hi[:, :, tok(b)], T0[:, :, tok(b)]).then_inc(xhi_ready, 1)
            for b in range(B):
                pool.wait_ge(xhi_ready, b + 1)
                TT(x_lo[:, :, tok(b)], T0[:, :, tok(b)], x_hi[:, :, tok(b)].bitcast(F32), ALU.subtract).then_inc(xlo_ready, 1)

            nc.gpsimd.sem_inc(hw_ready, 2)
            pool.wait_ge(wb_ready, 3 * B)

            def weigh(i, j):
                m, t = j % UNITS // 2, j % 2
                r, n = ROWS[m], i * PAIR + j
                pool.wait_ge(hu_ready, n + 1 + 2)
                pool.wait_ge(hlo_ready, n + 1)
                pool.sem_inc(weigh_turn, 1)
                w = wb[0:r, bass.ds(i * 2 + j // UNITS, 1), half(t)].rearrange("p o n -> p (o n)")
                TT(hw[0:r, j % 2], hu[0:r, j % 2], w, ALU.mult).then_inc(hw_ready, 1)

            def turn(i, last_turn):
                for j in range(PAIR):
                    weigh(i, j)
                    if last_turn and j >= UNITS:
                        continue
                    g = i * 2 + j // UNITS
                    slot = (j // UNITS + 1) % 2
                    if j % UNITS == 1:
                        pool.wait_ge(gu_hi_ready, g + 2)
                        lo_gu(slot, 0)
                    if j % UNITS == 2:
                        lo_gu(slot, 1)
                    if j % UNITS == 3:
                        pool.wait_ge(dn_hi_ready, g + 2)
                        lo_dn(slot, 0)
                    if j % UNITS == 4:
                        lo_dn(slot, 1)

            with pool.Fori(0, GROUPS // 2 - 1) as i:
                turn(i, False)
            turn(GROUPS // 2 - 1, True)

            pool.wait_ge(fT_ready, 4)
            nc.gpsimd.memset(v1[0:S, :, :, D1:D1 + 1], 1.0).then_inc(one1_set, 1)
            pool.wait_ge(ld_c, LD_C)
            nc.gpsimd.tensor_scalar(omm[:], mu[:], -1.0, 1.0, ALU.mult, ALU.add).then_inc(omm_ready, 1)
            pool.wait_ge(g4_ps, 1)
            nc.gpsimd.memset(pad[:, :, :, 0:1], 0.0).then_inc(pad_zero, 1)
            for n, (h, m) in enumerate([(h, m) for h in range(2) for m in range(KC)]):
                pool.wait_ge(kpos_ready, n + 1)
                TT(ksq[:, m, half(h)], kpos[:, n % 2], kpos[:, n % 2], ALU.mult).then_inc(ksq_ready, 1)

        @block.scalar
        def _(act):
            A = nc.scalar.activation

            def norm_scale(k, b):
                act.wait_ge(ln_mv, k * B + b + 1)
                A(lnv[0:S, b:b + 1], mv[0:S, b, 1:2], ACT.Ln, bias=epsb[0:S]).then_inc(ln_lg, 1)
                act.wait_ge(ln_lg, k * B + b + 1)
                A(rstd[0:S, b:b + 1], lnv[0:S, b:b + 1], ACT.Exp, scale=-0.5).then_inc(ln_rs, 1)

            def norms_then(k, evac):
                for b in range(B + 3):
                    if b < B:
                        norm_scale(k, b)
                    if b >= 3:
                        evac(b - 3)

            def cm_copy(ps_ready, banks, dst, done):
                def evac(b):
                    act.wait_ge(ps_ready, b + 1)
                    A(dst[:, :, tok(b)], banks[b % 2][:, 0:KC * S].rearrange("p (k s) -> p k s", s=S), ACT.Copy).then_inc(done, 1)
                return evac

            nc.scalar.preload_act_table_set("natural_log_exp_and_others")
            act.wait_ge(ones_set, 1)

            def h_evac(b):
                act.wait_ge(hT_ps, b + 1)
                for k in range(KC):
                    last = A(T0[:, k, tok(b)], PB[b % 2][:, k * S:(k + 1) * S], ACT.Identity,
                             bias=colb[:, 2 + k:3 + k], scale=colb[:, k:k + 1])
                last.then_inc(hT_ready, 1)

            act.wait_ge(ld_a, LD_A)
            norms_then(0, h_evac)
            for n, (h, m) in enumerate([(h, m) for h in range(2) for m in range(KC)]):
                act.wait_ge(vT_ps, n + 1)
                A(vT[:, m, half(h)], PB[4 + m][:, 0:HN], ACT.Identity, bias=colb[:, 4 + m:5 + m]).then_inc(vT_ready, 1)

            def exp0(b):
                act.wait_ge(s0_nb, b + 1)
                if b >= 4:
                    act.wait_ge(eT0_ps, b - 3)
                for q in range(KC):
                    last = A(e0[:, b % 4, q, :], PB[6 + b % 2][:, q * D:(q + 1) * D], ACT.Exp,
                             bias=nb0[:, b, q:q + 1], scale=SCALE0, accum_out=sum0[:, b, q:q + 1])
                last.then_inc(s0_exp, 1)

            def a_evac(b):
                act.wait_ge(aT_ps, b + 1)
                act.wait_ge(s0_rs, b + 1)
                for q in range(KC):
                    last = A(aT[:, b, q, :], PB[2 + b % 2][:, q * S:(q + 1) * S], ACT.Copy, scale=rs0[:, b, q:q + 1])
                last.then_inc(aT_ready, 1)

            for b in range(B + 4):
                if b < B:
                    exp0(b)
                if b >= 4:
                    a_evac(b - 4)
            norms_then(1, cm_copy(x1T_ps, PB[0:2], T1, x1T_ready))

            def exps(u, n_units, sub, e, scale, done):
                act.wait_ge(sub, u + 1)
                A(e[0:S, u % 4], e[0:S, u % 4], ACT.Exp, scale=scale).then_inc(done, 1)

            def exp_evac(u, ps_ready, eT, done):
                act.wait_ge(ps_ready, u + 1)
                A(eT[0:S, u % 4], heads(PB[6 + u % 2][0:S, 0:QH * S]), ACT.Copy).then_inc(done, 1)

            UN, U2 = B * H0 // QH, B * H1 // QH
            for u in range(UN + 2):
                if u < UN:
                    exps(u, UN, s1_sub, e1, D0 ** -0.5, s1_exp)
                if u >= 2:
                    exp_evac(u - 2, eT1_ps, eT1, eT1_ready)
            evac = cm_copy(cT1_ps, PB[2:4], ctxnT, cT1_ready)
            for b in range(B):
                evac(b)
            norms_then(2, cm_copy(x2T_ps, PB[0:2], T0, x2T_ready))
            act.wait_ge(g_step, 2)
            logits = PB[2][0:S, 0:B * (E + 1)].rearrange("p (b e) -> p b e", e=E + 1)
            A(gexp[0:S, :, E:E + 1], logits[:, :, E:E + 1], ACT.Exp, scale=-1.0).then_inc(g_exp, 1)
            A(gexp[0:S, :, 0:E], gexp[0:S, :, 0:E], ACT.Exp).then_inc(g_exp, 1)
            for n, (b, c) in enumerate([(b, c) for b in range(B) for c in range(3)]):
                act.wait_ge(wb_ps, n + 1)
                k = min(4, GROUPS - 4 * c)
                A(wb[:, 4 * c:4 * c + k, tok(b)], heads(PB[4 + n % 4][:, 0:k * S]), ACT.Copy).then_inc(wb_ready, 1)

            def silu(j, n):
                r = ROWS[j % UNITS // 2]
                act.wait_ge(gu_ps, n + 1)
                act.wait_ge(hu_ready, n + 1)
                A(sg[0:r, j % 2], PB[4 + 2 * (j % 2)][0:r, 0:HN], ACT.Silu).then_inc(silu_ready, 1)

            def hidden_hi(j, n):
                r = ROWS[j % UNITS // 2]
                act.wait_ge(hw_ready, n + 1 + 2)
                act.wait_ge(down_done, n + 1)
                A(h_hi[j % 3][0:r], hw[0:r, j % 2], ACT.Copy).then_inc(hhi_ready, 1)

            silu(0, 0)

            def turn(i, last_turn):
                for j in range(PAIR):
                    if not (last_turn and j + 1 >= PAIR):
                        silu((j + 1) % PAIR, i * PAIR + (j + 1))
                    hidden_hi(j, i * PAIR + j)

            with act.Fori(0, GROUPS // 2 - 1) as i:
                turn(i, False)
            turn(GROUPS // 2 - 1, True)
            for t in range(2):
                act.wait_ge(down_done, NU + 3 - 1 + t)
                for hc in range(KC):
                    A(fT[:, hc, half(t)], PB[2 * hc + t][:, 0:HN], ACT.Copy).then_inc(fT_ready, 1)

            nc.scalar.preload_act_table_set("natural_log_exp_and_others")
            norms_then(3, cm_copy(x3T_ps, PB[6:8], T1, x3T_ready))
            n = 0
            for h in range(2):
                for dst in (q1T, k1T):
                    for m in range(QC):
                        act.wait_ge(q1_ps, n + 1)
                        A(dst[:, m, half(h)], PB[n % 2][:, 0:HN], ACT.Copy).then_inc(q1_ready, 1)
                        n += 1
            for u in range(U2 + 2):
                if u < U2:
                    exps(u, U2, s2_sub, e2, D1 ** -0.5, s2_exp)
                if u >= 2:
                    exp_evac(u - 2, eT2_ps, eT2, eT2_ready)
            for b in range(B + 2):
                if b < B:
                    act.wait_ge(a1T_ps, b + 1)
                    if b >= 4:
                        act.wait_ge(y4_ps, b - 3)
                    A(a1T[:, b % 4], heads(PB[b % 2][:, 0:QC * S]), ACT.Copy).then_inc(a1T_ready, 1)
                if b >= 2:
                    norm_scale(4, b - 2)
            evac = cm_copy(x4T_ps, PB[6:8], T0, x4T_ready)
            for b in range(B):
                evac(b)
            for b in range(B):
                act.wait_ge(g4_ps, b + 1)
                f = FC - 1
                A(gT[:, b, 0:f], PB[b % 2][:, 0:f * S].rearrange("p (f s) -> p f s", s=S), ACT.Gelu_apprx_tanh)
                A(gT[0:FROWS[f], b, f], PB[b % 2][0:FROWS[f], f * S:(f + 1) * S], ACT.Gelu_apprx_tanh).then_inc(gelu_ready, 1)
            nc.scalar.preload_act_table_set("natural_log_exp_and_others")

            def pad_evac(b):
                act.wait_ge(x5T_ps, b + 1)
                A(pad[:, :, b, 1:S + 1], PB[4 + b % 2][:, 0:KC * S].rearrange("p (k s) -> p k s", s=S), ACT.Copy).then_inc(pad_ready, 1)

            norms_then(5, pad_evac)
            n = 0
            for h in range(2):
                for a in (1, 0):
                    for k in range(KC):
                        if n == 0:
                            act.wait_ge(pad_ready, B)
                        if n >= 2:
                            act.wait_ge(mix_ready, n - 1)
                        A(mixt[:, n % 2].rearrange("p (b s) -> p b s", s=S), pad[:, k, h * HB:(h + 1) * HB, 1:S + 1],
                          ACT.Copy, scale=mu[:, a, k:k + 1]).then_inc(mixt_ready, 1)
                        n += 1
            for n in range(4):
                act.wait_ge(kk_ps, n + 1)
                if n >= 2:
                    act.wait_ge(ksq_ready, n - 1)
                A(kpos[:, n % 2], PB[6 + n % 2][:, 0:HN], ACT.Relu).then_inc(kpos_ready, 1)
            for b in range(B + 1):
                if b < B:
                    act.wait_ge(r_ps, b + 1)
                    if b >= 2:
                        act.wait_ge(r_step, 2 * (b - 2) + 1)
                    A(rec[0:S, b % 2, 0], PB[b % 2][0:S, 0:D], ACT.Exp, scale=-1.0).then_inc(rexp_ready, 1)
                if b >= 1:
                    norm_scale(6, b - 1)

        @block.vector
        def _(dve):
            V = nc.vector

            def norm_stats(k, b):
                V.bn_stats(stats[0:S, b], (X if k == 0 else RES)[0:S, b]).then_inc(ln_st, 1)
                dve.wait_ge(ln_st, k * B + b + 1)
                V.bn_aggr(mv[0:S, b], stats[0:S, b]).then_inc(ln_mv, 1)

            def normalize(k, b, dst):
                dve.wait_ge(ln_rs, k * B + b + 1)
                V.tensor_scalar(dst[0:S, b], (X if k == 0 else RES)[0:S, b], mv[0:S, b, 0:1], rstd[0:S, b:b + 1],
                                ALU.subtract, ALU.mult).then_inc(ln_out, 1)

            def add_and_norm(k, dst, add):
                for b in range(B + 2):
                    if b < B:
                        add(b)
                        dve.wait_ge(summed, (k - 1) * B + b + 1)
                        norm_stats(k, b)
                    if b >= 2:
                        normalize(k, b - 2, dst)

            dve.wait_ge(ld_x, 16)
            for b in range(B + 2):
                if b < B:
                    norm_stats(0, b)
                if b >= 2:
                    normalize(0, b - 2, XN)
            for b in range(B):
                dve.wait_ge(qk_ps, b + 1)
                V.tensor_tensor(qk[0:S, b], PB[2 + b % 2][0:S, :], qk_b[0:S], ALU.add).then_inc(qk_ready, 1)

            def rotate(n, m, ps_ready, banks, col, done, summed_up):
                dve.wait_ge(ps_ready, n + 1)
                if n >= 2:
                    dve.wait_ge(summed_up, n - 1)
                for sw in range(2):
                    V.scalar_tensor_tensor(out=rot[:, n % 2, sw].rearrange("p (b s) -> p b s", s=S),
                                           in0=banks[sw][:, 0:HN].rearrange("p (b s) -> p b s", s=S),
                                           scalar=colb[:, col + 2 * sw + m:col + 2 * sw + m + 1],
                                           in1=rope[:, sw:sw + 1].broadcast_to([P, HB, S]),
                                           op0=ALU.add, op1=ALU.mult).then_inc(done, 1)

            dve.wait_ge(ld_k, LD_K)
            for n in range(4):
                rotate(n, n % 2, kp_ps, PB[6:8], 10, k_rot, kr_ready)
            dve.wait_ge(ones_set, 2)
            for b in range(B):
                dve.wait_ge(v_ps, b + 1)
                V.tensor_tensor(vaug[0:S, b, :, 0:D0], PB[4 + b % 2][0:S, 0:D].rearrange("p (h d) -> p h d", d=D0),
                                xv_b[0:S].rearrange("p (h d) -> p h d", d=D0), ALU.add).then_inc(v_ready, 1)
            def hi_gu(slot):
                V.tensor_copy(gu_hi[slot][:], w_gu[:]).then_inc(gu_hi_ready, 1)

            def hi_dn(slot):
                V.tensor_copy(dn_hi[slot][:, 0:MC - 1], w_dn[:, 0:MC - 1])
                V.tensor_copy(dn_hi[slot][0:ROWS[-1], MC - 1:MC], w_dn[0:ROWS[-1], MC - 1:MC]).then_inc(dn_hi_ready, 1)

            dve.wait_ge(ld_w, LD_W)
            hi_gu(0)
            hi_dn(0)

            def max0_of(b):
                dve.wait_ge(s0_ps, b + 1)
                V.tensor_reduce(max0[:, b], PB[6 + b % 2][:].rearrange("p (q k) -> p q k", k=D), X_AXIS, ALU.max,
                                negate=True).then_inc(s0_max, 1)

            def e_evac(b):
                dve.wait_ge(s0_exp, b + 1)
                V.reciprocal(rs0[:, b], sum0[:, b]).then_inc(s0_rs, 1)
                dve.wait_ge(eT0_ps, b + 1)
                if b >= 4:
                    dve.wait_ge(aT_ps, b - 3)
                V.tensor_copy(eT0[:, b % 4], PB[b % 2][:].rearrange("p (k q) -> p k q", q=D)).then_inc(eT0_ready, 1)

            for b in range(B + 2):
                if b < B:
                    max0_of(b)
                if b >= 2:
                    e_evac(b - 2)

            def add1(b):
                dve.wait_ge(y1_ps, b + 1)
                dve.wait_ge(resid, b + 1)
                V.tensor_tensor(RES[0:S, b], PB[4 + b % 2][0:S, 0:D], RES[0:S, b], ALU.add).then_inc(summed, 1)

            add_and_norm(1, XN, add1)
            for n in range(4):
                rotate(n, n % 2, qp_ps, PB[2:4], 6, q_rot, qr_ready)

            def softmax_in(u, ps_ready, mx, e, used, maxed, done):
                dve.wait_ge(ps_ready, u + 1)
                if u >= 4:
                    dve.wait_ge(used, u - 3)
                sc = heads(PB[4 + u % 2][0:S, 0:QH * S])
                m = mx[0:S, QH * u:QH * (u + 1)]
                V.tensor_reduce(m, sc, X_AXIS, ALU.max).then_inc(maxed, 1)
                dve.wait_ge(maxed, u + 1)
                V.tensor_tensor(e[0:S, u % 4], sc, m.unsqueeze(2).broadcast_to([S, QH, S]), ALU.subtract).then_inc(done, 1)

            def softmax_out(n, ps, rs, dst, dim, ps_ready, inverted, done):
                dve.wait_ge(ps_ready, n + 1)
                V.reciprocal(rs.unsqueeze(2), ps[:, :, dim:dim + 1]).then_inc(inverted, 1)
                dve.wait_ge(inverted, n + 1)
                V.tensor_tensor(dst, ps[:, :, 0:dim],
                                rs.unsqueeze(2).broadcast_to([S, ps.shape[1], dim]), ALU.mult).then_inc(done, 1)

            UN, U2 = B * H0 // QH, B * H1 // QH

            def out1(b):
                ps = PB[b % 2][0:S, 0:H0 * (D0 + 1)].rearrange("p (h d) -> p h d", d=D0 + 1)
                softmax_out(b, ps, rs1[0:S, b], ctxn[0:S, b].rearrange("p (h d) -> p h d", d=D0), D0, c1_ps, c1_rs, c1_ready)

            for u in range(UN):
                softmax_in(u, s1_ps, max1, e1, eT1_ps, s1_max, s1_sub)
                if u >= 8 and u % 4 == 0:
                    out1(u // 4 - 2)
            out1(B - 2)
            out1(B - 1)

            def add2(b):
                dve.wait_ge(y2_ps, b + 1)
                dve.wait_ge(resid, B + b + 1)
                V.tensor_tensor(RES[0:S, b], PB[4 + b % 2][0:S, 0:D], RES[0:S, b], ALU.add).then_inc(summed, 1)

            add_and_norm(2, X, add2)
            logits = PB[2][0:S, 0:B * (E + 1)].rearrange("p (b e) -> p b e", e=E + 1)
            ge, sc8 = gexp[0:S, :, 0:E], score[0:S, :, 0:E]
            dve.wait_ge(g_ps, B)
            V.reduce_max(gmax[0:S], logits[:, :, 0:E], X_AXIS).then_inc(g_step, 1)
            dve.wait_ge(g_step, 1)
            V.tensor_tensor(ge, logits[:, :, 0:E], gmax[0:S].unsqueeze(2).broadcast_to([S, B, E]), ALU.subtract).then_inc(g_step, 1)
            dve.wait_ge(g_exp, 2)
            V.reduce_sum(gsum[0:S], ge, X_AXIS).then_inc(g_step, 1)
            V.tensor_scalar_add(sig1[0:S].unsqueeze(2), gexp[0:S, :, E:E + 1], 1.0).then_inc(g_step, 1)
            dve.wait_ge(g_step, 4)
            V.reciprocal(grs[0:S], gsum[0:S]).then_inc(g_step, 1)
            V.reciprocal(wtm[0:S, :, E:E + 1], sig1[0:S].unsqueeze(2)).then_inc(g_step, 1)
            dve.wait_ge(g_step, 6)
            V.tensor_tensor(sc8, ge, grs[0:S].unsqueeze(2).broadcast_to([S, B, E]), ALU.mult).then_inc(g_step, 1)
            V.tensor_copy(wtm[0:S, :, E + 1:E + 2], wtm[0:S, :, E:E + 1]).then_inc(g_step, 1)
            dve.wait_ge(g_step, 8)
            dve.wait_ge(sent_set, 1)
            for b in range(B):
                last = V.max(out=top[0:S, b], in_=score[0:S, b])
            last.then_inc(g_step, 1)
            dve.wait_ge(g_step, 9)
            V.memset(top[0:S, :, TOPK:8], -1.0).then_inc(g_step, 1)
            dve.wait_ge(g_step, 10)
            for b in range(B):
                last = V.match_replace(picked[0:S, b], top[0:S, b], score[0:S, b], -2.0)
            last.then_inc(g_step, 1)
            dve.wait_ge(g_step, 11)
            V.scalar_tensor_tensor(out=wtm[0:S, :, 0:E], in0=picked[0:S, :, 0:E], scalar=-1.5, in1=sc8,
                                   op0=ALU.is_lt, op1=ALU.mult).then_inc(wtm_ready, 1)

            def multiply(j, n):
                r = ROWS[j % UNITS // 2]
                dve.wait_ge(silu_ready, n + 1)
                dve.wait_ge(hw_ready, n + 1)
                V.tensor_tensor(hu[0:r, j % 2], sg[0:r, j % 2], PB[5 + 2 * (j % 2)][0:r, 0:HN], ALU.mult).then_inc(hu_ready, 1)

            def hidden_lo(j, n):
                r = ROWS[j % UNITS // 2]
                dve.wait_ge(hhi_ready, n + 1)
                V.tensor_tensor(h_lo[j % 3][0:r], hw[0:r, j % 2], h_hi[j % 3][0:r].bitcast(F32), ALU.subtract).then_inc(hlo_ready, 1)

            V.sem_inc(hu_ready, 2)
            V.sem_inc(hlo_ready, 2)
            multiply(0, 0)

            def turn(i, last_turn):
                for j in range(PAIR):
                    if not (last_turn and j + 1 >= PAIR):
                        multiply((j + 1) % PAIR, i * PAIR + (j + 1))
                    hidden_lo(j, i * PAIR + j)
                    if last_turn and j >= UNITS:
                        continue
                    g = i * 2 + j // UNITS
                    slot = (j // UNITS + 1) % 2
                    if j % UNITS == 0:
                        dve.wait_ge(ld_w, (g + 2) * LD_W)
                        dve.wait_ge(down_done, g * UNITS + 3)
                        hi_gu(slot)
                    if j % UNITS == 1:
                        hi_dn(slot)

            with dve.Fori(0, GROUPS // 2 - 1) as i:
                turn(i, False)
            turn(GROUPS // 2 - 1, True)

            def add3(b):
                dve.wait_ge(y3_ps, b + 1)
                V.tensor_tensor(RES[0:S, b], PB[4 + b % 2][0:S, 0:D], X[0:S, b], ALU.add).then_inc(summed, 1)

            add_and_norm(3, XN, add3)
            for h in range(2):
                dve.wait_ge(lat_ps, h + 1)
                V.tensor_copy(latT[:, half(h)], PB[2 + h][0:R1, 0:HN]).then_inc(lat_ready, 1)
            dve.wait_ge(one1_set, 1)
            for b in range(B):
                dve.wait_ge(v1_ps, b + 1)
                V.tensor_copy(v1[0:S, b, :, 0:D1], PB[6 + b % 2][0:S].rearrange("p (h d) -> p h d", d=D1)).then_inc(v1_ready, 1)

            def out2(u):
                ps = PB[2 + u % 2][0:S, 0:QH * (D1 + 1)].rearrange("p (h d) -> p h d", d=D1 + 1)
                dst = a1[0:S, u // 2].rearrange("p (h j d) -> p h j d", j=2, d=D1)[:, :, u % 2, :]
                softmax_out(u, ps, rs2[0:S, QH * u:QH * (u + 1)], dst, D1, c2_ps, c2_rs, c2_ready)

            for u in range(U2 + 5):
                if u < U2:
                    softmax_in(u, s2_ps, max2, e2, eT2_ps, s2_max, s2_sub)
                if u >= 5:
                    out2(u - 5)

            def add4(b):
                dve.wait_ge(y4_ps, b + 1)
                V.tensor_tensor(RES[0:S, b], PB[4 + b % 2][0:S, 0:D], XN[0:S, b], ALU.add).then_inc(summed, 1)

            add_and_norm(4, X, add4)

            def add5(b):
                dve.wait_ge(y5_ps, b + 1)
                V.tensor_tensor(RES[0:S, b], PB[2 + b % 2][0:S, 0:D], X[0:S, b], ALU.add).then_inc(summed, 1)

            add_and_norm(5, XN, add5)
            dve.wait_ge(omm_ready, 1)
            dve.wait_ge(pad_zero, 1)
            n = 0
            for h in range(2):
                for a in (1, 0):
                    for k in range(KC):
                        dve.wait_ge(mixt_ready, n + 1)
                        V.scalar_tensor_tensor(out=mix[:, a, k, half(h)].rearrange("p (b s) -> p b s", s=S),
                                               in0=pad[:, k, h * HB:(h + 1) * HB, 0:S], scalar=omm[:, a, k:k + 1],
                                               in1=mixt[:, n % 2].rearrange("p (b s) -> p b s", s=S),
                                               op0=ALU.mult, op1=ALU.add).then_inc(mix_ready, 1)
                        n += 1
            for b in range(B + 1):
                if b < B:
                    dve.wait_ge(rexp_ready, b + 1)
                    V.tensor_scalar_add(rec[0:S, b % 2, 1], rec[0:S, b % 2, 0], 1.0).then_inc(r_step, 1)
                    dve.wait_ge(r_step, 2 * b + 1)
                    V.reciprocal(rec[0:S, b % 2, 1], rec[0:S, b % 2, 1]).then_inc(r_step, 1)
                    dve.wait_ge(y6_ps, b + 1)
                    dve.wait_ge(r_step, 2 * b + 2)
                    V.tensor_tensor(RES[0:S, b], PB[2 + b % 2][0:S, 0:D], rec[0:S, b % 2, 1], ALU.mult).then_inc(gated, 1)
                    dve.wait_ge(gated, b + 1)
                    V.tensor_tensor(RES[0:S, b], RES[0:S, b], XN[0:S, b], ALU.add).then_inc(summed, 1)
                    dve.wait_ge(summed, 5 * B + b + 1)
                    norm_stats(6, b)
                if b >= 1:
                    normalize(6, b - 1, X)


def _constants():
    half = D0 // 2
    pos = np.arange(S, dtype=np.float32)
    freqs = (np.float32(1.0) / np.float32(10000.0) ** (np.arange(half, dtype=np.float32) / np.float32(half))).astype(np.float32)
    ang = pos[:, None] * freqs[None, :]
    cos, sin = np.cos(ang).astype(np.float32), np.sin(ang).astype(np.float32)
    cc = np.concatenate([cos, cos], 1).T
    ss = np.concatenate([-sin, sin], 1).T
    rope = np.stack([np.tile(cc, (HC, 1)), np.tile(ss, (HC, 1))], 1)
    bf16 = mybir.dt.np(BF16)
    q, k = np.arange(S)[:, None], np.arange(S)[None, :]
    masked = (k > q) | (k < q - WINDOW)
    mask = np.tile(np.where(masked, np.float32(MASKED), np.float32(0)), (1, QH))
    return {
        "ident": np.eye(P, dtype=np.float32), "identb": np.eye(P).astype(bf16), "maskb": mask.astype(bf16),
        "rope": np.ascontiguousarray(rope, np.float32),
        "hmask": (np.arange(P)[:, None] // D0 == np.arange(HC)[None, :]).astype(np.float32),
    }


def _laid_out(a):
    def swapped(w):
        return w.reshape(H0, 2, D0 // 2, *w.shape[1:])[:, ::-1].reshape(w.shape)

    def cols(v):
        return v.reshape(KC, P).T

    ctx = a["ctx_1024"]
    gu, dn = a["L0_ffn_experts_gate_up"], a["L0_ffn_experts_down"]
    sg, su, sd = a["L0_ffn_shared_gate_w"], a["L0_ffn_shared_up_w"], a["L0_ffn_shared_down_w"]
    shared_gu = np.concatenate([sg.reshape(-1, I, D), su.reshape(-1, I, D)], 1)
    shared_dn = sd.reshape(D, -1, I).transpose(1, 2, 0)
    qb, kb = a["L0_xattn_q_b"], a["L0_xattn_k_b"]
    qw, kw = a["L0_xattn_q_w"], a["L0_xattn_k_w"]
    out = {
        "x": a["x"],
        "cA": ctx[:, :S].transpose(2, 0, 1).reshape(D, N),
        "cT": ctx.transpose(2, 0, 1), "cN": ctx,
        "qkvT": a["L0_attn_qkv_w"].T, "qk_b": a["L0_attn_qkv_b"][:2 * D],
        "projT": a["L0_attn_proj_w"].T, "proj_b": a["L0_attn_proj_b"],
        "xqT": np.concatenate([qw, swapped(qw)], 0).T, "xkT": np.concatenate([kw, swapped(kw)], 0).T,
        "xvT": a["L0_xattn_v_w"].T, "xv_b": a["L0_xattn_v_b"],
        "xoT": a["L0_xattn_o_w"].T, "xo_b": a["L0_xattn_o_b"],
        "colb": np.concatenate([cols(v) for v in (
            a["L0_attn_norm_w"], a["L0_attn_norm_b"], a["L0_attn_qkv_b"][2 * D:],
            qb, swapped(qb), kb, swapped(kb))], 1),
        "gateT": np.concatenate([a["L0_ffn_gate_w"], a["L0_ffn_shared_expert_gate_w"]], 0).T,
        "guT": np.concatenate([gu, shared_gu], 0).transpose(0, 2, 1),
        "dnT": np.concatenate([dn.transpose(0, 2, 1), shared_dn], 0),
        "wqT": a["L1_attn_Wq"].T, "wkdT": a["L1_attn_Wkv_down"].T, "wkuT": a["L1_attn_Wk_up"].T,
        "wvuT": a["L1_attn_Wv_up"].T, "woT": a["L1_attn_Wo"].T,
        "wrT": a["L1_ffn_W_r"].T, "wkT": a["L1_ffn_W_k"].T, "wvT": a["L1_ffn_W_v"].T,
        "mu": np.concatenate([cols(a["L1_ffn_mu_r"]), cols(a["L1_ffn_mu_k"])], 1),
    }
    return {**out, **_constants()}


def kernel(**inputs):
    import concourse.bacc as bacc
    from concourse.bass_utils import run_bass_kernel_spmd

    nc = bacc.Bacc("TRN2", target_bir_lowering=False, num_devices=1)
    arrays, aps = {}, {}
    for name, a in _laid_out({k: np.asarray(v) for k, v in inputs.items()}).items():
        a = np.ascontiguousarray(a)
        arrays[f"in_{name}"] = a
        aps[name] = nc.dram_tensor(f"in_{name}", a.shape, mybir.dt.from_np(a.dtype), kind="ExternalInput").ap()
    out = nc.dram_tensor("out_x", (B, S, D), F32, kind="ExternalOutput").ap()
    build(nc, aps, out)
    r = run_bass_kernel_spmd(nc, [arrays], core_ids=[0])
    return r.results[0]["out_x"]
```

```python
from contextlib import ExitStack

import numpy as np

import concourse.bass as bass
from concourse import mybir

F32, F32R, BF16 = mybir.dt.float32, mybir.dt.float32r, mybir.dt.bfloat16
ACT = mybir.ActivationFunctionType
ALU = mybir.AluOpType
X_AXIS = mybir.AxisListType.X

B, S, D = 8, 100, 256
SK = 361
P = 128
KC = D // P
N = B * S
HB = B // 2
HN = HB * S
H0, D0, WINDOW = 16, 16, 64
HC = P // D0
QH = 4
E, I, TOPK = 8, 352, 2
SI = 704
HID = E * I + SI
NC = -(-HID // P)
NU = 2 * NC
TURN = 4
WT = 8
NW = E + 1
H1, D1, R1 = 8, 64, 64
QC = H1 * D1 // P
FC = -(-SK // P)
FROWS = [min(P, SK - f * P) for f in range(FC)]
EPS = 1e-5
NG = E + 2
MASKED = -3e38
SCALE0 = float(np.float32(1.0 / np.sqrt(S)))


def build(nc, I_, out):
    ctx = ExitStack()
    with ctx:
        def sb(name, shape, dt=F32, where=ctx):
            return where.enter_context(nc.sbuf_tensor(name, shape, dt))

        def sem(name):
            return ctx.enter_context(nc.semaphore(name))

        X = sb("X", [P, B, D])
        XN = sb("XN", [P, B, D])
        RES = sb("RES", [P, B, D])
        T0 = [sb(f"T0_{p}", [P, KC, N], F32R) for p in ("hi", "lo")]
        T1 = [sb(f"T1_{p}", [P, KC, N], F32R) for p in ("hi", "lo")]
        ident = sb("ident", [P, P])
        stats = sb("stats", [P, B, 6])
        mv = sb("mv", [P, B, 2])
        lnv = sb("lnv", [P, B])
        rstd = sb("rstd", [P, B])
        epsb = sb("epsb", [P, 1])
        zero16 = sb("zero16", [P, HN], BF16)

        work = ExitStack()
        w_gu = [sb(f"w_gu{s}", [P, KC, 2 * P], F32, work) for s in range(TURN)]
        w_dn = [sb(f"w_dn{s}", [P, D], F32, work) for s in range(TURN)]
        gu = [[sb(f"gu_{p}{s}", [P, KC, 2 * P], F32R, work) for p in ("hi", "lo")] for s in range(TURN)]
        dn = [[sb(f"dn_{p}{s}", [P, D], F32R, work) for p in ("hi", "lo")] for s in range(TURN)]

        with ExitStack() as r:
            qk = sb("qk", [P, B, 2 * D], F32, r)
            vT = sb("vT", [P, KC, N], F32, r)
            e0 = sb("e0", [P, 4, KC, D], F32, r)
            eT0 = sb("eT0", [P, 4, KC, D], F32, r)
            aT = sb("aT", [P, B, KC, S], F32, r)
        with ExitStack() as r:
            kblk = sb("kblk", [P, 4, HC, S], F32, r)
            e1 = sb("e1", [P, 4, QH, S], F32, r)
            eT1 = sb("eT1", [P, 4, QH, S], F32, r)
            ctxn = sb("ctxn", [P, B, D], F32, r)
            ctxnT = sb("ctxnT", [P, KC, N], F32, r)
        with ExitStack() as r:
            wb = sb("wb", [P, NW, N], F32, r)
            wrow = sb("wrow", [P, 2, N], F32, r)
        with ExitStack() as r:
            sb("until_e0", [P, B * 2 * D + KC * N], F32, r)
            raw_cA = sb("raw_cA", [P, KC, N], F32, r)
            raw_qkv = sb("raw_qkv", [P, KC, 3 * D], F32, r)
            raw_xk = sb("raw_xk", [P, KC, D], F32, r)
            raw_xv = sb("raw_xv", [P, KC, D], F32, r)
            raw_xq = sb("raw_xq", [P, KC, D], F32, r)
            hst = sb("hst", [P, 4, KC, S], F32, r)
        sb("place1", [P, B * 2 * D + 2 * KC * N + 8 * KC * D], F32, work)

        with ExitStack() as r:
            kr = sb("kr", [P, KC, N], F32, r)
            swap = sb("swap", [P, 2, HN], F32, r)
            rot = sb("rot", [P, 2, 2, HN], F32, r)
            with ExitStack() as early:
                cA = [sb(f"cA_{p}", [P, KC, N], F32R, early) for p in ("hi", "lo")]
            with ExitStack() as late:
                qr = sb("qr", [P, KC, N], F32, late)
            sb("context_place", [P, 2 * KC * N], F32, r)
            vaug = sb("vaug", [P, B, H0, D0 + 1], F32, r)
            qkvT = [sb(f"qkvT_{p}", [P, KC, 3 * D], F32R, r) for p in ("hi", "lo")]
            projT = sb("projT", [P, KC, D], F32, r)
            xqT = [sb(f"xqT_{p}", [P, KC, D], F32R, r) for p in ("hi", "lo")]
            xkT = [sb(f"xkT_{p}", [P, KC, D], F32R, r) for p in ("hi", "lo")]
            xvT = [sb(f"xvT_{p}", [P, KC, D], F32R, r) for p in ("hi", "lo")]
            xoT = sb("xoT", [P, KC, D], F32, r)
            qk_b = sb("qk_b", [P, 2 * D], F32, r)
            proj_b = sb("proj_b", [P, D], F32, r)
            xv_b = sb("xv_b", [P, D], F32, r)
            xo_b = sb("xo_b", [P, D], F32, r)
            colb = sb("colb", [P, 14], F32, r)
            rope = sb("rope", [P, 2, S], F32, r)
            hmask = sb("hmask", [P, HC], F32, r)
            identb = sb("identb", [P, P], BF16, r)
            maskb = sb("maskb", [P, QH * S], BF16, r)
            raw_gate = sb("raw_gate", [P, KC, NG], F32, r)
            gateT = [sb(f"gateT_{p}", [P, KC, NG], F32R, r) for p in ("hi", "lo")]
            max0 = sb("max0", [P, B, KC], F32, r)
            nb0 = sb("nb0", [P, B, KC], F32, r)
            sum0 = sb("sum0", [P, B, KC], F32, r)
            rs0 = sb("rs0", [P, B, KC], F32, r)
            max1 = sb("max1", [P, 8 * B * H0 // 8], F32, r)
            rs1 = sb("rs1", [P, B, H0], F32, r)
            gmax = sb("gmax", [P, B], F32, r)
            gexp = sb("gexp", [P, B, E + 1], F32, r)
            gsum = sb("gsum", [P, B], F32, r)
            grs = sb("grs", [P, B], F32, r)
            score = sb("score", [P, B, 2 * E], F32, r)
            top = sb("top", [P, B, 8], F32, r)
            picked = sb("picked", [P, B, 2 * E], F32, r)
            wtm = sb("wtm", [P, B, NW], F32, r)
            sig1 = sb("sig1", [P, B], F32, r)
        with ExitStack() as r:
            sg = sb("sg", [P, 2, HN], F32, r)
            hu = sb("hu", [P, 2, HN], F32, r)
            hw = sb("hw", [P, 2, HN], F32, r)
            hid = [[sb(f"hid_{p}{s}", [P, HN], F32R, r) for p in ("hi", "lo")] for s in range(4)]
        sb("rings", [P, 14 * HN], F32, work)
        with ExitStack() as r:
            wqT = [sb(f"wqT_{p}", [P, KC, H1 * D1], F32R, r) for p in ("hi", "lo")]
            wkdT = [sb(f"wkdT_{p}", [P, KC, 2 * R1], F32R, r) for p in ("hi", "lo")]
            wkuT = sb("wkuT", [2 * R1, H1 * D1], F32R, r)
            wvuT = sb("wvuT", [2 * R1, H1 * D1], F32R, r)
            raw_wq = sb("raw_wq", [P, KC, H1 * D1], F32, r)
            raw_wkd = sb("raw_wkd", [P, KC, 2 * R1], F32, r)
            raw_wku = sb("raw_wku", [2 * R1, H1 * D1], F32, r)
            raw_wvu = sb("raw_wvu", [2 * R1, H1 * D1], F32, r)
            woT = sb("woT", [P, QC, D], F32, r)
            wrT = sb("wrT", [P, KC, D], F32, r)
            wkT = sb("wkT", [P, KC, D], F32, r)
            wvT = sb("wvT", [P, KC, D], F32, r)
            mu = sb("mu", [P, 2, KC], F32, r)
            omm = sb("omm", [P, 2, KC], F32, r)
            max2 = sb("max2", [P, B * H1], F32, r)
            rs2 = sb("rs2", [P, B * H1], F32, r)
        work.close()

        with ExitStack() as r:
            q1T = sb("q1T", [P, QC, N], F32, r)
            k1T = sb("k1T", [P, QC, N], F32, r)
            latT = [sb(f"latT_{p}", [2 * R1, N], F32R, r) for p in ("hi", "lo")]
            e2 = sb("e2", [P, 4, QH, S], F32, r)
            eT2 = sb("eT2", [P, 4, QH, S], F32, r)
            v1 = sb("v1", [P, B, H1, D1 + 1], F32, r)
            a1T = sb("a1T", [P, 4, QC, S], F32, r)
            cT = sb("cT", [P, KC, B, SK], F32, r)
        with ExitStack() as r:
            fT = sb("fT", [P, KC, N], F32, r)
        with ExitStack() as r:
            cN = sb("cN", [P, B, FC, D], F32, r)
            gT = sb("gT", [P, B, FC, S], F32, r)
            x4T = sb("x4T", [P, KC, N], F32, r)
            pad = sb("pad", [P, KC, B, S + 1], F32, r)
            mix = sb("mix", [P, 2, KC, N], F32, r)
            mixt = sb("mixt", [P, 2, HN], F32, r)
            kpos = sb("kpos", [P, 2, HN], F32, r)
            ksq = sb("ksq", [P, KC, N], F32, r)
            rg = sb("rg", [P, B, D], F32, r)

        a1 = [X, RES]

        PB = [ctx.enter_context(nc.psum_tensor(f"PB{i}", [P, 512], F32)) for i in range(8)]

        ld_a, ld_k, ld_q, ld_v, ld_b, ld_c, ld_ct = [
            sem("ld_" + n) for n in ("a", "k", "q", "v", "b", "c", "ct")]
        ld_x = [sem(f"ld_x{h}") for h in range(2)]
        ld_w = [sem(f"ld_w{s}") for s in range(TURN)]
        ones_set, zero_set, sent_set = sem("ones_set"), sem("zero_set"), sem("sent_set")
        ln_st, ln_mv, ln_lg, ln_rs, ln_out = [sem("ln_" + n) for n in ("st", "mv", "lg", "rs", "out")]
        twice = sem("twice")
        summed = sem("summed")
        resid = sem("resid")
        split_hi, split_lo, split_dve = sem("split_hi"), sem("split_lo"), sem("split_dve")
        hT_ps, h_hi, hT_ready = sem("hT_ps"), sem("h_hi"), sem("hT_ready")
        h_ready = [sem("h_even"), sem("h_odd")]
        qk_ps, qk_ready = sem("qk_ps"), sem("qk_ready")
        vT_ps, vT_ready = sem("vT_ps"), sem("vT_ready")
        kp_ps, k_rot, kr_ready = sem("kp_ps"), sem("k_rot"), sem("kr_ready")
        v_ps, v_ready = sem("v_ps"), sem("v_ready")
        s0_ps, s0_max, s0_nb, s0_exp, s0_rs = [sem("s0_" + n) for n in ("ps", "max", "nb", "exp", "rs")]
        eT0_ps, eT0_ready = sem("eT0_ps"), sem("eT0_ready")
        aT_ps, aT_ready = sem("aT_ps"), sem("aT_ready")
        y1_ps = sem("y1_ps")
        x1T_ps, x1T_hi, x1T_ready = sem("x1T_ps"), sem("x1T_hi"), sem("x1T_ready")
        swapped = sem("swapped")
        qp_ps, q_rot, qr_ready = sem("qp_ps"), sem("q_rot"), sem("qr_ready")
        kblk_ready = sem("kblk_ready")
        s1_ps, s1_max, s1_sub, s1_exp = [sem("s1_" + n) for n in ("ps", "max", "sub", "exp")]
        eT1_ps, eT1_ready = sem("eT1_ps"), sem("eT1_ready")
        c1_ps, c1_rs, c1_ready = sem("c1_ps"), sem("c1_rs"), sem("c1_ready")
        cT1_ps, cT1_ready = sem("cT1_ps"), sem("cT1_ready")
        y2_ps = sem("y2_ps")
        x2T_ps, x2T_hi, x2T_ready = sem("x2T_ps"), sem("x2T_hi"), sem("x2T_ready")
        g_ps, g_step, g_exp, wtm_ready = sem("g_ps"), sem("g_step"), sem("g_exp"), sem("wtm_ready")
        wb_ps, wb_ready = sem("wb_ps"), sem("wb_ready")
        gu_hi_ready, w_hi_ready, gu_lo_ready, w_lo_ready = [sem(n) for n in ("gu_hi_ready", "w_hi_ready", "gu_lo_ready", "w_lo_ready")]
        gu_ps, silu_ready, hu_ready, hw_ready = sem("gu_ps"), sem("silu_ready"), sem("hu_ready"), sem("hw_ready")
        hhi_ready, hlo_ready, down_done = sem("hhi_ready"), sem("hlo_ready"), sem("down_done")
        load_turn, row_copy, wrow_ready = sem("load_turn"), sem("row_copy"), sem("wrow_ready")
        fT_ready = sem("fT_ready")
        y3_ps = sem("y3_ps")
        x3T_ps, x3T_hi, x3T_ready = sem("x3T_ps"), sem("x3T_hi"), sem("x3T_ready")
        lat_ps, lat_hi, lat_ready = sem("lat_ps"), sem("lat_hi"), sem("lat_ready")
        wc_hi, wc_whole, wc_ready = sem("wc_hi"), sem("wc_whole"), sem("wc_ready")
        q1_ps, q1_ready = sem("q1_ps"), sem("q1_ready")
        v1_ps, v1_ready, one1_set = sem("v1_ps"), sem("v1_ready"), sem("one1_set")
        s2_ps, s2_max, s2_sub, s2_exp = [sem("s2_" + n) for n in ("ps", "max", "sub", "exp")]
        eT2_ps, eT2_ready = sem("eT2_ps"), sem("eT2_ready")
        c2_ps, c2_rs, c2_ready = sem("c2_ps"), sem("c2_rs"), sem("c2_ready")
        a1T_ps, a1T_ready = sem("a1T_ps"), sem("a1T_ready")
        y4_ps = sem("y4_ps")
        x4T_ps, x4T_ready = sem("x4T_ps"), sem("x4T_ready")
        g4_ps, gelu_ready = sem("g4_ps"), sem("gelu_ready")
        y5_ps = sem("y5_ps")
        x5T_ps, pad_ready, pad_zero = sem("x5T_ps"), sem("pad_ready"), sem("pad_zero")
        omm_ready, mixt_ready, mix_ready = sem("omm_ready"), sem("mixt_ready"), sem("mix_ready")
        kk_ps, kpos_ready, ksq_ready = sem("kk_ps"), sem("kpos_ready"), sem("ksq_ready")
        gated = sem("gated")
        r_ps, rg_ready, y6_ps = sem("r_ps"), sem("rg_ready"), sem("y6_ps")
        stored = sem("stored")

        def tok(b):
            return slice(b * S, (b + 1) * S)

        def half(h):
            return slice(h * HN, (h + 1) * HN)

        def heads(ap):
            return ap.rearrange("p (j s) -> p j s", s=S)

        def tripled(a, b, at, bt):
            return [(a[p][at], b[q][bt]) for p, q in ((0, 0), (0, 1), (1, 0))]

        def chunks(a, cols_a, b, cols_b):
            return [x for k in range(KC) for x in tripled(a, b, (slice(None), k, cols_a), (slice(None), k, cols_b))]

        EVERY = slice(None)

        UN, U2 = B * H0 // QH, B * H1 // QH
        HB4 = [PB[0], PB[1], PB[6], PB[7]]
        SB1 = [PB[4], PB[5], PB[2]]
        SB2 = [PB[4], PB[5], PB[0], PB[1]]

        OUT, CTXT, PROJECT, NORMED, X2T, X2T_LO = 9, 11, 12, 13, 17, 18

        def turn_of(u, first):
            b = (u - first) // QH
            return b if (u - first) % QH == 0 and 0 <= b < B else None

        block = ctx.enter_context(nc.Block())

        @block.sync
        def _(sp):
            def rows(name):
                return I_[name].rearrange("(k p) n -> p k n", p=P)

            def all_rows(name, width):
                return I_[name].rearrange("(o n) -> o n", o=1).broadcast_to([S, width])

            for h in range(2):
                sp.dma_start(X[0:S, h * HB:(h + 1) * HB], I_["x"][h * HB:(h + 1) * HB].rearrange("b s d -> s b d")).then_inc(ld_x[h], 16)
                if h == 0:
                    sp.dma_start(ident[:], I_["ident"]).then_inc(ld_a, 16)
                    sp.dma_start(colb[:], I_["colb"]).then_inc(ld_a, 16)
            sp.dma_start(raw_qkv[:], rows("qkvT")).then_inc(ld_q, 16)
            sp.dma_start(qk_b[0:S], all_rows("qk_b", 2 * D)).then_inc(ld_q, 16)
            sp.dma_start(raw_cA[:], rows("cA")).then_inc(ld_k, 16)
            sp.dma_start(raw_xk[:], rows("xkT")).then_inc(ld_k, 16)
            sp.dma_start(raw_xv[:], rows("xvT")).then_inc(ld_v, 16)
            sp.dma_start(rope[:], I_["rope"]).then_inc(ld_v, 16)
            sp.dma_start(xv_b[0:S], all_rows("xv_b", D)).then_inc(ld_v, 16)
            sp.dma_start(raw_xq[:], rows("xqT")).then_inc(ld_v, 16)
            sp.dma_start(raw_gate[:], rows("gateT")).then_inc(ld_v, 16)
            sp.dma_start(proj_b[0:S], all_rows("proj_b", D)).then_inc(ld_b, 16)
            sp.dma_start(projT[:], rows("projT")).then_inc(ld_b, 16)
            sp.dma_start(hmask[:], I_["hmask"]).then_inc(ld_b, 16)
            sp.dma_start(identb[:], I_["identb"]).then_inc(ld_b, 16)
            sp.dma_start(maskb[0:S], I_["maskb"]).then_inc(ld_b, 16)
            sp.dma_start(xoT[:], rows("xoT")).then_inc(ld_b, 16)
            sp.dma_start(xo_b[0:S], all_rows("xo_b", D)).then_inc(ld_b, 16)

            def load_chunk(c, slot):
                gate_up = I_["guT"].rearrange("c (k p) n -> p c k n", p=P)
                sp.dma_start(w_gu[slot][:], gate_up[:, bass.ds(c, 1)].rearrange("p c k n -> p (c k) n")).then_inc(ld_w[slot], 16)
                down = I_["dnT"].rearrange("c p n -> p c n")
                sp.dma_start(w_dn[slot][:], down[:, bass.ds(c, 1)].rearrange("p c n -> p (c n)")).then_inc(ld_w[slot], 16)

            for c in range(TURN):
                load_chunk(c, c)
            sp.wait_ge(wb_ready, 3 * B)
            sp.dma_start(raw_wq[:], rows("wqT")).then_inc(ld_c, 16)
            for i in range(2):
                sp.dma_start(raw_wkd[:, :, i * R1:(i + 1) * R1], rows("wkdT")).then_inc(ld_c, 16)
                sp.dma_start(raw_wku[i * R1:(i + 1) * R1], I_["wkuT"]).then_inc(ld_c, 16)
                sp.dma_start(raw_wvu[i * R1:(i + 1) * R1], I_["wvuT"]).then_inc(ld_c, 16)
            sp.dma_start(woT[:], rows("woT")).then_inc(ld_c, 16)
            sp.dma_start(wrT[:], rows("wrT")).then_inc(ld_c, 16)
            sp.dma_start(wkT[:], rows("wkT")).then_inc(ld_c, 16)
            sp.dma_start(wvT[:], rows("wvT")).then_inc(ld_c, 16)
            sp.dma_start(mu[:], I_["mu"].rearrange("p (a k) -> p a k", a=2)).then_inc(ld_c, 16)
            with sp.Fori(1, NC // TURN) as i:
                for s in range(TURN):
                    first = sp.snap(i * TURN + s)
                    sp.wait_ge(w_lo_ready, first - (TURN - 1))
                    sp.sem_inc(load_turn, 1)
                    load_chunk(first, s)
            cf = (FC - 1) * P
            sp.wait_ge(fT_ready, 4)
            sp.dma_start(cT[:], I_["cT"].rearrange("(k p) b n -> p k b n", p=P)).then_inc(ld_ct, 16)
            sp.wait_ge(s2_ps, U2)
            for b in range(B):
                sp.dma_start(cN[:, b, 0:FC - 1], I_["cN"][b, 0:cf].rearrange("(f p) d -> p f d", p=P)).then_inc(ld_ct, 16)
            sp.dma_start(cN[0:SK - cf, :, FC - 1], I_["cN"][:, cf:SK].rearrange("b p d -> p b d")).then_inc(ld_ct, 16)
            for b in range(B):
                sp.wait_ge(ln_out, 6 * B + b + 1)
                sp.dma_start(out[b], X[0:S, b]).then_inc(stored, 16)
            sp.wait_ge(stored, 16 * B)
        LD_A, LD_K, LD_Q, LD_V, LD_B, LD_W, LD_C, LD_CT = [16 * n for n in (2, 2, 2, 5, 7, 2, 12, B + 2)]

        @block.tensor
        def _(pe):
            mm = nc.tensor.matmul

            def to_cm(src, bank, b):
                for k in range(KC):
                    last = nc.tensor.transpose(bank[:, k * S:(k + 1) * S], src[0:S, b, k * P:(k + 1) * P], ident[0:S, 0:S])
                return last

            def product(out_, pairs):
                for n, (a, m) in enumerate(pairs):
                    last = mm(out_, a, m, start=(n == 0), stop=(n == len(pairs) - 1))
                return last

            def behind(sums, transposed):
                for b in range(B + 3):
                    if b < B:
                        sums(b)
                    if b >= 3:
                        transposed(b - 3)

            pe.wait_ge(ld_a, LD_A)
            for b in range(B):
                pe.wait_ge(ln_out, b + 1)
                if b >= 4:
                    pe.wait_ge(hT_ready, b - 3)
                to_cm(XN, HB4[b % 4], b).then_inc(hT_ps, 1)
            pe.wait_ge(split_dve, 1)
            for b in range(B):
                pe.wait_ge(hT_ready, b + 1)
                if b >= 2:
                    pe.wait_ge(qk_ready, b - 1)
                product(PB[2 + b % 2][0:S, :], chunks(T0, tok(b), qkvT, slice(0, 2 * D))).then_inc(qk_ps, 1)
            pe.wait_ge(split_dve, 2)
            for h in range(2):
                for m in range(KC):
                    if h:
                        pe.wait_ge(vT_ready, m + 1)
                    product(PB[4 + m][:, 0:HN], chunks(qkvT, slice(2 * D + m * P, 2 * D + (m + 1) * P), T0, half(h))).then_inc(vT_ps, 1)
            def keys1(n):
                if n < 2:
                    pe.wait_ge(vT_ready, 3 + n)
                else:
                    pe.wait_ge(k_rot, 2 * (n - 1))
                if n == 0:
                    pe.wait_ge(split_lo, 2)
                m = n % 2
                product(PB[4 + n % 2][:, 0:HN], chunks(xkT, slice(m * P, (m + 1) * P), cA, half(n // 2))).then_inc(kp_ps, 1)

            def values_of_context(b):
                if b < 2:
                    pe.wait_ge(k_rot, 6 + 2 * b)
                else:
                    pe.wait_ge(v_ready, b - 1)
                if b == 0:
                    pe.wait_ge(split_lo, 3)
                product(PB[4 + b % 2][0:S, 0:D], chunks(cA, tok(b), xvT, EVERY)).then_inc(v_ps, 1)

            def scores0(b):
                if b >= 2:
                    pe.wait_ge(s0_exp, b - 1)
                pe.wait_ge(qk_ready, b + 1)
                for q in range(KC):
                    last = product(PB[6 + b % 2][:, q * D:(q + 1) * D], [(qk[0:S, b, q * P:(q + 1) * P], qk[0:S, b, D:2 * D])])
                last.then_inc(s0_ps, 1)

            def transposes0(b):
                if b < 2:
                    pe.wait_ge(hT_ready, B)
                else:
                    pe.wait_ge(eT0_ready, b - 1)
                pe.wait_ge(s0_exp, b + 1)
                for k in range(KC):
                    for q in range(KC):
                        last = nc.tensor.transpose(PB[b % 2][:, k * D + q * P:k * D + (q + 1) * P],
                                                   e0[:, b % 4, q, k * P:(k + 1) * P], ident[:])
                last.then_inc(eT0_ps, 1)

            def values0(b):
                if b < 2:
                    pe.wait_ge(qk_ready, B)
                else:
                    pe.wait_ge(aT_ready, b - 1)
                pe.wait_ge(eT0_ready, b + 1)
                pe.wait_ge(vT_ready, 2 * (b // HB) + 2)
                for q in range(KC):
                    last = product(PB[2 + b % 2][:, q * S:(q + 1) * S],
                                   [(eT0[:, b % 4, k, q * P:(q + 1) * P], vT[:, k, tok(b)]) for k in range(KC)])
                last.then_inc(aT_ps, 1)

            for b in range(B + 4):
                if b < B:
                    scores0(b)
                if 2 <= b < B + 2:
                    transposes0(b - 2)
                if b < 4:
                    keys1(b)
                else:
                    values_of_context(b - 4)
                if b >= 4:
                    values0(b - 4)
            pe.wait_ge(ld_b, LD_B)
            def project0(b):
                if b < 2:
                    pe.wait_ge(v_ready, B)
                else:
                    pe.wait_ge(summed, b - 1)
                pe.wait_ge(aT_ready, b + 1)
                product(PB[4 + b % 2][0:S, 0:D], [(aT[:, b, q, :], projT[:, q, :]) for q in range(KC)]).then_inc(y1_ps, 1)

            def x1_to_cm(b):
                if b < 2:
                    pe.wait_ge(eT0_ready, B)
                else:
                    pe.wait_ge(x1T_ready, b - 1)
                pe.wait_ge(ln_out, B + b + 1)
                to_cm(XN, PB[b % 2], b).then_inc(x1T_ps, 1)

            behind(project0, x1_to_cm)
            pe.wait_ge(split_dve, 3)
            pe.wait_ge(aT_ready, B)
            for n, (h, m) in enumerate([(h, m) for h in range(2) for m in range(KC)]):
                if n >= 2:
                    pe.wait_ge(q_rot, 2 * (n - 1))
                pe.wait_ge(x1T_ready, HB * (h + 1))
                product(PB[2 + n % 2][:, 0:HN], chunks(xqT, slice(m * P, (m + 1) * P), T1, half(h))).then_inc(qp_ps, 1)

            def scores1(u):
                b, c, j = u // 4, u // 2 % 2, u % 2
                bank = SB1[u % 3][0:S, 0:QH * S]
                if u == 0:
                    pe.wait_ge(summed, B)
                elif u == 2:
                    pe.wait_ge(q_rot, 8)
                elif u >= 3:
                    pe.wait_ge(s1_sub, u - 2)
                pe.wait_ge(qr_ready, 2 * (b // HB) + c + 1)
                pe.wait_ge(kblk_ready, u // 2 + 1)
                product(bank, [(qr[:, c, tok(b)], kblk[:, u // 2 % 4, QH * j:QH * (j + 1), :]),
                               (identb[0:S, 0:S], maskb[0:S, :])]).then_inc(s1_ps, 1)

            def transposes1(u):
                if u < 2:
                    pe.wait_ge(s0_exp, B)
                else:
                    pe.wait_ge(eT1_ready, u - 1)
                pe.wait_ge(s1_exp, u + 1)
                for h in range(QH):
                    last = nc.tensor.transpose(PB[6 + u % 2][0:S, h * S:(h + 1) * S], e1[0:S, u % 4, h, :], ident[0:S, 0:S])
                last.then_inc(eT1_ps, 1)

            def values1(u):
                b, w = u // 4, D0 + 1
                if u % 4 == 0:
                    if b < 2:
                        pe.wait_ge(x1T_ready, B)
                    else:
                        pe.wait_ge(c1_ready, b - 1)
                pe.wait_ge(eT1_ready, u + 1)
                for h in range(QH):
                    hh = QH * (u % 4) + h
                    last = product(PB[b % 2][0:S, hh * w:(hh + 1) * w], [(eT1[0:S, u % 4, h, :], vaug[0:S, b, hh, :])])
                if u % 4 == 3:
                    last.then_inc(c1_ps, 1)

            def ctx_to_cm(b):
                if b:
                    pe.wait_ge(summed, B + b)
                if b >= 2:
                    pe.wait_ge(x2T_ready, b - 1)
                pe.wait_ge(c1_ready, b + 1)
                to_cm(ctxn, PB[3], b).then_inc(cT1_ps, 1)

            def project1(b):
                pe.wait_ge(cT1_ready, b + 1)
                product(PB[3][0:S, 0:D], [(ctxnT[:, k, tok(b)], xoT[:, k, :]) for k in range(KC)]).then_inc(y2_ps, 1)

            def x2_to_cm(b):
                pe.wait_ge(summed, B + min(b + 2, B))
                if b == B - 1:
                    pe.wait_ge(x2T_ready, b)
                pe.wait_ge(ln_out, 2 * B + b + 1)
                to_cm(X, PB[3], b).then_inc(x2T_ps, 1)

            def gate_up(j, n):
                slot, t = j // 2 % TURN, j % 2
                pe.wait_ge(hu_ready, n + 1)
                for up in range(2):
                    last = product(PB[4 + 2 * t + up][:, 0:HN], chunks(gu[slot], slice(up * P, (up + 1) * P), T0, half(t)))
                last.then_inc(gu_ps, 1)

            for u in range(QH * (B - 1) + X2T + 1):
                if u < UN:
                    scores1(u)
                if 3 <= u < UN + 3:
                    transposes1(u - 3)
                for first, step in ((CTXT, ctx_to_cm), (PROJECT, project1), (X2T, x2_to_cm)):
                    b = turn_of(u, first)
                    if b is not None:
                        step(b)
                if 5 <= u < UN + 5:
                    values1(u - 5)
            pe.wait_ge(split_dve, 5)
            for b in range(B):
                pe.wait_ge(x2T_ready, b + 1)
                product(PB[2][0:S, b * NG:(b + 1) * NG], chunks(T0, tok(b), gateT, EVERY)).then_inc(g_ps, 1)

            acc = [[PB[2 * hc + t][:, 0:HN] for t in range(2)] for hc in range(KC)]

            def down(j, n, last_turn):
                slot, t = j // 2 % TURN, j % 2
                pe.wait_ge(hlo_ready, n + 1 + 2)
                for hc in range(KC):
                    pairs = tripled(dn[slot], hid[j % 4], (EVERY, slice(hc * P, (hc + 1) * P)), EVERY)
                    for i, (a, v) in enumerate(pairs):
                        last = mm(acc[hc][t], a, v, start=False, stop=last_turn and j >= WT - 2 and i == 2)
                last.then_inc(down_done, 1)

            pe.wait_ge(eT1_ready, UN)
            pe.wait_ge(w_lo_ready, 1)
            gate_up(0, 0)
            gate_up(1, 1)
            pe.wait_ge(wtm_ready, 1)
            for n, (b, c) in enumerate([(b, c) for b in range(B) for c in range(3)]):
                if n >= 4:
                    pe.wait_ge(wb_ready, n - 3)
                for j, g in enumerate(range(4 * c, min(4 * c + 4, NW))):
                    last = nc.tensor.transpose(PB[n % 4][:, j * S:(j + 1) * S],
                                               wtm[0:S, b, g:g + 1].broadcast_to([S, P]), ident[0:S, 0:S])
                last.then_inc(wb_ps, 1)
            pe.wait_ge(zero_set, 1)
            pe.wait_ge(wb_ready, 3 * B)
            for hc in range(KC):
                for t in range(2):
                    mm(acc[hc][t], zero16[:, 0:P], zero16[:], start=True, stop=False).then_inc(down_done, 1)

            def turn(i, last_turn):
                for j in range(WT):
                    if not (last_turn and j + 2 >= WT):
                        if j % 2 == 0:
                            pe.wait_ge(w_lo_ready, i * TURN + (j // 2 + 2))
                        gate_up(j + 2, i * WT + (j + 2))
                    down(j, i * WT + j, last_turn)

            with pe.Fori(0, NC // TURN - 1) as i:
                turn(i, False)
            turn(NC // TURN - 1, True)

            def result_to_tm(b):
                if b < 2:
                    pe.wait_ge(hu_ready, NU + 2)
                else:
                    pe.wait_ge(summed, 2 * B + b - 1)
                pe.wait_ge(fT_ready, 2 * (b // HB) + 2)
                for k in range(KC):
                    last = nc.tensor.transpose(PB[4 + b % 2][0:S, k * P:(k + 1) * P], fT[:, k, tok(b)], ident[:])
                last.then_inc(y3_ps, 1)

            def x3_to_cm(b):
                if b >= 2:
                    pe.wait_ge(x3T_ready, b - 1)
                pe.wait_ge(ln_out, 3 * B + b + 1)
                to_cm(XN, PB[6 + b % 2], b).then_inc(x3T_ps, 1)

            behind(result_to_tm, x3_to_cm)
            pe.wait_ge(wc_ready, 1)
            pe.wait_ge(fT_ready, 4)
            n = 0
            for h in range(2):
                pe.wait_ge(x3T_ready, HB * (h + 1))
                product(PB[2 + h][:, 0:HN], chunks(wkdT, EVERY, T1, half(h))).then_inc(lat_ps, 1)
                for kind in range(2):
                    for m in range(QC):
                        if n >= 2:
                            pe.wait_ge(q1_ready, n - 1)
                        cols = slice(m * P, (m + 1) * P)
                        if kind == 0:
                            pairs = chunks(wqT, cols, T1, half(h))
                        else:
                            pe.wait_ge(lat_ready, h + 1)
                            pairs = [(wkuT[:, cols], latT[p][:, half(h)]) for p in range(2)]
                        product(PB[n % 2][:, 0:HN], pairs).then_inc(q1_ps, 1)
                        n += 1
            for b in range(B):
                if b < 2:
                    pe.wait_ge(x3T_ready, B)
                else:
                    pe.wait_ge(v1_ready, b - 1)
                product(PB[6 + b % 2][0:S, :], [(latT[p][:, tok(b)], wvuT[:]) for p in range(2)]).then_inc(v1_ps, 1)

            def scores2(u):
                b, j = u // 2, u % 2
                if u < 2:
                    pe.wait_ge(summed, 3 * B)
                elif u >= 4:
                    pe.wait_ge(s2_sub, u - 3)
                for h in range(QH):
                    c, lo = h, j * D1
                    last = product(SB2[u % 4][0:S, h * S:(h + 1) * S],
                                   [(q1T[lo:lo + D1, c, tok(b)], k1T[lo:lo + D1, c, tok(b)])])
                last.then_inc(s2_ps, 1)

            def transposes2(u):
                if u < 2:
                    pe.wait_ge(v1_ready, B)
                else:
                    pe.wait_ge(eT2_ready, u - 1)
                pe.wait_ge(s2_exp, u + 1)
                for h in range(QH):
                    last = nc.tensor.transpose(PB[6 + u % 2][0:S, h * S:(h + 1) * S], e2[0:S, u % 4, h, :], ident[0:S, 0:S])
                last.then_inc(eT2_ps, 1)

            def values2(u):
                w = D1 + 1
                if u >= 2:
                    pe.wait_ge(c2_ready, u - 1)
                pe.wait_ge(eT2_ready, u + 1)
                for h in range(QH):
                    last = product(PB[2 + u % 2][0:S, h * w:(h + 1) * w],
                                   [(eT2[0:S, u % 4, h, :], v1[0:S, u // 2, 2 * h + u % 2, :])])
                last.then_inc(c2_ps, 1)

            pe.wait_ge(q1_ready, 2 * 2 * QC)
            for u in range(U2 + 5):
                if u < U2:
                    scores2(u)
                if 3 <= u < U2 + 3:
                    transposes2(u - 3)
                if u >= 5:
                    values2(u - 5)
            pe.wait_ge(s2_sub, U2)

            def project(b):
                product(PB[4 + b % 2][0:S, 0:D], [(a1T[:, b % 4, c, :], woT[:, c, :]) for c in range(QC)]).then_inc(y4_ps, 1)

            for b in range(B):
                if b >= 2:
                    pe.wait_ge(a1T_ready, b - 1)
                pe.wait_ge(c2_ready, 2 * b + 2)
                for c in range(QC):
                    last = nc.tensor.transpose(PB[b % 2][:, c * S:(c + 1) * S],
                                               a1[c // 2][0:S, b, c % 2 * P:(c % 2 + 1) * P], ident[0:S, 0:S])
                last.then_inc(a1T_ps, 1)
                if b >= 1:
                    pe.wait_ge(a1T_ready, b)
                if b >= 3:
                    pe.wait_ge(summed, 3 * B + b - 2)
                if b >= 1:
                    project(b - 1)
            pe.wait_ge(a1T_ready, B)
            pe.wait_ge(summed, 3 * B + B - 2)
            project(B - 1)
            for b in range(B):
                if b < 2:
                    pe.wait_ge(eT2_ready, U2)
                else:
                    pe.wait_ge(x4T_ready, b - 1)
                pe.wait_ge(ln_out, 4 * B + b + 1)
                to_cm(X, PB[6 + b % 2], b).then_inc(x4T_ps, 1)
            pe.wait_ge(ld_ct, LD_CT)
            for b in range(B):
                if b < 2:
                    pe.wait_ge(a1T_ready, B)
                else:
                    pe.wait_ge(gelu_ready, b - 1)
                pe.wait_ge(x4T_ready, b + 1)
                for f, r in enumerate(FROWS):
                    last = product(PB[b % 2][0:r, f * S:(f + 1) * S],
                                   [(cT[:, k, b, f * P:f * P + r], x4T[:, k, tok(b)]) for k in range(KC)])
                last.then_inc(g4_ps, 1)
            for b in range(B):
                if b < 2:
                    pe.wait_ge(c2_ready, U2)
                else:
                    pe.wait_ge(summed, 4 * B + b - 1)
                pe.wait_ge(gelu_ready, b + 1)
                product(PB[2 + b % 2][0:S, 0:D], [(gT[0:r, b, f, :], cN[0:r, b, f, :]) for f, r in enumerate(FROWS)]).then_inc(y5_ps, 1)
            for b in range(B):
                if b < 2:
                    pe.wait_ge(summed, 4 * B)
                else:
                    pe.wait_ge(pad_ready, b - 1)
                pe.wait_ge(ln_out, 5 * B + b + 1)
                to_cm(XN, PB[4 + b % 2], b).then_inc(x5T_ps, 1)
            for b in range(B):
                if b < 2:
                    pe.wait_ge(gelu_ready, B)
                else:
                    pe.wait_ge(rg_ready, b - 1)
                pe.wait_ge(mix_ready, 2 if b < HB else 6)
                product(PB[b % 2][0:S, 0:D], [(mix[:, 0, k, tok(b)], wrT[:, k, :]) for k in range(KC)]).then_inc(r_ps, 1)
            for n, (h, m) in enumerate([(h, m) for h in range(2) for m in range(KC)]):
                if n < 2:
                    pe.wait_ge(x4T_ready, B)
                else:
                    pe.wait_ge(kpos_ready, n - 1)
                pe.wait_ge(mix_ready, 4 * h + 4)
                product(PB[6 + n % 2][:, 0:HN], [(wkT[:, k, m * P:(m + 1) * P], mix[:, 1, k, half(h)]) for k in range(KC)]).then_inc(kk_ps, 1)
            for b in range(B):
                if b < 2:
                    pe.wait_ge(summed, 5 * B)
                else:
                    pe.wait_ge(gated, b - 1)
                pe.wait_ge(ksq_ready, 2 * (b // HB) + 2)
                product(PB[2 + b % 2][0:S, 0:D], [(ksq[:, k, tok(b)], wvT[:, k, :]) for k in range(KC)]).then_inc(y6_ps, 1)

        @block.gpsimd
        def _(pool):
            TT = nc.gpsimd.tensor_tensor
            nc.gpsimd.memset(epsb[:], EPS).then_inc(ones_set, 1)
            nc.gpsimd.memset(vaug[0:S, :, :, D0:D0 + 1], 1.0).then_inc(ones_set, 1)
            nc.gpsimd.memset(zero16[:], 0.0).then_inc(zero_set, 1)
            nc.gpsimd.memset(score[0:S, :, E:2 * E], -1.0).then_inc(sent_set, 1)
            for b in range(B):
                pool.wait_ge(h_hi, b + 1)
                TT(T0[1][:, :, tok(b)], hst[:, b % 4], T0[0][:, :, tok(b)].bitcast(F32), ALU.subtract).then_inc(hT_ready, 1)
            for n, (dst, raw) in enumerate(((cA, raw_cA), (xkT, raw_xk), (xvT, raw_xv))):
                pool.wait_ge(split_hi, n + 3)
                TT(dst[1][:], raw[:], dst[0][:].bitcast(F32), ALU.subtract).then_inc(split_lo, 1)
            pool.wait_ge(ld_x[0], 16)
            pool.wait_ge(ld_x[1], 16)
            pool.wait_ge(ld_b, LD_B)
            for b in range(B):
                TT(RES[0:S, b], X[0:S, b], proj_b[0:S], ALU.add).then_inc(twice, 1)
            for b in range(B):
                pool.wait_ge(twice, b + 1)
                TT(RES[0:S, b], RES[0:S, b], X[0:S, b], ALU.add).then_inc(resid, 1)
            for n, (h, m) in enumerate([(h, m) for h in range(2) for m in range(KC)]):
                pool.wait_ge(k_rot, 2 * n + 2)
                TT(kr[:, m, half(h)], rot[:, n % 2, 0], rot[:, n % 2, 1], ALU.add).then_inc(kr_ready, 1)
            def key_blocks(n):
                b, c = n // 2, n % 2
                if n >= 4:
                    pool.wait_ge(s1_ps, 2 * (n - 4) + 2)
                pool.wait_ge(kr_ready, 2 * (b // HB) + c + 1)
                TT(kblk[:, n % 4], kr[:, c, tok(b)].unsqueeze(1).broadcast_to([P, HC, S]),
                   hmask[:].unsqueeze(2).broadcast_to([P, HC, S]), ALU.mult).then_inc(kblk_ready, 1)

            pool.wait_ge(s0_ps, B)
            for n in range(4):
                key_blocks(n)
            for b in range(B):
                pool.wait_ge(ln_out, B + b + 1)
                TT(RES[0:S, b], XN[0:S, b], xo_b[0:S], ALU.add).then_inc(resid, 1)
            for n, (h, m) in enumerate([(h, m) for h in range(2) for m in range(KC)]):
                pool.wait_ge(q_rot, 2 * n + 2)
                TT(qr[:, m, half(h)], rot[:, n % 2, 0], rot[:, n % 2, 1], ALU.add).then_inc(qr_ready, 1)
            for n in range(4, 2 * B):
                key_blocks(n)
            copies = 0
            for c in range(NC):
                if c == 0:
                    pool.wait_ge(wb_ready, 3 * B)
                if c >= 2:
                    pool.wait_ge(hw_ready, 2 * (c - 1))
                row, until = c * P, (c + 1) * P
                while row < until:
                    x = min(row // I, E)
                    end = until if x == E else min(until, (x + 1) * I)
                    if row % P == P // 4:
                        end = min(end, row + P // 4)
                    rows = slice(row % P, row % P + end - row)
                    if copies:
                        pool.wait_ge(row_copy, copies)
                    nc.gpsimd.tensor_copy(wrow[rows, c % 2], wb[rows, x]).then_inc(row_copy, 1)
                    copies += 1
                    row = end
                pool.wait_ge(row_copy, copies)
                nc.gpsimd.sem_inc(wrow_ready, 1)

            pool.wait_ge(wc_hi, 4)
            TT(wkdT[1][:], raw_wkd[:], wkdT[0][:].bitcast(F32), ALU.subtract)
            TT(wqT[1][:], raw_wq[:], wqT[0][:].bitcast(F32), ALU.subtract).then_inc(wc_whole, 1)
            pool.wait_ge(wc_whole, 1)
            for w, raw in ((wkuT, raw_wku), (wvuT, raw_wvu)):
                last = TT(w[R1:], raw[R1:], w[R1:].bitcast(F32), ALU.subtract)
            last.then_inc(wc_ready, 1)
            pool.wait_ge(wc_ready, 1)
            pool.wait_ge(fT_ready, 4)
            nc.gpsimd.memset(v1[0:S, :, :, D1:D1 + 1], 1.0).then_inc(one1_set, 1)
            pool.wait_ge(ld_c, LD_C)
            nc.gpsimd.tensor_scalar(omm[:], mu[:], -1.0, 1.0, ALU.mult, ALU.add).then_inc(omm_ready, 1)
            pool.wait_ge(g4_ps, 1)
            nc.gpsimd.memset(pad[:, :, :, 0:1], 0.0).then_inc(pad_zero, 1)
            for n, (h, m) in enumerate([(h, m) for h in range(2) for m in range(KC)]):
                pool.wait_ge(kpos_ready, n + 1)
                TT(ksq[:, m, half(h)], kpos[:, n % 2], kpos[:, n % 2], ALU.mult).then_inc(ksq_ready, 1)

        @block.scalar
        def _(act):
            A = nc.scalar.activation

            def norm_scale(k, b):
                act.wait_ge(ln_mv, k * B + b + 1)
                A(lnv[0:S, b:b + 1], mv[0:S, b, 1:2], ACT.Ln, bias=epsb[0:S]).then_inc(ln_lg, 1)
                act.wait_ge(ln_lg, k * B + b + 1)
                A(rstd[0:S, b:b + 1], lnv[0:S, b:b + 1], ACT.Exp, scale=-0.5).then_inc(ln_rs, 1)

            def norms_then(k, evac):
                for b in range(B + 3):
                    if b < B:
                        norm_scale(k, b)
                    if b >= 3:
                        evac(b - 3)

            def cm_copy(ps_ready, banks, dst, done):
                dst = dst[0] if isinstance(dst, list) else dst

                def evac(b):
                    act.wait_ge(ps_ready, b + 1)
                    A(dst[:, :, tok(b)], banks[b % len(banks)][:, 0:KC * S].rearrange("p (k s) -> p k s", s=S), ACT.Copy).then_inc(done, 1)
                return evac

            nc.scalar.preload_act_table_set("natural_log_exp_and_others")
            act.wait_ge(ones_set, 1)

            def hi_of(dst, raw, cols=slice(None)):
                A(dst[0][:, :, cols], raw[:, :, cols], ACT.Copy).then_inc(split_hi, 1)

            def h_of(b):
                act.wait_ge(hT_ps, b + 1)
                if b >= 4:
                    act.wait_ge(hT_ready, b - 3)
                for k in range(KC):
                    last = A(hst[:, b % 4, k, :], HB4[b % 4][:, k * S:(k + 1) * S], ACT.Identity,
                             bias=colb[:, 2 + k:3 + k], scale=colb[:, k:k + 1])
                last.then_inc(h_ready[1], 1)

            def h_hi_of(b):
                if b == 1:
                    act.wait_ge(ld_a, LD_A)
                if b % 2:
                    h_of(b)
                act.wait_ge(h_ready[b % 2], b // 2 + 1)
                A(T0[0][:, :, tok(b)], hst[:, b % 4], ACT.Copy).then_inc(h_hi, 1)

            for b in range(B + 4):
                if b < B:
                    norm_scale(0, b)
                if b == B - 1:
                    act.wait_ge(ld_q, LD_Q)
                    hi_of(qkvT, raw_qkv, slice(0, 2 * D))
                if b >= 4:
                    h_hi_of(b - 4)
            hi_of(qkvT, raw_qkv, slice(2 * D, 3 * D))
            act.wait_ge(ld_k, LD_K)
            hi_of(cA, raw_cA)
            hi_of(xkT, raw_xk)
            act.wait_ge(ld_v, LD_V)
            hi_of(xvT, raw_xv)
            hi_of(xqT, raw_xq)
            for n, (h, m) in enumerate([(h, m) for h in range(2) for m in range(KC)]):
                act.wait_ge(vT_ps, n + 1)
                A(vT[:, m, half(h)], PB[4 + m][:, 0:HN], ACT.Identity, bias=colb[:, 4 + m:5 + m]).then_inc(vT_ready, 1)

            def weights_hi(slot):
                A(gu[slot][0][:], w_gu[slot][:], ACT.Copy)
                A(dn[slot][0][:], w_dn[slot][:], ACT.Copy).then_inc(w_hi_ready, 1)

            def exp0(b):
                act.wait_ge(s0_nb, b + 1)
                if b >= 4:
                    act.wait_ge(eT0_ps, b - 3)
                for q in range(KC):
                    last = A(e0[:, b % 4, q, :], PB[6 + b % 2][:, q * D:(q + 1) * D], ACT.Exp,
                             bias=nb0[:, b, q:q + 1], scale=SCALE0, accum_out=sum0[:, b, q:q + 1])
                last.then_inc(s0_exp, 1)

            def a_evac(b):
                act.wait_ge(aT_ps, b + 1)
                act.wait_ge(s0_rs, b + 1)
                for q in range(KC):
                    last = A(aT[:, b, q, :], PB[2 + b % 2][:, q * S:(q + 1) * S], ACT.Copy, scale=rs0[:, b, q:q + 1])
                last.then_inc(aT_ready, 1)

            act.wait_ge(split_lo, 3)
            act.wait_ge(split_dve, 3)
            for b in range(B + 4):
                if b < B:
                    exp0(b)
                if b >= 4:
                    a_evac(b - 4)
            norms_then(1, cm_copy(x1T_ps, PB[0:2], T1, x1T_hi))

            def exps(u, n_units, sub, e, scale, done):
                act.wait_ge(sub, u + 1)
                A(e[0:S, u % 4], e[0:S, u % 4], ACT.Exp, scale=scale).then_inc(done, 1)

            def exp_evac(u, ps_ready, eT, done):
                act.wait_ge(ps_ready, u + 1)
                A(eT[0:S, u % 4], heads(PB[6 + u % 2][0:S, 0:QH * S]), ACT.Copy).then_inc(done, 1)

            ctxn_evac = cm_copy(cT1_ps, [PB[3]], ctxnT, cT1_ready)
            x2_evac = cm_copy(x2T_ps, [PB[3]], T0, x2T_hi)
            for u in range(QH * (B - 1) + X2T + 1):
                if u in (UN // 2, UN // 2 + 4):
                    s = (u - UN // 2) // 4
                    act.wait_ge(ld_w[s], LD_W)
                    weights_hi(s)
                if u < UN:
                    exps(u, UN, s1_sub, e1, D0 ** -0.5, s1_exp)
                if 3 <= u < UN + 3:
                    exp_evac(u - 3, eT1_ps, eT1, eT1_ready)
                for first, step in ((CTXT, ctxn_evac), (PROJECT, lambda b: norm_scale(2, b)), (X2T, x2_evac)):
                    b = turn_of(u, first)
                    if b is not None:
                        step(b)
            act.wait_ge(g_step, 2)
            logits = PB[2][0:S, 0:B * NG].rearrange("p (b e) -> p b e", e=NG)
            A(gexp[0:S, :, E:E + 1], logits[:, :, E:E + 1], ACT.Exp, scale=-1.0).then_inc(g_exp, 1)
            A(gexp[0:S, :, 0:E], gexp[0:S, :, 0:E], ACT.Exp).then_inc(g_exp, 1)
            for n, (b, c) in enumerate([(b, c) for b in range(B) for c in range(3)]):
                act.wait_ge(wb_ps, n + 1)
                k = min(4, NW - 4 * c)
                A(wb[:, 4 * c:4 * c + k, tok(b)], heads(PB[n % 4][:, 0:k * S]), ACT.Copy).then_inc(wb_ready, 1)

            def silu(j, n):
                act.wait_ge(gu_ps, n + 1)
                act.wait_ge(hu_ready, n + 1)
                A(sg[:, j % 2], PB[4 + 2 * (j % 2)][:, 0:HN], ACT.Silu).then_inc(silu_ready, 1)

            def hidden_hi(j, n):
                act.wait_ge(hw_ready, n + 1)
                act.wait_ge(down_done, n + 1)
                A(hid[j % 4][0][:], hw[:, j % 2], ACT.Copy).then_inc(hhi_ready, 1)

            first_weights = [(wkdT[0][:], raw_wkd[:]), (wqT[0][:], raw_wq[:]), (wkuT[:], raw_wku[:]), (wvuT[:], raw_wvu[:])]

            def turn(i, last_turn):
                for j in range(WT):
                    silu(j, i * WT + j)
                    if last_turn and j < len(first_weights):
                        if j == 0:
                            act.wait_ge(ld_c, LD_C)
                        A(*first_weights[j], ACT.Copy).then_inc(wc_hi, 1)
                    hidden_hi(j, i * WT + j)
                    if j % 2 == 0 and not (last_turn and j // 2 + 2 >= TURN):
                        ahead = j // 2 + 2
                        act.wait_ge(ld_w[ahead % TURN], i * LD_W + (ahead // TURN + 1) * LD_W)
                        act.wait_ge(down_done, i * WT + (j + 2))
                        weights_hi(ahead % TURN)

            with act.Fori(0, NC // TURN - 1) as i:
                turn(i, False)
            turn(NC // TURN - 1, True)
            for t in range(2):
                act.wait_ge(down_done, NU + 4 - 1 + t)
                for hc in range(KC):
                    A(fT[:, hc, half(t)], PB[2 * hc + t][:, 0:HN], ACT.Copy).then_inc(fT_ready, 1)

            nc.scalar.preload_act_table_set("natural_log_exp_and_others")
            norms_then(3, cm_copy(x3T_ps, PB[6:8], T1, x3T_hi))
            n = 0
            for h in range(2):
                act.wait_ge(lat_ps, h + 1)
                A(latT[0][:, half(h)], PB[2 + h][:, 0:HN], ACT.Copy).then_inc(lat_hi, 1)
                for dst in (q1T, k1T):
                    for m in range(QC):
                        act.wait_ge(q1_ps, n + 1)
                        A(dst[:, m, half(h)], PB[n % 2][:, 0:HN], ACT.Copy).then_inc(q1_ready, 1)
                        n += 1
            for u in range(U2 + 3):
                if u < U2:
                    exps(u, U2, s2_sub, e2, D1 ** -0.5, s2_exp)
                if u >= 3:
                    exp_evac(u - 3, eT2_ps, eT2, eT2_ready)
            for b in range(B + 2):
                if b < B:
                    act.wait_ge(a1T_ps, b + 1)
                    if b >= 4:
                        act.wait_ge(y4_ps, b - 3)
                    A(a1T[:, b % 4], heads(PB[b % 2][:, 0:QC * S]), ACT.Copy).then_inc(a1T_ready, 1)
                if b >= 2:
                    norm_scale(4, b - 2)
            evac = cm_copy(x4T_ps, PB[6:8], x4T, x4T_ready)
            for b in range(B):
                evac(b)
            for b in range(B):
                act.wait_ge(g4_ps, b + 1)
                f = FC - 1
                A(gT[:, b, 0:f], PB[b % 2][:, 0:f * S].rearrange("p (f s) -> p f s", s=S), ACT.Gelu_apprx_tanh)
                A(gT[0:FROWS[f], b, f], PB[b % 2][0:FROWS[f], f * S:(f + 1) * S], ACT.Gelu_apprx_tanh).then_inc(gelu_ready, 1)
            nc.scalar.preload_act_table_set("natural_log_exp_and_others")

            def pad_evac(b):
                act.wait_ge(x5T_ps, b + 1)
                A(pad[:, :, b, 1:S + 1], PB[4 + b % 2][:, 0:KC * S].rearrange("p (k s) -> p k s", s=S), ACT.Copy).then_inc(pad_ready, 1)

            norms_then(5, pad_evac)
            n = 0
            for h in range(2):
                for a in (0, 1):
                    for k in range(KC):
                        if n == 0:
                            act.wait_ge(pad_ready, B)
                        if n >= 2:
                            act.wait_ge(mix_ready, n - 1)
                        A(mixt[:, n % 2].rearrange("p (b s) -> p b s", s=S), pad[:, k, h * HB:(h + 1) * HB, 1:S + 1],
                          ACT.Copy, scale=mu[:, a, k:k + 1]).then_inc(mixt_ready, 1)
                        n += 1
            for b in range(B):
                act.wait_ge(r_ps, b + 1)
                A(rg[0:S, b], PB[b % 2][0:S, 0:D], ACT.Sigmoid).then_inc(rg_ready, 1)
            for n in range(4):
                act.wait_ge(kk_ps, n + 1)
                if n >= 2:
                    act.wait_ge(ksq_ready, n - 1)
                A(kpos[:, n % 2], PB[6 + n % 2][:, 0:HN], ACT.Relu).then_inc(kpos_ready, 1)
            nc.scalar.preload_act_table_set("natural_log_exp_and_others")
            for b in range(B):
                norm_scale(6, b)

        @block.vector
        def _(dve):
            V = nc.vector

            def norm_stats(k, b):
                V.bn_stats(stats[0:S, b], (X if k == 0 else RES)[0:S, b]).then_inc(ln_st, 1)
                dve.wait_ge(ln_st, k * B + b + 1)
                V.bn_aggr(mv[0:S, b], stats[0:S, b]).then_inc(ln_mv, 1)

            def normalize(k, b, dst):
                dve.wait_ge(ln_rs, k * B + b + 1)
                V.tensor_scalar(dst[0:S, b], (X if k == 0 else RES)[0:S, b], mv[0:S, b, 0:1], rstd[0:S, b:b + 1],
                                ALU.subtract, ALU.mult).then_inc(ln_out, 1)

            def add_and_norm(k, dst, add, lower=None):
                for b in range(B + (4 if lower else 2)):
                    if b < B:
                        add(b)
                        dve.wait_ge(summed, (k - 1) * B + b + 1)
                        norm_stats(k, b)
                    if 2 <= b < B + 2:
                        normalize(k, b - 2, dst)
                    if lower and b >= 4:
                        lower(b - 4)

            def h_of(b):
                dve.wait_ge(hT_ps, b + 1)
                if b >= 4:
                    dve.wait_ge(hT_ready, b - 3)
                for k in range(KC):
                    last = V.tensor_scalar(hst[:, b % 4, k, :], HB4[b % 4][:, k * S:(k + 1) * S],
                                           colb[:, k:k + 1], colb[:, 2 + k:3 + k], ALU.mult, ALU.add)
                last.then_inc(h_ready[0], 1)

            for b in range(B + 3):
                if b % HB == 0 and b < B:
                    dve.wait_ge(ld_x[b // HB], 16)
                if b < B:
                    norm_stats(0, b)
                if 2 <= b < B + 2:
                    normalize(0, b - 2, XN)
                if b == 4:
                    dve.wait_ge(ld_a, LD_A)
                if b >= 4 and b % 2 == 0:
                    h_of(b - 4)

            def lo_of(dst, raw, cols=slice(None)):
                V.tensor_tensor(dst[1][:, :, cols], raw[:, :, cols], dst[0][:, :, cols].bitcast(F32), ALU.subtract).then_inc(split_dve, 1)

            dve.wait_ge(split_hi, 1)
            lo_of(qkvT, raw_qkv, slice(0, 2 * D))
            dve.wait_ge(split_hi, 2)
            lo_of(qkvT, raw_qkv, slice(2 * D, 3 * D))

            exchange = [p // D0 * D0 + (p + D0 // 2) % D0 for p in range(32)]

            def rotate(n, first, ps_ready, banks, col, done, summed_up):
                m = n % 2
                cols = [colb[:, col + 2 * sw + m:col + 2 * sw + m + 1] for sw in range(2)]

                def seqs(ap):
                    return ap.rearrange("p (b s) -> p b s", s=S)

                def turned(sw, src):
                    V.scalar_tensor_tensor(out=seqs(rot[:, n % 2, sw]), in0=seqs(src), scalar=cols[sw],
                                           in1=rope[:, sw:sw + 1].broadcast_to([P, HB, S]),
                                           op0=ALU.add, op1=ALU.mult).then_inc(done, 1)

                dve.wait_ge(ps_ready, n + 1)
                if n >= 2:
                    dve.wait_ge(done, 2 * (n - 1))
                V.stream_shuffle(swap[:, n % 2], banks[n % 2][:, 0:HN], exchange).then_inc(swapped, 1)
                if n >= 2:
                    dve.wait_ge(summed_up, n - 1)
                turned(0, banks[n % 2][:, 0:HN])
                dve.wait_ge(swapped, first + n + 1)
                turned(1, swap[:, n % 2])

            dve.wait_ge(ones_set, 2)

            def context_value(b):
                dve.wait_ge(v_ps, b + 1)
                V.tensor_tensor(vaug[0:S, b, :, 0:D0], PB[4 + b % 2][0:S, 0:D].rearrange("p (h d) -> p h d", d=D0),
                                xv_b[0:S].rearrange("p (h d) -> p h d", d=D0), ALU.add).then_inc(v_ready, 1)

            for b in range(B):
                dve.wait_ge(qk_ps, b + 1)
                V.tensor_tensor(qk[0:S, b], PB[2 + b % 2][0:S, :], qk_b[0:S], ALU.add).then_inc(qk_ready, 1)

            def weights_lo(slot):
                V.tensor_tensor(gu[slot][1][:], w_gu[slot][:], gu[slot][0][:].bitcast(F32), ALU.subtract)
                V.tensor_tensor(dn[slot][1][:], w_dn[slot][:], dn[slot][0][:].bitcast(F32), ALU.subtract).then_inc(w_lo_ready, 1)

            dve.wait_ge(split_hi, 6)
            lo_of(xqT, raw_xq)
            V.tensor_copy(gateT[0][:], raw_gate[:]).then_inc(split_dve, 1)
            dve.wait_ge(split_dve, 4)
            lo_of(gateT, raw_gate)

            def max0_of(b):
                dve.wait_ge(s0_ps, b + 1)
                V.tensor_reduce(max0[:, b], PB[6 + b % 2][:].rearrange("p (q k) -> p q k", k=D), X_AXIS, ALU.max,
                                negate=True).then_inc(s0_max, 1)
                dve.wait_ge(s0_max, b + 1)
                V.tensor_scalar_mul(nb0[:, b], max0[:, b], SCALE0).then_inc(s0_nb, 1)

            def e_evac(b):
                dve.wait_ge(s0_exp, b + 1)
                V.reciprocal(rs0[:, b], sum0[:, b]).then_inc(s0_rs, 1)
                dve.wait_ge(eT0_ps, b + 1)
                if b >= 4:
                    dve.wait_ge(aT_ps, b - 3)
                V.tensor_copy(eT0[:, b % 4], PB[b % 2][:].rearrange("p (k q) -> p k q", q=D)).then_inc(eT0_ready, 1)

            for b in range(B + 5):
                if b < B:
                    max0_of(b)
                if 2 <= b < B + 2:
                    e_evac(b - 2)
                if 1 <= b < 5:
                    rotate(b - 1, 0, kp_ps, PB[4:6], 10, k_rot, kr_ready)
                if b >= 5:
                    context_value(b - 5)

            def add1(b):
                dve.wait_ge(y1_ps, b + 1)
                dve.wait_ge(resid, b + 1)
                V.tensor_tensor(RES[0:S, b], PB[4 + b % 2][0:S, 0:D], RES[0:S, b], ALU.add).then_inc(summed, 1)

            def lower_part(dst, banks, hi_ready, done):
                def lower(b):
                    dve.wait_ge(hi_ready, b + 1)
                    V.tensor_tensor(dst[1][:, :, tok(b)], banks[b % len(banks)][:, 0:KC * S].rearrange("p (k s) -> p k s", s=S),
                                    dst[0][:, :, tok(b)].bitcast(F32), ALU.subtract).then_inc(done, 1)
                return lower

            add_and_norm(1, XN, add1, lower_part(T1, PB[0:2], x1T_hi, x1T_ready))
            for n in range(4):
                if n < 2:
                    dve.wait_ge(kr_ready, 3 + n)
                rotate(n, 4, qp_ps, PB[2:4], 6, q_rot, qr_ready)

            def softmax_in(u, ps_ready, banks, mx, e, used, maxed, done):
                dve.wait_ge(ps_ready, u + 1)
                if u >= 4:
                    dve.wait_ge(used, u - 3)
                sc = heads(banks[u % len(banks)][0:S, 0:QH * S])
                m = mx[0:S, QH * u:QH * (u + 1)]
                V.tensor_reduce(m, sc, X_AXIS, ALU.max).then_inc(maxed, 1)
                dve.wait_ge(maxed, u + 1)
                V.tensor_tensor(e[0:S, u % 4], sc, m.unsqueeze(2).broadcast_to([S, QH, S]), ALU.subtract).then_inc(done, 1)

            def softmax_out(n, ps, rs, dst, dim, ps_ready, inverted, done):
                dve.wait_ge(ps_ready, n + 1)
                V.reciprocal(rs.unsqueeze(2), ps[:, :, dim:dim + 1]).then_inc(inverted, 1)
                dve.wait_ge(inverted, n + 1)
                V.tensor_tensor(dst, ps[:, :, 0:dim],
                                rs.unsqueeze(2).broadcast_to([S, ps.shape[1], dim]), ALU.mult).then_inc(done, 1)


            def out1(b):
                ps = PB[b % 2][0:S, 0:H0 * (D0 + 1)].rearrange("p (h d) -> p h d", d=D0 + 1)
                softmax_out(b, ps, rs1[0:S, b], ctxn[0:S, b].rearrange("p (h d) -> p h d", d=D0), D0, c1_ps, c1_rs, c1_ready)

            def add2(b):
                dve.wait_ge(y2_ps, b + 1)
                dve.wait_ge(resid, B + b + 1)
                V.tensor_tensor(RES[0:S, b], PB[3][0:S, 0:D], RES[0:S, b], ALU.add).then_inc(summed, 1)
                dve.wait_ge(summed, B + b + 1)
                norm_stats(2, b)

            x2_lower = lower_part(T0, [PB[3]], x2T_hi, x2T_ready)
            for u in range(QH * (B - 1) + X2T_LO + 1):
                if u in (UN // 2 + 1, UN // 2 + 5):
                    s = (u - UN // 2) // 4
                    dve.wait_ge(w_hi_ready, s + 1)
                    weights_lo(s)
                if u < UN:
                    softmax_in(u, s1_ps, SB1, max1, e1, eT1_ps, s1_max, s1_sub)
                for first, step in ((OUT, out1), (PROJECT, add2), (NORMED, lambda b: normalize(2, b, X)), (X2T_LO, x2_lower)):
                    b = turn_of(u, first)
                    if b is not None:
                        step(b)
            V.sem_inc(hu_ready, 2)
            V.sem_inc(hlo_ready, 2)
            logits = PB[2][0:S, 0:B * NG].rearrange("p (b e) -> p b e", e=NG)
            ge, sc8 = gexp[0:S, :, 0:E], score[0:S, :, 0:E]
            dve.wait_ge(g_ps, B)
            V.reduce_max(gmax[0:S], logits[:, :, 0:E], X_AXIS).then_inc(g_step, 1)
            dve.wait_ge(g_step, 1)
            V.tensor_tensor(ge, logits[:, :, 0:E], gmax[0:S].unsqueeze(2).broadcast_to([S, B, E]), ALU.subtract).then_inc(g_step, 1)
            dve.wait_ge(g_exp, 2)
            V.reduce_sum(gsum[0:S], ge, X_AXIS).then_inc(g_step, 1)
            V.tensor_scalar_add(sig1[0:S].unsqueeze(2), gexp[0:S, :, E:E + 1], 1.0).then_inc(g_step, 1)
            dve.wait_ge(g_step, 4)
            V.reciprocal(grs[0:S], gsum[0:S]).then_inc(g_step, 1)
            V.reciprocal(wtm[0:S, :, E:E + 1], sig1[0:S].unsqueeze(2)).then_inc(g_step, 1)
            dve.wait_ge(g_step, 6)
            V.tensor_tensor(sc8, ge, grs[0:S].unsqueeze(2).broadcast_to([S, B, E]), ALU.mult).then_inc(g_step, 1)
            dve.wait_ge(g_step, 7)
            dve.wait_ge(sent_set, 1)
            for b in range(B):
                last = V.max(out=top[0:S, b], in_=score[0:S, b])
            last.then_inc(g_step, 1)
            dve.wait_ge(g_step, 8)
            V.memset(top[0:S, :, TOPK:8], -1.0).then_inc(g_step, 1)
            dve.wait_ge(g_step, 9)
            for b in range(B):
                last = V.match_replace(picked[0:S, b], top[0:S, b], score[0:S, b], -2.0)
            last.then_inc(g_step, 1)
            dve.wait_ge(g_step, 10)
            V.scalar_tensor_tensor(out=wtm[0:S, :, 0:E], in0=picked[0:S, :, 0:E], scalar=-1.5, in1=sc8,
                                   op0=ALU.is_lt, op1=ALU.mult).then_inc(wtm_ready, 1)

            def multiply(j, n):
                dve.wait_ge(silu_ready, n + 1)
                V.tensor_tensor(hu[:, j % 2], sg[:, j % 2], PB[5 + 2 * (j % 2)][:, 0:HN], ALU.mult).then_inc(hu_ready, 1)

            def weigh(j, n):
                dve.wait_ge(hu_ready, n + 1 + 2)
                dve.wait_ge(hlo_ready, n + 1)
                V.tensor_tensor(hw[:, j % 2], hu[:, j % 2], wrow[:, j // 2 % 2, half(j % 2)], ALU.mult).then_inc(hw_ready, 1)

            def hidden_lo(j, n):
                dve.wait_ge(hhi_ready, n + 1)
                V.tensor_tensor(hid[j % 4][1][:], hw[:, j % 2], hid[j % 4][0][:].bitcast(F32), ALU.subtract).then_inc(hlo_ready, 1)


            def turn(i, last_turn):
                for j in range(WT):
                    multiply(j, i * WT + j)
                    if j % 2 == 0:
                        dve.wait_ge(wrow_ready, i * TURN + (j // 2 + 1))
                    weigh(j, i * WT + j)
                    hidden_lo(j, i * WT + j)
                    if j % 2 == 0 and not (last_turn and j // 2 + 2 >= TURN):
                        dve.wait_ge(w_hi_ready, i * TURN + (j // 2 + 3))
                        weights_lo((j // 2 + 2) % TURN)

            with dve.Fori(0, NC // TURN - 1) as i:
                turn(i, False)
            turn(NC // TURN - 1, True)

            def add3(b):
                dve.wait_ge(y3_ps, b + 1)
                V.tensor_tensor(RES[0:S, b], PB[4 + b % 2][0:S, 0:D], X[0:S, b], ALU.add).then_inc(summed, 1)

            add_and_norm(3, XN, add3, lower_part(T1, PB[6:8], x3T_hi, x3T_ready))
            for h in range(2):
                dve.wait_ge(lat_hi, h + 1)
                V.tensor_tensor(latT[1][:, half(h)], PB[2 + h][:, 0:HN], latT[0][:, half(h)].bitcast(F32), ALU.subtract).then_inc(lat_ready, 1)
            dve.wait_ge(one1_set, 1)
            for b in range(B):
                dve.wait_ge(v1_ps, b + 1)
                V.tensor_copy(v1[0:S, b, :, 0:D1], PB[6 + b % 2][0:S].rearrange("p (h d) -> p h d", d=D1)).then_inc(v1_ready, 1)

            def out2(u):
                ps = PB[2 + u % 2][0:S, 0:QH * (D1 + 1)].rearrange("p (h d) -> p h d", d=D1 + 1)
                dst = a1[u % 2][0:S, u // 2].rearrange("p (h d) -> p h d", d=D1)
                softmax_out(u, ps, rs2[0:S, QH * u:QH * (u + 1)], dst, D1, c2_ps, c2_rs, c2_ready)

            for u in range(U2 + 6):
                if u < U2:
                    softmax_in(u, s2_ps, SB2, max2, e2, eT2_ps, s2_max, s2_sub)
                if u >= 6:
                    out2(u - 6)

            def add4(b):
                dve.wait_ge(y4_ps, b + 1)
                V.tensor_tensor(RES[0:S, b], PB[4 + b % 2][0:S, 0:D], XN[0:S, b], ALU.add).then_inc(summed, 1)

            add_and_norm(4, X, add4)

            def add5(b):
                dve.wait_ge(y5_ps, b + 1)
                V.tensor_tensor(RES[0:S, b], PB[2 + b % 2][0:S, 0:D], X[0:S, b], ALU.add).then_inc(summed, 1)

            add_and_norm(5, XN, add5)
            dve.wait_ge(omm_ready, 1)
            dve.wait_ge(pad_zero, 1)
            n = 0
            for h in range(2):
                for a in (0, 1):
                    for k in range(KC):
                        dve.wait_ge(mixt_ready, n + 1)
                        V.scalar_tensor_tensor(out=mix[:, a, k, half(h)].rearrange("p (b s) -> p b s", s=S),
                                               in0=pad[:, k, h * HB:(h + 1) * HB, 0:S], scalar=omm[:, a, k:k + 1],
                                               in1=mixt[:, n % 2].rearrange("p (b s) -> p b s", s=S),
                                               op0=ALU.mult, op1=ALU.add).then_inc(mix_ready, 1)
                        n += 1
            dve.wait_ge(rg_ready, B)
            for b in range(B + 2):
                if b < B:
                    dve.wait_ge(y6_ps, b + 1)
                    V.tensor_tensor(RES[0:S, b], PB[2 + b % 2][0:S, 0:D], rg[0:S, b], ALU.mult).then_inc(gated, 1)
                    dve.wait_ge(gated, b + 1)
                    V.tensor_tensor(RES[0:S, b], RES[0:S, b], XN[0:S, b], ALU.add).then_inc(summed, 1)
                    dve.wait_ge(summed, 5 * B + b + 1)
                    norm_stats(6, b)
                if b >= 2:
                    normalize(6, b - 2, X)


def _constants():
    half = D0 // 2
    pos = np.arange(S, dtype=np.float32)
    freqs = (np.float32(1.0) / np.float32(10000.0) ** (np.arange(half, dtype=np.float32) / np.float32(half))).astype(np.float32)
    ang = pos[:, None] * freqs[None, :]
    cos, sin = np.cos(ang).astype(np.float32), np.sin(ang).astype(np.float32)
    cc = np.concatenate([cos, cos], 1).T
    ss = np.concatenate([-sin, sin], 1).T
    rope = np.stack([np.tile(cc, (HC, 1)), np.tile(ss, (HC, 1))], 1)
    bf16 = mybir.dt.np(BF16)
    q, k = np.arange(S)[:, None], np.arange(S)[None, :]
    masked = (k > q) | (k < q - WINDOW)
    mask = np.tile(np.where(masked, np.float32(MASKED), np.float32(0)), (1, QH))
    return {
        "ident": np.eye(P, dtype=np.float32), "identb": np.eye(P).astype(bf16), "maskb": mask.astype(bf16),
        "rope": np.ascontiguousarray(rope, np.float32),
        "hmask": (np.arange(P)[:, None] // D0 == np.arange(HC)[None, :]).astype(np.float32),
    }


def _laid_out(a):
    def swapped(w):
        return w.reshape(H0, 2, D0 // 2, *w.shape[1:])[:, ::-1].reshape(w.shape)

    def cols(v):
        return v.reshape(KC, P).T

    ctx = a["ctx_1024"]
    gu, dn = a["L0_ffn_experts_gate_up"], a["L0_ffn_experts_down"]
    sg, su, sd = a["L0_ffn_shared_gate_w"], a["L0_ffn_shared_up_w"], a["L0_ffn_shared_down_w"]

    def hidden(experts, shared):
        rows = np.concatenate([experts.reshape(-1, D), shared], 0)
        return np.concatenate([rows, np.zeros((NC * P - HID, D), rows.dtype)], 0).reshape(NC, P, D)

    qb, kb = a["L0_xattn_q_b"], a["L0_xattn_k_b"]
    qw, kw = a["L0_xattn_q_w"], a["L0_xattn_k_w"]
    out = {
        "x": a["x"],
        "cA": ctx[:, :S].transpose(2, 0, 1).reshape(D, N),
        "cT": ctx.transpose(2, 0, 1), "cN": ctx,
        "qkvT": a["L0_attn_qkv_w"].T, "qk_b": a["L0_attn_qkv_b"][:2 * D],
        "projT": a["L0_attn_proj_w"].T, "proj_b": a["L0_attn_proj_b"],
        "xqT": qw.T, "xkT": kw.T,
        "xvT": a["L0_xattn_v_w"].T, "xv_b": a["L0_xattn_v_b"],
        "xoT": a["L0_xattn_o_w"].T, "xo_b": a["L0_xattn_o_b"],
        "colb": np.concatenate([cols(v) for v in (
            a["L0_attn_norm_w"], a["L0_attn_norm_b"], a["L0_attn_qkv_b"][2 * D:],
            qb, swapped(qb), kb, swapped(kb))], 1),
        "gateT": np.concatenate([a["L0_ffn_gate_w"], a["L0_ffn_shared_expert_gate_w"], np.zeros((1, D), np.float32)], 0).T,
        "guT": np.concatenate([hidden(gu[:, :I], sg), hidden(gu[:, I:], su)], 1).transpose(0, 2, 1),
        "dnT": hidden(dn.transpose(0, 2, 1), sd.T),
        "wqT": a["L1_attn_Wq"].T, "wkdT": a["L1_attn_Wkv_down"].T, "wkuT": a["L1_attn_Wk_up"].T,
        "wvuT": a["L1_attn_Wv_up"].T,
        "woT": a["L1_attn_Wo"].T.reshape(H1 // 2, 2, D1, D).transpose(1, 0, 2, 3).reshape(H1 * D1, D),
        "wrT": a["L1_ffn_W_r"].T, "wkT": a["L1_ffn_W_k"].T, "wvT": a["L1_ffn_W_v"].T,
        "mu": np.concatenate([cols(a["L1_ffn_mu_r"]), cols(a["L1_ffn_mu_k"])], 1),
    }
    return {**out, **_constants()}


def kernel(**inputs):
    import concourse.bacc as bacc
    from concourse.bass_utils import run_bass_kernel_spmd

    nc = bacc.Bacc("TRN2", target_bir_lowering=False, num_devices=1)
    arrays, aps = {}, {}
    for name, a in _laid_out({k: np.asarray(v) for k, v in inputs.items()}).items():
        a = np.ascontiguousarray(a)
        arrays[f"in_{name}"] = a
        aps[name] = nc.dram_tensor(f"in_{name}", a.shape, mybir.dt.from_np(a.dtype), kind="ExternalInput").ap()
    out = nc.dram_tensor("out_x", (B, S, D), F32, kind="ExternalOutput").ap()
    build(nc, aps, out)
    r = run_bass_kernel_spmd(nc, [arrays], core_ids=[0])
    return r.results[0]["out_x"]
```

```python
from contextlib import ExitStack

import numpy as np

import concourse.bass as bass
from concourse import mybir

F32, F32R, BF16 = mybir.dt.float32, mybir.dt.float32r, mybir.dt.bfloat16
ACT = mybir.ActivationFunctionType
ALU = mybir.AluOpType
X_AXIS = mybir.AxisListType.X

B, S, D = 8, 100, 256
SK = 361
P = 128
KC = D // P
N = B * S
HB = B // 2
HN = HB * S
H0, D0, WINDOW = 16, 16, 64
HC = P // D0
QH = 4
E, I, TOPK = 8, 352, 2
SI = 704
HID = E * I + SI
NC = -(-HID // P)
NU = 2 * NC
TURN = 4
WT = 2 * TURN
NW = E + 1
H1, D1, R1 = 8, 64, 64
QC = H1 * D1 // P
FC = -(-SK // P)
FROWS = [min(P, SK - f * P) for f in range(FC)]
EPS = 1e-5
NG = E + 2
MASKED = -3e38
SCALE0 = float(np.float32(1.0 / np.sqrt(S)))


def build(nc, I_, out):
    ctx = ExitStack()
    with ctx:
        def sb(name, shape, dt=F32, where=ctx):
            return where.enter_context(nc.sbuf_tensor(name, shape, dt))

        def sem(name):
            return ctx.enter_context(nc.semaphore(name))

        X = sb("X", [P, B, D])
        XN = sb("XN", [P, B, D])
        RES = sb("RES", [P, B, D])
        with ExitStack() as r:
            x4T = sb("x4T", [P, KC, N], F32, r)
        T0 = [sb("T0_hi", [P, KC, N], F32R)]
        with ExitStack() as r:
            cmst = sb("cmst", [P, 4, KC, S], F32, r)
        T0.append(sb("T0_lo", [P, KC, N], F32R))
        T1 = [sb(f"T1_{p}", [P, KC, N], F32R) for p in ("hi", "lo")]
        ident = sb("ident", [P, P])
        stats = sb("stats", [P, B, 6])
        mv = sb("mv", [P, B, 2])
        lnv = sb("lnv", [P, B])
        rstd = sb("rstd", [P, B])
        epsb = sb("epsb", [P, 1])
        zero16 = sb("zero16", [P, HN], BF16)

        work = ExitStack()
        w_gu = [sb(f"w_gu{s}", [P, KC, 2 * P], F32, work) for s in range(TURN)]
        w_dn = [sb(f"w_dn{s}", [P, D], F32, work) for s in range(TURN)]
        gu = [[sb(f"gu_{p}{s}", [P, KC, 2 * P], F32R, work) for p in ("hi", "lo")] for s in range(TURN)]
        dn = [[sb(f"dn_{p}{s}", [P, D], F32R, work) for p in ("hi", "lo")] for s in range(TURN)]

        with ExitStack() as r:
            qk = sb("qk", [P, B, 2 * D], F32, r)
            vT = sb("vT", [P, KC, N], F32, r)
            e0 = sb("e0", [P, 4, KC, D], F32, r)
            eT0 = sb("eT0", [P, 4, KC, D], F32, r)
            aT = sb("aT", [P, B, KC, S], F32, r)
        with ExitStack() as r:
            kblk = sb("kblk", [P, 4, HC, S], F32, r)
            e1 = sb("e1", [P, 4, QH, S], F32, r)
            eT1 = sb("eT1", [P, 4, QH, S], F32, r)
            ctxn = sb("ctxn", [P, B, D], F32, r)
            ctxnT = sb("ctxnT", [P, KC, N], F32, r)
        with ExitStack() as r:
            wb = sb("wb", [P, NW, N], F32, r)
            wrow = sb("wrow", [P, 2, N], F32, r)
        with ExitStack() as r:
            sb("until_e0", [P, B * 2 * D + KC * N], F32, r)
            raw_cA = sb("raw_cA", [P, KC, N], F32, r)
            raw_qkv = sb("raw_qkv", [P, KC, 3 * D], F32, r)
            raw_xk = sb("raw_xk", [P, KC, D], F32, r)
            raw_xv = sb("raw_xv", [P, KC, D], F32, r)
            raw_xq = sb("raw_xq", [P, KC, D], F32, r)
            hst = sb("hst", [P, 4, KC, S], F32, r)
        sb("place1", [P, B * 2 * D + 2 * KC * N + 8 * KC * D], F32, work)

        with ExitStack() as r:
            kr = sb("kr", [P, KC, N], F32, r)
            swap = sb("swap", [P, 2, HN], F32, r)
            rot = sb("rot", [P, 2, 2, HN], F32, r)
            with ExitStack() as early:
                cA = [sb(f"cA_{p}", [P, KC, N], F32R, early) for p in ("hi", "lo")]
            with ExitStack() as late:
                qr = sb("qr", [P, KC, N], F32, late)
            sb("context_place", [P, 2 * KC * N], F32, r)
            vaug = sb("vaug", [P, B, H0, D0 + 1], F32, r)
            qkvT = [sb(f"qkvT_{p}", [P, KC, 3 * D], F32R, r) for p in ("hi", "lo")]
            projT = sb("projT", [P, KC, D], F32, r)
            xqT = [sb(f"xqT_{p}", [P, KC, D], F32R, r) for p in ("hi", "lo")]
            xkT = [sb(f"xkT_{p}", [P, KC, D], F32R, r) for p in ("hi", "lo")]
            xvT = [sb(f"xvT_{p}", [P, KC, D], F32R, r) for p in ("hi", "lo")]
            xoT = sb("xoT", [P, KC, D], F32, r)
            qk_b = sb("qk_b", [P, 2 * D], F32, r)
            proj_b = sb("proj_b", [P, D], F32, r)
            xv_b = sb("xv_b", [P, D], F32, r)
            xo_b = sb("xo_b", [P, D], F32, r)
            colb = sb("colb", [P, 14], F32, r)
            rope = sb("rope", [P, 2, S], F32, r)
            hmask = sb("hmask", [P, HC], F32, r)
            identb = sb("identb", [P, P], BF16, r)
            maskb = sb("maskb", [P, QH * S], BF16, r)
            raw_gate = sb("raw_gate", [P, KC, NG], F32, r)
            gateT = [sb(f"gateT_{p}", [P, KC, NG], F32R, r) for p in ("hi", "lo")]
            max0 = sb("max0", [P, B, KC], F32, r)
            nb0 = sb("nb0", [P, B, KC], F32, r)
            sum0 = sb("sum0", [P, B, KC], F32, r)
            rs0 = sb("rs0", [P, B, KC], F32, r)
            max1 = sb("max1", [P, B * H0], F32, r)
            rs1 = sb("rs1", [P, B, H0], F32, r)
            gmax = sb("gmax", [P, B], F32, r)
            gexp = sb("gexp", [P, B, E + 1], F32, r)
            gsum = sb("gsum", [P, B], F32, r)
            grs = sb("grs", [P, B], F32, r)
            score = sb("score", [P, B, 2 * E], F32, r)
            top = sb("top", [P, B, 8], F32, r)
            picked = sb("picked", [P, B, 2 * E], F32, r)
            wtm = sb("wtm", [P, B, NW], F32, r)
            sig1 = sb("sig1", [P, B], F32, r)
        with ExitStack() as r:
            sg = sb("sg", [P, 2, HN], F32, r)
            hu = sb("hu", [P, 2, HN], F32, r)
            hw = sb("hw", [P, 2, HN], F32, r)
            hid = [[sb(f"hid_{p}{s}", [P, HN], F32R, r) for p in ("hi", "lo")] for s in range(4)]
        sb("rings", [P, 14 * HN], F32, work)
        with ExitStack() as r:
            wqT = [sb(f"wqT_{p}", [P, KC, H1 * D1], F32R, r) for p in ("hi", "lo")]
            wkdT = [sb(f"wkdT_{p}", [P, KC, 2 * R1], F32R, r) for p in ("hi", "lo")]
            wkuT = sb("wkuT", [2 * R1, H1 * D1], F32R, r)
            wvuT = sb("wvuT", [2 * R1, H1 * D1], F32R, r)
            raw_wq = sb("raw_wq", [P, KC, H1 * D1], F32, r)
            raw_wkd = sb("raw_wkd", [P, KC, 2 * R1], F32, r)
            raw_wku = sb("raw_wku", [2 * R1, H1 * D1], F32, r)
            raw_wvu = sb("raw_wvu", [2 * R1, H1 * D1], F32, r)
            woT = sb("woT", [P, QC, D], F32, r)
            wrT = sb("wrT", [P, KC, D], F32, r)
            wkT = sb("wkT", [P, KC, D], F32, r)
            wvT = sb("wvT", [P, KC, D], F32, r)
            mu = sb("mu", [P, 2, KC], F32, r)
            omm = sb("omm", [P, 2, KC], F32, r)
            max2 = sb("max2", [P, B * H1], F32, r)
            rs2 = sb("rs2", [P, B * H1], F32, r)
        work.close()

        with ExitStack() as r:
            q1T = sb("q1T", [P, QC, N], F32, r)
            k1T = sb("k1T", [P, QC, N], F32, r)
            latT = [sb(f"latT_{p}", [2 * R1, N], F32R, r) for p in ("hi", "lo")]
            e2 = sb("e2", [P, 4, QH, S], F32, r)
            eT2 = sb("eT2", [P, 4, QH, S], F32, r)
            v1 = sb("v1", [P, B, H1, D1 + 1], F32, r)
            a1T = sb("a1T", [P, 4, QC, S], F32, r)
            cT = sb("cT", [P, KC, B, SK], F32, r)
        with ExitStack() as r:
            fT = sb("fT", [P, KC, N], F32, r)
        with ExitStack() as r:
            cN = sb("cN", [P, B, FC, D], F32, r)
            gT = sb("gT", [P, B, FC, S], F32, r)
            pad = sb("pad", [P, KC, B, S + 1], F32, r)
            mix = sb("mix", [P, 2, KC, N], F32, r)
            mixt = sb("mixt", [P, 4, HN], F32, r)
            kpos = sb("kpos", [P, 2, HN], F32, r)
            ksq = sb("ksq", [P, KC, N], F32, r)
            rg = sb("rg", [P, B, D], F32, r)

        a1 = [X, RES]

        PB = [ctx.enter_context(nc.psum_tensor(f"PB{i}", [P, 512], F32)) for i in range(8)]

        ld_a, ld_k, ld_q, ld_v, ld_b, ld_c, ld_ct = [
            sem("ld_" + n) for n in ("a", "k", "q", "v", "b", "c", "ct")]
        ld_x = [sem(f"ld_x{h}") for h in range(2)]
        ld_w = [sem(f"ld_w{s}") for s in range(TURN)]
        ones_set, zero_set, sent_set = sem("ones_set"), sem("zero_set"), sem("sent_set")
        ln_st, ln_mv, ln_lg, ln_rs, ln_out = [sem("ln_" + n) for n in ("st", "mv", "lg", "rs", "out")]
        twice = sem("twice")
        summed = sem("summed")
        resid = sem("resid")
        split_hi, split_lo, split_dve = sem("split_hi"), sem("split_lo"), sem("split_dve")
        hT_ps, h_hi, hT_ready = sem("hT_ps"), sem("h_hi"), sem("hT_ready")
        h_ready = [sem("h_even"), sem("h_odd")]
        qk_ps, qk_ready = sem("qk_ps"), sem("qk_ready")
        vT_ps, vT_ready = sem("vT_ps"), sem("vT_ready")
        kp_ps, k_rot, kr_ready = sem("kp_ps"), sem("k_rot"), sem("kr_ready")
        v_ps, v_ready = sem("v_ps"), sem("v_ready")
        s0_ps, s0_max, s0_nb, s0_exp, s0_rs = [sem("s0_" + n) for n in ("ps", "max", "nb", "exp", "rs")]
        eT0_ps, eT0_ready = sem("eT0_ps"), sem("eT0_ready")
        aT_ps, aT_ready = sem("aT_ps"), sem("aT_ready")
        y1_ps = sem("y1_ps")
        x1T_ps, x1T_hi, x1T_ready = sem("x1T_ps"), sem("x1T_hi"), sem("x1T_ready")
        swapped = sem("swapped")
        qp_ps, q_rot, qr_ready = sem("qp_ps"), sem("q_rot"), sem("qr_ready")
        kblk_ready = sem("kblk_ready")
        s1_ps, s1_max, s1_sub, s1_exp = [sem("s1_" + n) for n in ("ps", "max", "sub", "exp")]
        eT1_ps, eT1_ready = sem("eT1_ps"), sem("eT1_ready")
        c1_ps, c1_rs, c1_ready = sem("c1_ps"), sem("c1_rs"), sem("c1_ready")
        cT1_ps, cT1_ready = sem("cT1_ps"), sem("cT1_ready")
        y2_ps = sem("y2_ps")
        x2T_ps, x2T_hi, x2T_ready = sem("x2T_ps"), sem("x2T_hi"), sem("x2T_ready")
        g_ps, g_step, g_exp, wtm_ready = sem("g_ps"), sem("g_step"), sem("g_exp"), sem("wtm_ready")
        wb_ps = sem("wb_ps")
        wb_ready = [sem("wb_even"), sem("wb_odd")]
        w_hi_ready, w_lo_ready = sem("w_hi_ready"), sem("w_lo_ready")
        gu_ps, silu_ready, hu_ready, hw_ready = sem("gu_ps"), sem("silu_ready"), sem("hu_ready"), sem("hw_ready")
        hhi_ready, hlo_ready, down_done = sem("hhi_ready"), sem("hlo_ready"), sem("down_done")
        load_turn, row_copy, wrow_ready = sem("load_turn"), sem("row_copy"), sem("wrow_ready")
        fT_ready = sem("fT_ready")
        y3_ps = sem("y3_ps")
        x3T_ps, x3T_hi, x3T_ready = sem("x3T_ps"), sem("x3T_hi"), sem("x3T_ready")
        lat_ps, lat_hi, lat_ready = sem("lat_ps"), sem("lat_hi"), sem("lat_ready")
        wc_hi, wc_whole, wc_ready = sem("wc_hi"), sem("wc_whole"), sem("wc_ready")
        q1_ps, q1_ready = sem("q1_ps"), sem("q1_ready")
        v1_ps, v1_ready, one1_set = sem("v1_ps"), sem("v1_ready"), sem("one1_set")
        s2_ps, s2_max, s2_sub, s2_exp = [sem("s2_" + n) for n in ("ps", "max", "sub", "exp")]
        eT2_ps, eT2_ready = sem("eT2_ps"), sem("eT2_ready")
        c2_ps, c2_rs, c2_ready = sem("c2_ps"), sem("c2_rs"), sem("c2_ready")
        a1T_ps, a1T_ready = sem("a1T_ps"), sem("a1T_ready")
        y4_ps = sem("y4_ps")
        x4T_ps, x4T_ready = sem("x4T_ps"), sem("x4T_ready")
        g4_ps, gelu_ready = sem("g4_ps"), sem("gelu_ready")
        y5_ps = sem("y5_ps")
        x5T_ps, pad_ready, pad_zero = sem("x5T_ps"), sem("pad_ready"), sem("pad_zero")
        omm_ready, mixt_ready, mix_ready = sem("omm_ready"), sem("mixt_ready"), sem("mix_ready")
        kk_ps, kpos_ready, ksq_ready = sem("kk_ps"), sem("kpos_ready"), sem("ksq_ready")
        gated, summed_last = sem("gated"), sem("summed_last")
        r_ps, rg_ready, y6_ps = sem("r_ps"), sem("rg_ready"), sem("y6_ps")
        stored = sem("stored")

        def tok(b):
            return slice(b * S, (b + 1) * S)

        def half(h):
            return slice(h * HN, (h + 1) * HN)

        def heads(ap):
            return ap.rearrange("p (j s) -> p j s", s=S)

        def tripled(a, b, at, bt):
            return [(a[p][at], b[q][bt]) for p, q in ((0, 0), (0, 1), (1, 0))]

        def chunks(a, cols_a, b, cols_b):
            return [x for k in range(KC) for x in tripled(a, b, (slice(None), k, cols_a), (slice(None), k, cols_b))]

        EVERY = slice(None)

        UN, U2 = B * H0 // QH, B * H1 // QH
        HB4 = [PB[0], PB[1], PB[6], PB[7]]
        RB = [PB[4], PB[5], PB[0], PB[2]]
        SB1 = [PB[4], PB[5], PB[2]]
        SB2 = [PB[4], PB[5], PB[0], PB[1]]

        OUT, CTXT, PROJECT, NORMED, X2T, X2T_LO = 9, 11, 12, 13, 17, 18
        ROUTER = UN + 3

        def turn_of(u, first):
            b = (u - first) // QH
            return b if (u - first) % QH == 0 and 0 <= b < B else None

        def wb_tile(n):
            c, b = n // B, n % B
            k = min(4, NW - 4 * c)
            return wb[:, 4 * c:4 * c + k, tok(b)], heads(PB[n % 4][:, 0:k * S])

        block = ctx.enter_context(nc.Block())

        @block.sync
        def _(sp):
            def rows(name):
                return I_[name].rearrange("(k p) n -> p k n", p=P)

            def all_rows(name, width):
                return I_[name].rearrange("(o n) -> o n", o=1).broadcast_to([S, width])

            for h in range(2):
                sp.dma_start(X[0:S, h * HB:(h + 1) * HB], I_["x"][h * HB:(h + 1) * HB].rearrange("b s d -> s b d")).then_inc(ld_x[h], 16)
                if h == 0:
                    sp.dma_start(ident[:], I_["ident"]).then_inc(ld_a, 16)
                    sp.dma_start(colb[:], I_["colb"]).then_inc(ld_a, 16)
            sp.dma_start(raw_qkv[:], rows("qkvT")).then_inc(ld_q, 16)
            sp.dma_start(qk_b[0:S], all_rows("qk_b", 2 * D)).then_inc(ld_q, 16)
            sp.dma_start(raw_cA[:], rows("cA")).then_inc(ld_k, 16)
            sp.dma_start(raw_xk[:], rows("xkT")).then_inc(ld_k, 16)
            sp.dma_start(raw_xv[:], rows("xvT")).then_inc(ld_v, 16)
            sp.dma_start(rope[:], I_["rope"]).then_inc(ld_v, 16)
            sp.dma_start(xv_b[0:S], all_rows("xv_b", D)).then_inc(ld_v, 16)
            sp.dma_start(raw_xq[:], rows("xqT")).then_inc(ld_v, 16)
            sp.dma_start(raw_gate[:], rows("gateT")).then_inc(ld_v, 16)
            sp.dma_start(proj_b[0:S], all_rows("proj_b", D)).then_inc(ld_b, 16)
            sp.dma_start(projT[:], rows("projT")).then_inc(ld_b, 16)
            sp.dma_start(hmask[:], I_["hmask"]).then_inc(ld_b, 16)
            sp.dma_start(identb[:], I_["identb"]).then_inc(ld_b, 16)
            sp.dma_start(maskb[0:S], I_["maskb"]).then_inc(ld_b, 16)
            sp.dma_start(xoT[:], rows("xoT")).then_inc(ld_b, 16)
            sp.dma_start(xo_b[0:S], all_rows("xo_b", D)).then_inc(ld_b, 16)

            def load_chunk(c, slot):
                gate_up = I_["guT"].rearrange("c (k p) n -> p c k n", p=P)
                sp.dma_start(w_gu[slot][:], gate_up[:, bass.ds(c, 1)].rearrange("p c k n -> p (c k) n")).then_inc(ld_w[slot], 16)
                down = I_["dnT"].rearrange("c p n -> p c n")
                sp.dma_start(w_dn[slot][:], down[:, bass.ds(c, 1)].rearrange("p c n -> p (c n)")).then_inc(ld_w[slot], 16)

            for c in range(TURN):
                load_chunk(c, c)
            for i in range(2):
                sp.wait_ge(wb_ready[i], 3 * B // 2)
            sp.dma_start(raw_wq[:], rows("wqT")).then_inc(ld_c, 16)
            for i in range(2):
                sp.dma_start(raw_wkd[:, :, i * R1:(i + 1) * R1], rows("wkdT")).then_inc(ld_c, 16)
                sp.dma_start(raw_wku[i * R1:(i + 1) * R1], I_["wkuT"]).then_inc(ld_c, 16)
                sp.dma_start(raw_wvu[i * R1:(i + 1) * R1], I_["wvuT"]).then_inc(ld_c, 16)
            sp.dma_start(woT[:], rows("woT")).then_inc(ld_c, 16)
            sp.dma_start(wrT[:], rows("wrT")).then_inc(ld_c, 16)
            sp.dma_start(wkT[:], rows("wkT")).then_inc(ld_c, 16)
            sp.dma_start(wvT[:], rows("wvT")).then_inc(ld_c, 16)
            sp.dma_start(mu[:], I_["mu"].rearrange("p (a k) -> p a k", a=2)).then_inc(ld_c, 16)
            with sp.Fori(1, NC // TURN) as i:
                for s in range(TURN):
                    first = sp.snap(i * TURN + s)
                    sp.wait_ge(w_lo_ready, first - (TURN - 1))
                    sp.sem_inc(load_turn, 1)
                    load_chunk(first, s)
            cf = (FC - 1) * P
            sp.wait_ge(fT_ready, 4)
            sp.dma_start(cT[:], I_["cT"].rearrange("(k p) b n -> p k b n", p=P)).then_inc(ld_ct, 16)
            sp.wait_ge(s2_ps, U2)
            for b in range(B):
                sp.dma_start(cN[:, b, 0:FC - 1], I_["cN"][b, 0:cf].rearrange("(f p) d -> p f d", p=P)).then_inc(ld_ct, 16)
            sp.dma_start(cN[0:SK - cf, :, FC - 1], I_["cN"][:, cf:SK].rearrange("b p d -> p b d")).then_inc(ld_ct, 16)
            for b in range(B):
                sp.wait_ge(ln_out, 6 * B + b + 1)
                sp.dma_start(out[b], X[0:S, b]).then_inc(stored, 16)
            sp.wait_ge(stored, 16 * B)
        LD_A, LD_K, LD_Q, LD_V, LD_B, LD_W, LD_C, LD_CT = [16 * n for n in (2, 2, 2, 5, 7, 2, 12, B + 2)]

        @block.tensor
        def _(pe):
            mm = nc.tensor.matmul

            def to_cm(src, bank, b):
                for k in range(KC):
                    last = nc.tensor.transpose(bank[:, k * S:(k + 1) * S], src[0:S, b, k * P:(k + 1) * P], ident[0:S, 0:S])
                return last

            def product(out_, pairs):
                for n, (a, m) in enumerate(pairs):
                    last = mm(out_, a, m, start=(n == 0), stop=(n == len(pairs) - 1))
                return last

            def behind(sums, transposed):
                for b in range(B + 3):
                    if b < B:
                        sums(b)
                    if b >= 3:
                        transposed(b - 3)

            pe.wait_ge(ld_a, LD_A)
            for b in range(B):
                pe.wait_ge(ln_out, b + 1)
                if b >= 4:
                    pe.wait_ge(hT_ready, b - 3)
                to_cm(XN, HB4[b % 4], b).then_inc(hT_ps, 1)
            pe.wait_ge(split_dve, 1)
            for b in range(B):
                pe.wait_ge(hT_ready, b + 1)
                if b >= 2:
                    pe.wait_ge(qk_ready, b - 1)
                product(PB[2 + b % 2][0:S, :], chunks(T0, tok(b), qkvT, slice(0, 2 * D))).then_inc(qk_ps, 1)
            pe.wait_ge(split_dve, 2)
            for h in range(2):
                for m in range(KC):
                    if h:
                        pe.wait_ge(vT_ready, m + 1)
                    product(PB[4 + m][:, 0:HN], chunks(qkvT, slice(2 * D + m * P, 2 * D + (m + 1) * P), T0, half(h))).then_inc(vT_ps, 1)
            def keys1(n):
                if n < 2:
                    pe.wait_ge(vT_ready, 3 + n)
                else:
                    pe.wait_ge(k_rot, 2 * (n - 1))
                if n == 0:
                    pe.wait_ge(split_lo, 2)
                m = n % 2
                product(PB[4 + n % 2][:, 0:HN], chunks(xkT, slice(m * P, (m + 1) * P), cA, half(n // 2))).then_inc(kp_ps, 1)

            def values_of_context(b):
                if b < 2:
                    pe.wait_ge(k_rot, 6 + 2 * b)
                else:
                    pe.wait_ge(v_ready, b - 1)
                if b == 0:
                    pe.wait_ge(split_lo, 3)
                product(PB[4 + b % 2][0:S, 0:D], chunks(cA, tok(b), xvT, EVERY)).then_inc(v_ps, 1)

            def scores0(b):
                if b >= 2:
                    pe.wait_ge(s0_exp, b - 1)
                pe.wait_ge(qk_ready, b + 1)
                for q in range(KC):
                    last = product(PB[6 + b % 2][:, q * D:(q + 1) * D], [(qk[0:S, b, q * P:(q + 1) * P], qk[0:S, b, D:2 * D])])
                last.then_inc(s0_ps, 1)

            def transposes0(b):
                if b < 2:
                    pe.wait_ge(hT_ready, B)
                else:
                    pe.wait_ge(eT0_ready, b - 1)
                pe.wait_ge(s0_exp, b + 1)
                for k in range(KC):
                    for q in range(KC):
                        last = nc.tensor.transpose(PB[b % 2][:, k * D + q * P:k * D + (q + 1) * P],
                                                   e0[:, b % 4, q, k * P:(k + 1) * P], ident[:])
                last.then_inc(eT0_ps, 1)

            def values0(b):
                if b < 2:
                    pe.wait_ge(qk_ready, B)
                else:
                    pe.wait_ge(aT_ready, b - 1)
                pe.wait_ge(eT0_ready, b + 1)
                pe.wait_ge(vT_ready, 2 * (b // HB) + 2)
                for q in range(KC):
                    last = product(PB[2 + b % 2][:, q * S:(q + 1) * S],
                                   [(eT0[:, b % 4, k, q * P:(q + 1) * P], vT[:, k, tok(b)]) for k in range(KC)])
                last.then_inc(aT_ps, 1)

            for b in range(B + 4):
                if b < B:
                    scores0(b)
                if 2 <= b < B + 2:
                    transposes0(b - 2)
                if b < 4:
                    keys1(b)
                else:
                    values_of_context(b - 4)
                if b >= 4:
                    values0(b - 4)
            pe.wait_ge(ld_b, LD_B)
            def project0(b):
                if b == 0:
                    pe.wait_ge(v_ready, B)
                    pe.wait_ge(s0_exp, B)
                elif b >= 4:
                    pe.wait_ge(ln_out, B + b - 3)
                pe.wait_ge(resid, b + 1)
                pe.wait_ge(aT_ready, b + 1)
                product(PB[4 + b % 4][0:S, 0:D], [(aT[:, b, q, :], projT[:, q, :]) for q in range(KC)]
                        + [(ident[0:S, 0:S], RES[0:S, b])]).then_inc(y1_ps, 1)

            def x1_to_cm(b):
                if b < 2:
                    pe.wait_ge(eT0_ready, B)
                else:
                    pe.wait_ge(x1T_hi, b - 1)
                pe.wait_ge(ln_out, B + b + 1)
                to_cm(XN, PB[b % 2], b).then_inc(x1T_ps, 1)

            behind(project0, x1_to_cm)
            pe.wait_ge(split_dve, 3)
            pe.wait_ge(aT_ready, B)
            for n, (h, m) in enumerate([(h, m) for h in range(2) for m in range(KC)]):
                if n >= 2:
                    pe.wait_ge(q_rot, 2 * (n - 1))
                pe.wait_ge(x1T_ready, HB * (h + 1))
                product(PB[2 + n % 2][:, 0:HN], chunks(xqT, slice(m * P, (m + 1) * P), T1, half(h))).then_inc(qp_ps, 1)

            def scores1(u):
                b, c, j = u // 4, u // 2 % 2, u % 2
                bank = SB1[u % 3][0:S, 0:QH * S]
                if u == 0:
                    pe.wait_ge(ln_out, 2 * B)
                elif u == 2:
                    pe.wait_ge(q_rot, 8)
                elif u >= 3:
                    pe.wait_ge(s1_sub, u - 2)
                pe.wait_ge(qr_ready, 2 * (b // HB) + c + 1)
                pe.wait_ge(kblk_ready, u // 2 + 1)
                product(bank, [(qr[:, c, tok(b)], kblk[:, u // 2 % 4, QH * j:QH * (j + 1), :]),
                               (identb[0:S, 0:S], maskb[0:S, :])]).then_inc(s1_ps, 1)

            def transposes1(u):
                if u < 2:
                    pe.wait_ge(s0_exp, B)
                else:
                    pe.wait_ge(eT1_ready, u - 1)
                pe.wait_ge(s1_exp, u + 1)
                for h in range(QH):
                    last = nc.tensor.transpose(PB[6 + u % 2][0:S, h * S:(h + 1) * S], e1[0:S, u % 4, h, :], ident[0:S, 0:S])
                last.then_inc(eT1_ps, 1)

            def values1(u):
                b, w = u // 4, D0 + 1
                if u % 4 == 0:
                    if b < 2:
                        pe.wait_ge(x1T_ready, B)
                    else:
                        pe.wait_ge(c1_ready, b - 1)
                pe.wait_ge(eT1_ready, u + 1)
                for h in range(QH):
                    hh = QH * (u % 4) + h
                    last = product(PB[b % 2][0:S, hh * w:(hh + 1) * w], [(eT1[0:S, u % 4, h, :], vaug[0:S, b, hh, :])])
                if u % 4 == 3:
                    last.then_inc(c1_ps, 1)

            def ctx_to_cm(b):
                if b:
                    pe.wait_ge(summed, b)
                if b >= 2:
                    pe.wait_ge(x2T_ready, b - 1)
                pe.wait_ge(c1_ready, b + 1)
                to_cm(ctxn, PB[3], b).then_inc(cT1_ps, 1)

            def project1(b):
                pe.wait_ge(cT1_ready, b + 1)
                product(PB[3][0:S, 0:D], [(ctxnT[:, k, tok(b)], xoT[:, k, :]) for k in range(KC)]).then_inc(y2_ps, 1)

            def x2_to_cm(b):
                pe.wait_ge(summed, min(b + 2, B))
                if b == B - 1:
                    pe.wait_ge(x2T_ready, b)
                pe.wait_ge(ln_out, 2 * B + b + 1)
                to_cm(X, PB[3], b).then_inc(x2T_ps, 1)

            def gate_up(j, n):
                slot, t = j // 2 % TURN, j % 2
                pe.wait_ge(hu_ready, n + 1)
                for up in range(2):
                    last = product(PB[4 + 2 * t + up][:, 0:HN], chunks(gu[slot], slice(up * P, (up + 1) * P), T0, half(t)))
                last.then_inc(gu_ps, 1)

            def router(b):
                if b == 0:
                    pe.wait_ge(s1_sub, UN)
                    pe.wait_ge(split_dve, 5)
                pe.wait_ge(x2T_ready, b + 1)
                product(PB[2][0:S, b * NG:(b + 1) * NG], chunks(T0, tok(b), gateT, EVERY)).then_inc(g_ps, 1)

            for u in range(QH * (B - 1) + X2T + 1):
                if u < UN:
                    scores1(u)
                if 3 <= u < UN + 3:
                    transposes1(u - 3)
                for first, step in ((CTXT, ctx_to_cm), (PROJECT, project1), (X2T, x2_to_cm)):
                    b = turn_of(u, first)
                    if b is not None:
                        step(b)
                if 5 <= u < UN + 5:
                    values1(u - 5)
                if ROUTER <= u < ROUTER + B - 2:
                    router(u - ROUTER)
            router(B - 2)
            router(B - 1)

            acc = [[PB[2 * hc + t][:, 0:HN] for t in range(2)] for hc in range(KC)]

            def down(j, n, last_turn):
                slot, t = j // 2 % TURN, j % 2
                pe.wait_ge(hlo_ready, n + 1 + 2)
                for hc in range(KC):
                    pairs = tripled(dn[slot], hid[j % 4], (EVERY, slice(hc * P, (hc + 1) * P)), EVERY)
                    for i, (a, v) in enumerate(pairs):
                        last = mm(acc[hc][t], a, v, start=False, stop=last_turn and j >= WT - 2 and i == 2)
                last.then_inc(down_done, 1)

            pe.wait_ge(eT1_ready, UN)
            pe.wait_ge(w_lo_ready, 1)
            gate_up(0, 0)
            gate_up(1, 1)
            pe.wait_ge(wtm_ready, 1)
            for n, (c, b) in enumerate([(c, b) for c in range(3) for b in range(B)]):
                if n >= 4:
                    pe.wait_ge(wb_ready[n % 2], n // 2 - 1)
                for j, g in enumerate(range(4 * c, min(4 * c + 4, NW))):
                    last = nc.tensor.transpose(PB[n % 4][:, j * S:(j + 1) * S],
                                               wtm[0:S, b, g:g + 1].broadcast_to([S, P]), ident[0:S, 0:S])
                last.then_inc(wb_ps, 1)
            pe.wait_ge(zero_set, 1)
            for i in range(2):
                pe.wait_ge(wb_ready[i], 3 * B // 2)
            for hc in range(KC):
                for t in range(2):
                    mm(acc[hc][t], zero16[:, 0:P], zero16[:], start=True, stop=False).then_inc(down_done, 1)

            def turn(i, last_turn):
                for j in range(WT):
                    if not (last_turn and j + 2 >= WT):
                        if j % 2 == 0:
                            pe.wait_ge(w_lo_ready, i * TURN + (j // 2 + 2))
                        gate_up(j + 2, i * WT + (j + 2))
                    down(j, i * WT + j, last_turn)

            with pe.Fori(0, NC // TURN - 1) as i:
                turn(i, False)
            turn(NC // TURN - 1, True)

            def result_to_tm(b):
                if b == 0:
                    pe.wait_ge(hu_ready, NU + 2)
                pe.wait_ge(fT_ready, 2 * (b // HB) + 2)
                if b >= 4:
                    pe.wait_ge(ln_out, 3 * B + b - 3)
                for k in range(KC):
                    last = product(RB[b % 4][0:S, k * P:(k + 1) * P],
                                   [(fT[:, k, tok(b)], ident[:]), (ident[0:S, 0:S], X[0:S, b, k * P:(k + 1) * P])])
                last.then_inc(y3_ps, 1)

            def x3_to_cm(b):
                if b >= 2:
                    pe.wait_ge(x3T_hi, b - 1)
                pe.wait_ge(ln_out, 3 * B + b + 1)
                to_cm(XN, PB[6 + b % 2], b).then_inc(x3T_ps, 1)

            behind(result_to_tm, x3_to_cm)
            pe.wait_ge(wc_ready, 1)
            pe.wait_ge(fT_ready, 4)
            n = 0
            for h in range(2):
                pe.wait_ge(x3T_ready, HB * (h + 1))
                product(PB[2 + h][:, 0:HN], chunks(wkdT, EVERY, T1, half(h))).then_inc(lat_ps, 1)
                for kind in range(2):
                    for m in range(QC):
                        if n >= 2:
                            pe.wait_ge(q1_ready, n - 1)
                        cols = slice(m * P, (m + 1) * P)
                        if kind == 0:
                            pairs = chunks(wqT, cols, T1, half(h))
                        else:
                            pe.wait_ge(lat_ready, h + 1)
                            pairs = [(wkuT[:, cols], latT[p][:, half(h)]) for p in range(2)]
                        product(PB[n % 2][:, 0:HN], pairs).then_inc(q1_ps, 1)
                        n += 1
            def values_of_latent(b):
                if b < 2:
                    pe.wait_ge(lat_ready, 2)
                else:
                    pe.wait_ge(v1_ready, b - 1)
                product(PB[2 + b % 2][0:S, :], [(latT[p][:, tok(b)], wvuT[:]) for p in range(2)]).then_inc(v1_ps, 1)

            def scores2(u):
                b, j = u // 2, u % 2
                if u < 2:
                    pe.wait_ge(ln_out, 4 * B)
                elif u >= 4:
                    pe.wait_ge(s2_sub, u - 3)
                for h in range(QH):
                    c, lo = h, j * D1
                    last = product(SB2[u % 4][0:S, h * S:(h + 1) * S],
                                   [(q1T[lo:lo + D1, c, tok(b)], k1T[lo:lo + D1, c, tok(b)])])
                last.then_inc(s2_ps, 1)

            def transposes2(u):
                if u >= 2:
                    pe.wait_ge(eT2_ready, u - 1)
                pe.wait_ge(s2_exp, u + 1)
                for h in range(QH):
                    last = nc.tensor.transpose(PB[6 + u % 2][0:S, h * S:(h + 1) * S], e2[0:S, u % 4, h, :], ident[0:S, 0:S])
                last.then_inc(eT2_ps, 1)

            def values2(u):
                w = D1 + 1
                if u >= 2:
                    pe.wait_ge(c2_ready, u - 1)
                else:
                    pe.wait_ge(v1_ready, B)
                pe.wait_ge(eT2_ready, u + 1)
                for h in range(QH):
                    last = product(PB[2 + u % 2][0:S, h * w:(h + 1) * w],
                                   [(eT2[0:S, u % 4, h, :], v1[0:S, u // 2, 2 * h + u % 2, :])])
                last.then_inc(c2_ps, 1)

            pe.wait_ge(q1_ready, 2 * 2 * QC)
            for u in range(U2 + 5):
                if u < U2:
                    scores2(u)
                if u < B // 2:
                    values_of_latent(2 * u)
                    values_of_latent(2 * u + 1)
                if 3 <= u < U2 + 3:
                    transposes2(u - 3)
                if u >= 5:
                    values2(u - 5)
            pe.wait_ge(s2_sub, U2)

            def project(b):
                product(PB[4 + b % 2][0:S, 0:D], [(a1T[:, b % 4, c, :], woT[:, c, :]) for c in range(QC)]).then_inc(y4_ps, 1)

            def heads_to_cm(b):
                if b >= 2:
                    pe.wait_ge(a1T_ready, b - 1)
                pe.wait_ge(c2_ready, 2 * b + 2)
                for c in range(QC):
                    last = nc.tensor.transpose(PB[b % 2][:, c * S:(c + 1) * S],
                                               a1[c // 2][0:S, b, c % 2 * P:(c % 2 + 1) * P], ident[0:S, 0:S])
                last.then_inc(a1T_ps, 1)

            def project2(b):
                pe.wait_ge(a1T_ready, b + 1)
                if b >= 2:
                    pe.wait_ge(summed, B + b - 1)
                product(PB[4 + b % 2][0:S, 0:D], [(a1T[:, b % 4, c, :], woT[:, c, :]) for c in range(QC)]).then_inc(y4_ps, 1)

            def x4_to_cm(b):
                if b < 2:
                    pe.wait_ge(eT2_ready, U2)
                else:
                    pe.wait_ge(x4T_ready, b - 1)
                pe.wait_ge(ln_out, 4 * B + b + 1)
                to_cm(X, PB[6 + b % 2], b).then_inc(x4T_ps, 1)

            def up_of_context(b):
                if b >= 2:
                    pe.wait_ge(gelu_ready, b - 1)
                elif b == 0:
                    pe.wait_ge(ld_ct, LD_CT)
                    pe.wait_ge(a1T_ready, B)
                pe.wait_ge(x4T_ready, b + 1)
                for f, r in enumerate(FROWS):
                    last = product(PB[b % 2][0:r, f * S:(f + 1) * S],
                                   [(cT[:, k, b, f * P:f * P + r], x4T[:, k, tok(b)]) for k in range(KC)])
                last.then_inc(g4_ps, 1)

            for b in range(B + 4):
                if b < B:
                    heads_to_cm(b)
                if 1 <= b < B + 1:
                    project2(b - 1)
                if b >= 4:
                    x4_to_cm(b - 4)
                if b in (B, B + 1):
                    up_of_context(b - B)
            for b in range(2, B):
                up_of_context(b)

            def down_of_context(b):
                if b < 2:
                    pe.wait_ge(c2_ready, U2)
                else:
                    pe.wait_ge(summed, 2 * B + b - 1)
                pe.wait_ge(gelu_ready, b + 1)
                product(PB[2 + b % 2][0:S, 0:D], [(gT[0:r, b, f, :], cN[0:r, b, f, :]) for f, r in enumerate(FROWS)]).then_inc(y5_ps, 1)

            def x5_to_cm(b):
                if b < 2:
                    pe.wait_ge(summed, 2 * B)
                else:
                    pe.wait_ge(pad_ready, b - 1)
                pe.wait_ge(ln_out, 5 * B + b + 1)
                to_cm(XN, PB[4 + b % 2], b).then_inc(x5T_ps, 1)

            behind(down_of_context, x5_to_cm)
            for b in range(B):
                if b == 0:
                    pe.wait_ge(gelu_ready, B)
                    pe.wait_ge(summed, 3 * B)
                elif b >= 4:
                    pe.wait_ge(rg_ready, b - 3)
                pe.wait_ge(mix_ready, 2 * (b // HB) + 2)
                product(PB[b % 4][0:S, 0:D], [(mix[:, 0, k, tok(b)], wrT[:, k, :]) for k in range(KC)]).then_inc(r_ps, 1)
            for n, (h, m) in enumerate([(h, m) for h in range(2) for m in range(KC)]):
                if n < 2:
                    pe.wait_ge(x4T_ready, B)
                else:
                    pe.wait_ge(kpos_ready, n - 1)
                pe.wait_ge(mix_ready, 2 * h + 6)
                product(PB[6 + n % 2][:, 0:HN], [(wkT[:, k, m * P:(m + 1) * P], mix[:, 1, k, half(h)]) for k in range(KC)]).then_inc(kk_ps, 1)
            for b in range(B):
                if b < 2:
                    pe.wait_ge(rg_ready, B)
                else:
                    pe.wait_ge(gated, b - 1)
                pe.wait_ge(ksq_ready, 2 * (b // HB) + 2)
                product(PB[2 + b % 2][0:S, 0:D], [(ksq[:, k, tok(b)], wvT[:, k, :]) for k in range(KC)]).then_inc(y6_ps, 1)

        @block.gpsimd
        def _(pool):
            TT = nc.gpsimd.tensor_tensor
            nc.gpsimd.memset(epsb[:], EPS).then_inc(ones_set, 1)
            nc.gpsimd.memset(vaug[0:S, :, :, D0:D0 + 1], 1.0).then_inc(ones_set, 1)
            nc.gpsimd.memset(zero16[:], 0.0).then_inc(zero_set, 1)
            nc.gpsimd.memset(score[0:S, :, E:2 * E], -1.0).then_inc(sent_set, 1)
            for b in range(B):
                pool.wait_ge(h_hi, b + 1)
                TT(T0[1][:, :, tok(b)], hst[:, b % 4], T0[0][:, :, tok(b)].bitcast(F32), ALU.subtract).then_inc(hT_ready, 1)
            for n, (dst, raw) in enumerate(((cA, raw_cA), (xkT, raw_xk), (xvT, raw_xv))):
                pool.wait_ge(split_hi, n + 3)
                TT(dst[1][:], raw[:], dst[0][:].bitcast(F32), ALU.subtract).then_inc(split_lo, 1)
            pool.wait_ge(ld_x[0], 16)
            pool.wait_ge(ld_x[1], 16)
            pool.wait_ge(ld_b, LD_B)
            for b in range(B):
                TT(RES[0:S, b], X[0:S, b], proj_b[0:S], ALU.add).then_inc(twice, 1)
            for b in range(B):
                pool.wait_ge(twice, b + 1)
                TT(RES[0:S, b], RES[0:S, b], X[0:S, b], ALU.add).then_inc(resid, 1)
            for n, (h, m) in enumerate([(h, m) for h in range(2) for m in range(KC)]):
                pool.wait_ge(k_rot, 2 * n + 2)
                TT(kr[:, m, half(h)], rot[:, n % 2, 0], rot[:, n % 2, 1], ALU.add).then_inc(kr_ready, 1)
            def key_blocks(n):
                b, c = n // 2, n % 2
                if n >= 4:
                    pool.wait_ge(s1_ps, 2 * (n - 4) + 2)
                pool.wait_ge(kr_ready, 2 * (b // HB) + c + 1)
                TT(kblk[:, n % 4], kr[:, c, tok(b)].unsqueeze(1).broadcast_to([P, HC, S]),
                   hmask[:].unsqueeze(2).broadcast_to([P, HC, S]), ALU.mult).then_inc(kblk_ready, 1)

            pool.wait_ge(s0_ps, B)
            for n in range(4):
                key_blocks(n)
            def lower_part(b, hi, ready):
                pool.wait_ge(hi, b + 1)
                TT(T1[1][:, :, tok(b)], cmst[:, b % 4], T1[0][:, :, tok(b)].bitcast(F32), ALU.subtract).then_inc(ready, 1)

            for b in range(B):
                lower_part(b, x1T_hi, x1T_ready)
            for n, (h, m) in enumerate([(h, m) for h in range(2) for m in range(KC)]):
                pool.wait_ge(q_rot, 2 * n + 2)
                TT(qr[:, m, half(h)], rot[:, n % 2, 0], rot[:, n % 2, 1], ALU.add).then_inc(qr_ready, 1)
            for n in range(4, 2 * B):
                key_blocks(n)
                b = n - 4
                if b < B:
                    pool.wait_ge(ln_out, B + b + 1)
                    TT(RES[0:S, b], XN[0:S, b], xo_b[0:S], ALU.add).then_inc(resid, 1)
            copies = groups = 0
            for c in range(NC):
                if c >= 2:
                    pool.wait_ge(hw_ready, 2 * (c - 1))
                row, until = c * P, (c + 1) * P
                while row < until:
                    x = min(row // I, E)
                    end = until if x == E else min(until, (x + 1) * I)
                    if row % P == P // 4:
                        end = min(end, row + P // 4)
                    rows = slice(row % P, row % P + end - row)
                    if x >= 4 * groups:
                        groups += 1
                        for i in range(2):
                            pool.wait_ge(wb_ready[i], groups * B // 2)
                    if copies:
                        pool.wait_ge(row_copy, copies)
                    nc.gpsimd.tensor_copy(wrow[rows, c % 2], wb[rows, x]).then_inc(row_copy, 1)
                    copies += 1
                    row = end
                pool.wait_ge(row_copy, copies)
                nc.gpsimd.sem_inc(wrow_ready, 1)

            pool.wait_ge(wc_hi, 4)
            TT(wkdT[1][:], raw_wkd[:], wkdT[0][:].bitcast(F32), ALU.subtract)
            TT(wqT[1][:], raw_wq[:], wqT[0][:].bitcast(F32), ALU.subtract).then_inc(wc_whole, 1)
            pool.wait_ge(wc_whole, 1)
            for w, raw in ((wkuT, raw_wku), (wvuT, raw_wvu)):
                last = TT(w[R1:], raw[R1:], w[R1:].bitcast(F32), ALU.subtract)
            last.then_inc(wc_ready, 1)
            pool.wait_ge(wc_ready, 1)
            pool.wait_ge(fT_ready, 4)
            nc.gpsimd.memset(v1[0:S, :, :, D1:D1 + 1], 1.0).then_inc(one1_set, 1)
            for b in range(B):
                lower_part(b, x3T_hi, x3T_ready)
            pool.wait_ge(ld_c, LD_C)
            nc.gpsimd.tensor_scalar(omm[:], mu[:], -1.0, 1.0, ALU.mult, ALU.add).then_inc(omm_ready, 1)
            pool.wait_ge(g4_ps, 1)
            nc.gpsimd.memset(pad[:, :, :, 0:1], 0.0).then_inc(pad_zero, 1)
            for n, (h, m) in enumerate([(h, m) for h in range(2) for m in range(KC)]):
                pool.wait_ge(kpos_ready, n + 1)
                TT(ksq[:, m, half(h)], kpos[:, n % 2], kpos[:, n % 2], ALU.mult).then_inc(ksq_ready, 1)
            for b in range(B):
                pool.wait_ge(gated, b + 1)
                TT(RES[0:S, b], RES[0:S, b], XN[0:S, b], ALU.add).then_inc(summed_last, 1)

        @block.scalar
        def _(act):
            A = nc.scalar.activation

            def norm_scale(k, b):
                act.wait_ge(ln_mv, k * B + b + 1)
                A(lnv[0:S, b:b + 1], mv[0:S, b, 1:2], ACT.Ln, bias=epsb[0:S]).then_inc(ln_lg, 1)
                act.wait_ge(ln_lg, k * B + b + 1)
                A(rstd[0:S, b:b + 1], lnv[0:S, b:b + 1], ACT.Exp, scale=-0.5).then_inc(ln_rs, 1)

            def norms_then(k, evac):
                for b in range(B + 3):
                    if b < B:
                        norm_scale(k, b)
                    if b >= 3:
                        evac(b - 3)

            def cm_copy(ps_ready, banks, dst, done):
                dst = dst[0] if isinstance(dst, list) else dst

                def evac(b):
                    act.wait_ge(ps_ready, b + 1)
                    A(dst[:, :, tok(b)], banks[b % len(banks)][:, 0:KC * S].rearrange("p (k s) -> p k s", s=S), ACT.Copy).then_inc(done, 1)
                return evac

            def staged_copy(ps_ready, banks, done, ready):
                def evac(b):
                    act.wait_ge(ps_ready, b + 1)
                    if b >= 4:
                        act.wait_ge(ready, b - 3)
                    ps = banks[b % 2][:, 0:KC * S].rearrange("p (k s) -> p k s", s=S)
                    A(cmst[:, b % 4], ps, ACT.Copy)
                    A(T1[0][:, :, tok(b)], ps, ACT.Copy).then_inc(done, 1)
                return evac

            nc.scalar.preload_act_table_set("natural_log_exp_and_others")
            act.wait_ge(ones_set, 1)

            def hi_of(dst, raw, cols=slice(None)):
                A(dst[0][:, :, cols], raw[:, :, cols], ACT.Copy).then_inc(split_hi, 1)

            def h_of(b):
                act.wait_ge(hT_ps, b + 1)
                if b >= 4:
                    act.wait_ge(hT_ready, b - 3)
                for k in range(KC):
                    last = A(hst[:, b % 4, k, :], HB4[b % 4][:, k * S:(k + 1) * S], ACT.Identity,
                             bias=colb[:, 2 + k:3 + k], scale=colb[:, k:k + 1])
                last.then_inc(h_ready[1], 1)

            def h_hi_of(b):
                if b == 1:
                    act.wait_ge(ld_a, LD_A)
                if b % 2:
                    h_of(b)
                act.wait_ge(h_ready[b % 2], b // 2 + 1)
                A(T0[0][:, :, tok(b)], hst[:, b % 4], ACT.Copy).then_inc(h_hi, 1)

            for b in range(B + 4):
                if b < B:
                    norm_scale(0, b)
                if b == B - 1:
                    act.wait_ge(ld_q, LD_Q)
                    hi_of(qkvT, raw_qkv, slice(0, 2 * D))
                if b >= 4:
                    h_hi_of(b - 4)
            hi_of(qkvT, raw_qkv, slice(2 * D, 3 * D))
            act.wait_ge(ld_k, LD_K)
            hi_of(cA, raw_cA)
            hi_of(xkT, raw_xk)
            act.wait_ge(ld_v, LD_V)
            hi_of(xvT, raw_xv)
            hi_of(xqT, raw_xq)
            for n, (h, m) in enumerate([(h, m) for h in range(2) for m in range(KC)]):
                act.wait_ge(vT_ps, n + 1)
                A(vT[:, m, half(h)], PB[4 + m][:, 0:HN], ACT.Identity, bias=colb[:, 4 + m:5 + m]).then_inc(vT_ready, 1)

            def weights_hi(slot):
                A(gu[slot][0][:], w_gu[slot][:], ACT.Copy)
                A(dn[slot][0][:], w_dn[slot][:], ACT.Copy).then_inc(w_hi_ready, 1)

            def exp0(b):
                act.wait_ge(s0_nb, b + 1)
                if b >= 4:
                    act.wait_ge(eT0_ps, b - 3)
                for q in range(KC):
                    last = A(e0[:, b % 4, q, :], PB[6 + b % 2][:, q * D:(q + 1) * D], ACT.Exp,
                             bias=nb0[:, b, q:q + 1], scale=SCALE0, accum_out=sum0[:, b, q:q + 1])
                last.then_inc(s0_exp, 1)

            def a_evac(b):
                act.wait_ge(aT_ps, b + 1)
                act.wait_ge(s0_rs, b + 1)
                for q in range(KC):
                    last = A(aT[:, b, q, :], PB[2 + b % 2][:, q * S:(q + 1) * S], ACT.Copy, scale=rs0[:, b, q:q + 1])
                last.then_inc(aT_ready, 1)

            act.wait_ge(split_lo, 3)
            act.wait_ge(split_dve, 3)
            for b in range(B + 4):
                if b < B:
                    exp0(b)
                if b >= 4:
                    a_evac(b - 4)
            norms_then(1, staged_copy(x1T_ps, PB[0:2], x1T_hi, x1T_ready))

            def exps(u, sub, e, scale, done):
                act.wait_ge(sub, u + 1)
                A(e[0:S, u % 4], e[0:S, u % 4], ACT.Exp, scale=scale).then_inc(done, 1)

            def exp_evac(u, ps_ready, eT, done):
                act.wait_ge(ps_ready, u + 1)
                A(eT[0:S, u % 4], heads(PB[6 + u % 2][0:S, 0:QH * S]), ACT.Copy).then_inc(done, 1)

            ctxn_evac = cm_copy(cT1_ps, [PB[3]], ctxnT, cT1_ready)
            x2_evac = cm_copy(x2T_ps, [PB[3]], T0, x2T_hi)
            for u in range(QH * (B - 1) + X2T + 1):
                if u in (UN // 2, UN // 2 + 4):
                    s = (u - UN // 2) // 4
                    act.wait_ge(ld_w[s], LD_W)
                    weights_hi(s)
                if u < UN:
                    exps(u, s1_sub, e1, D0 ** -0.5, s1_exp)
                if 3 <= u < UN + 3:
                    exp_evac(u - 3, eT1_ps, eT1, eT1_ready)
                for first, step in ((CTXT, ctxn_evac), (PROJECT, lambda b: norm_scale(2, b)), (X2T, x2_evac)):
                    b = turn_of(u, first)
                    if b is not None:
                        step(b)
            act.wait_ge(g_step, 2)
            logits = PB[2][0:S, 0:B * NG].rearrange("p (b e) -> p b e", e=NG)
            A(gexp[0:S, :, E:E + 1], logits[:, :, E:E + 1], ACT.Exp, scale=-1.0).then_inc(g_exp, 1)
            A(gexp[0:S, :, 0:E], gexp[0:S, :, 0:E], ACT.Exp).then_inc(g_exp, 1)
            nc.scalar.preload_act_table_set("silu_and_others")
            for n in range(0, 3 * B, 2):
                act.wait_ge(wb_ps, n + 1)
                A(*wb_tile(n), ACT.Copy).then_inc(wb_ready[0], 1)

            def silu(j, n):
                act.wait_ge(gu_ps, n + 1)
                act.wait_ge(hu_ready, n + 1)
                A(sg[:, j % 2], PB[4 + 2 * (j % 2)][:, 0:HN], ACT.Silu).then_inc(silu_ready, 1)

            def hidden_hi(j, n):
                act.wait_ge(hw_ready, n + 1)
                act.wait_ge(down_done, n + 1)
                A(hid[j % 4][0][:], hw[:, j % 2], ACT.Copy).then_inc(hhi_ready, 1)

            first_weights = [(wkdT[0][:], raw_wkd[:]), (wqT[0][:], raw_wq[:]), (wkuT[:], raw_wku[:]), (wvuT[:], raw_wvu[:])]

            def turn(i, last_turn):
                for j in range(WT):
                    silu(j, i * WT + j)
                    if last_turn and j == WT - 1:
                        nc.scalar.preload_act_table_set("natural_log_exp_and_others")
                    if last_turn and j < len(first_weights):
                        if j == 0:
                            act.wait_ge(ld_c, LD_C)
                        A(*first_weights[j], ACT.Copy).then_inc(wc_hi, 1)
                    hidden_hi(j, i * WT + j)
                    if j % 2 == 0 and not (last_turn and j // 2 + 2 >= TURN):
                        ahead = j // 2 + 2
                        act.wait_ge(ld_w[ahead % TURN], i * LD_W + (ahead // TURN + 1) * LD_W)
                        act.wait_ge(down_done, i * WT + (j + 2))
                        weights_hi(ahead % TURN)

            with act.Fori(0, NC // TURN - 1) as i:
                turn(i, False)
            turn(NC // TURN - 1, True)
            for t in range(2):
                act.wait_ge(down_done, NU + 4 - 1 + t)
                for hc in range(KC):
                    A(fT[:, hc, half(t)], PB[2 * hc + t][:, 0:HN], ACT.Copy).then_inc(fT_ready, 1)

            norms_then(3, staged_copy(x3T_ps, PB[6:8], x3T_hi, x3T_ready))
            n = 0
            for h in range(2):
                act.wait_ge(lat_ps, h + 1)
                A(latT[0][:, half(h)], PB[2 + h][:, 0:HN], ACT.Copy).then_inc(lat_hi, 1)
                for dst in (q1T, k1T):
                    for m in range(QC):
                        act.wait_ge(q1_ps, n + 1)
                        A(dst[:, m, half(h)], PB[n % 2][:, 0:HN], ACT.Copy).then_inc(q1_ready, 1)
                        n += 1
            act.wait_ge(one1_set, 1)

            def latent_value(b):
                act.wait_ge(v1_ps, b + 1)
                A(v1[0:S, b, :, 0:D1], PB[2 + b % 2][0:S].rearrange("p (h d) -> p h d", d=D1), ACT.Copy).then_inc(v1_ready, 1)

            for u in range(U2 + 3):
                if u < B // 2:
                    latent_value(2 * u)
                if u < U2:
                    exps(u, s2_sub, e2, D1 ** -0.5, s2_exp)
                if u < B // 2:
                    latent_value(2 * u + 1)
                if u >= 3:
                    exp_evac(u - 3, eT2_ps, eT2, eT2_ready)
            x4_evac = cm_copy(x4T_ps, PB[6:8], x4T, x4T_ready)
            for b in range(B + 4):
                if b < B:
                    act.wait_ge(a1T_ps, b + 1)
                    if b >= 4:
                        act.wait_ge(y4_ps, b - 3)
                    A(a1T[:, b % 4], heads(PB[b % 2][:, 0:QC * S]), ACT.Copy).then_inc(a1T_ready, 1)
                if 2 <= b < B + 2:
                    norm_scale(4, b - 2)
                if b == B + 2:
                    nc.scalar.preload_act_table_set("gelu_apprx_tanh_and_others")
                if b >= 4:
                    x4_evac(b - 4)
            for b in range(B):
                act.wait_ge(g4_ps, b + 1)
                f = FC - 1
                A(gT[:, b, 0:f], PB[b % 2][:, 0:f * S].rearrange("p (f s) -> p f s", s=S), ACT.Gelu_apprx_tanh)
                A(gT[0:FROWS[f], b, f], PB[b % 2][0:FROWS[f], f * S:(f + 1) * S], ACT.Gelu_apprx_tanh).then_inc(gelu_ready, 1)
            nc.scalar.preload_act_table_set("natural_log_exp_and_others")

            def pad_evac(b):
                act.wait_ge(x5T_ps, b + 1)
                A(pad[:, :, b, 1:S + 1], PB[4 + b % 2][:, 0:KC * S].rearrange("p (k s) -> p k s", s=S), ACT.Copy).then_inc(pad_ready, 1)

            def scaled(n):
                a, h, k = n // 4, n // 2 % 2, n % 2
                if n == 2:
                    act.wait_ge(pad_ready, B)
                elif n == 0:
                    act.wait_ge(pad_ready, HB)
                if n >= 4:
                    act.wait_ge(mix_ready, n - 3)
                A(mixt[:, n % 4].rearrange("p (b s) -> p b s", s=S), pad[:, k, h * HB:(h + 1) * HB, 1:S + 1],
                  ACT.Copy, scale=mu[:, a, k:k + 1]).then_inc(mixt_ready, 1)

            for b in range(B + 3):
                if b < B:
                    norm_scale(5, b)
                if b >= 3:
                    pad_evac(b - 3)
                if b == B - 1:
                    scaled(0)
                    scaled(1)
            nc.scalar.preload_act_table_set("sigmoid_and_others")
            for n in range(2, 8):
                scaled(n)
            for b in range(B):
                act.wait_ge(r_ps, b + 1)
                A(rg[0:S, b], PB[b % 4][0:S, 0:D], ACT.Sigmoid).then_inc(rg_ready, 1)
            nc.scalar.preload_act_table_set("natural_log_exp_and_others")
            for n in range(4):
                act.wait_ge(kk_ps, n + 1)
                if n >= 2:
                    act.wait_ge(ksq_ready, n - 1)
                A(kpos[:, n % 2], PB[6 + n % 2][:, 0:HN], ACT.Relu).then_inc(kpos_ready, 1)
            for b in range(B):
                norm_scale(6, b)

        @block.vector
        def _(dve):
            V = nc.vector

            V.sem_inc(hu_ready, 2)
            V.sem_inc(hlo_ready, 2)

            def norm_source(k, b):
                if k == 1:
                    return PB[4 + b % 4][0:S, 0:D]
                if k == 3:
                    return RB[b % 4][0:S, 0:D]
                return (X if k == 0 else RES)[0:S, b]

            def norm_stats(k, b):
                V.bn_stats(stats[0:S, b], norm_source(k, b)).then_inc(ln_st, 1)
                dve.wait_ge(ln_st, k * B + b + 1)
                V.bn_aggr(mv[0:S, b], stats[0:S, b]).then_inc(ln_mv, 1)

            def normalize(k, b, dst):
                dve.wait_ge(ln_rs, k * B + b + 1)
                V.tensor_scalar(dst[0:S, b], norm_source(k, b), mv[0:S, b, 0:1], rstd[0:S, b:b + 1],
                                ALU.subtract, ALU.mult).then_inc(ln_out, 1)

            def add_and_norm(k, first, dst, add):
                for b in range(B + 2):
                    if b < B:
                        add(b)
                        dve.wait_ge(summed, first + b + 1)
                        norm_stats(k, b)
                    if b >= 2:
                        normalize(k, b - 2, dst)

            def norm_of_bank(k, dst, ready):
                for b in range(B + 2):
                    if b < B:
                        dve.wait_ge(ready, b + 1)
                        norm_stats(k, b)
                    if b >= 2:
                        normalize(k, b - 2, dst)

            def h_of(b):
                dve.wait_ge(hT_ps, b + 1)
                if b >= 4:
                    dve.wait_ge(hT_ready, b - 3)
                for k in range(KC):
                    last = V.tensor_scalar(hst[:, b % 4, k, :], HB4[b % 4][:, k * S:(k + 1) * S],
                                           colb[:, k:k + 1], colb[:, 2 + k:3 + k], ALU.mult, ALU.add)
                last.then_inc(h_ready[0], 1)

            for b in range(B + 3):
                if b % HB == 0 and b < B:
                    dve.wait_ge(ld_x[b // HB], 16)
                if b < B:
                    norm_stats(0, b)
                if 2 <= b < B + 2:
                    normalize(0, b - 2, XN)
                if b == 4:
                    dve.wait_ge(ld_a, LD_A)
                if b >= 4 and b % 2 == 0:
                    h_of(b - 4)

            def lo_of(dst, raw, cols=slice(None)):
                V.tensor_tensor(dst[1][:, :, cols], raw[:, :, cols], dst[0][:, :, cols].bitcast(F32), ALU.subtract).then_inc(split_dve, 1)

            dve.wait_ge(split_hi, 1)
            lo_of(qkvT, raw_qkv, slice(0, 2 * D))
            dve.wait_ge(split_hi, 2)
            lo_of(qkvT, raw_qkv, slice(2 * D, 3 * D))

            exchange = [p // D0 * D0 + (p + D0 // 2) % D0 for p in range(32)]

            def rotate(n, first, ps_ready, banks, col, done, summed_up):
                m = n % 2
                cols = [colb[:, col + 2 * sw + m:col + 2 * sw + m + 1] for sw in range(2)]

                def seqs(ap):
                    return ap.rearrange("p (b s) -> p b s", s=S)

                def turned(sw, src):
                    V.scalar_tensor_tensor(out=seqs(rot[:, n % 2, sw]), in0=seqs(src), scalar=cols[sw],
                                           in1=rope[:, sw:sw + 1].broadcast_to([P, HB, S]),
                                           op0=ALU.add, op1=ALU.mult).then_inc(done, 1)

                dve.wait_ge(ps_ready, n + 1)
                if n >= 2:
                    dve.wait_ge(done, 2 * (n - 1))
                V.stream_shuffle(swap[:, n % 2], banks[n % 2][:, 0:HN], exchange).then_inc(swapped, 1)
                if n >= 2:
                    dve.wait_ge(summed_up, n - 1)
                turned(0, banks[n % 2][:, 0:HN])
                dve.wait_ge(swapped, first + n + 1)
                turned(1, swap[:, n % 2])

            dve.wait_ge(ones_set, 2)

            def context_value(b):
                dve.wait_ge(v_ps, b + 1)
                V.tensor_tensor(vaug[0:S, b, :, 0:D0], PB[4 + b % 2][0:S, 0:D].rearrange("p (h d) -> p h d", d=D0),
                                xv_b[0:S].rearrange("p (h d) -> p h d", d=D0), ALU.add).then_inc(v_ready, 1)

            for b in range(B):
                dve.wait_ge(qk_ps, b + 1)
                V.tensor_tensor(qk[0:S, b], PB[2 + b % 2][0:S, :], qk_b[0:S], ALU.add).then_inc(qk_ready, 1)

            def weights_lo(slot):
                V.tensor_tensor(gu[slot][1][:], w_gu[slot][:], gu[slot][0][:].bitcast(F32), ALU.subtract)
                V.tensor_tensor(dn[slot][1][:], w_dn[slot][:], dn[slot][0][:].bitcast(F32), ALU.subtract).then_inc(w_lo_ready, 1)

            dve.wait_ge(split_hi, 6)
            lo_of(xqT, raw_xq)
            V.tensor_copy(gateT[0][:], raw_gate[:]).then_inc(split_dve, 1)
            dve.wait_ge(split_dve, 4)
            lo_of(gateT, raw_gate)

            def max0_of(b):
                dve.wait_ge(s0_ps, b + 1)
                V.tensor_reduce(max0[:, b], PB[6 + b % 2][:].rearrange("p (q k) -> p q k", k=D), X_AXIS, ALU.max,
                                negate=True).then_inc(s0_max, 1)
                dve.wait_ge(s0_max, b + 1)
                V.tensor_scalar_mul(nb0[:, b], max0[:, b], SCALE0).then_inc(s0_nb, 1)

            def e_evac(b):
                dve.wait_ge(s0_exp, b + 1)
                V.reciprocal(rs0[:, b], sum0[:, b]).then_inc(s0_rs, 1)
                dve.wait_ge(eT0_ps, b + 1)
                if b >= 4:
                    dve.wait_ge(aT_ps, b - 3)
                V.tensor_copy(eT0[:, b % 4], PB[b % 2][:].rearrange("p (k q) -> p k q", q=D)).then_inc(eT0_ready, 1)

            for b in range(B + 5):
                if b < B:
                    max0_of(b)
                if 2 <= b < B + 2:
                    e_evac(b - 2)
                if 1 <= b < 5:
                    rotate(b - 1, 0, kp_ps, PB[4:6], 10, k_rot, kr_ready)
                if b >= 5:
                    context_value(b - 5)

            def lower_part(dst, banks, hi_ready, done):
                def lower(b):
                    dve.wait_ge(hi_ready, b + 1)
                    V.tensor_tensor(dst[1][:, :, tok(b)], banks[b % len(banks)][:, 0:KC * S].rearrange("p (k s) -> p k s", s=S),
                                    dst[0][:, :, tok(b)].bitcast(F32), ALU.subtract).then_inc(done, 1)
                return lower

            norm_of_bank(1, XN, y1_ps)
            for n in range(4):
                if n < 2:
                    dve.wait_ge(kr_ready, 3 + n)
                rotate(n, 4, qp_ps, PB[2:4], 6, q_rot, qr_ready)

            def maxima(u, ps_ready, banks, mx, used, maxed):
                dve.wait_ge(ps_ready, u + 1)
                if u >= 4:
                    dve.wait_ge(used, u - 3)
                V.tensor_reduce(mx[0:S, QH * u:QH * (u + 1)], heads(banks[u % len(banks)][0:S, 0:QH * S]),
                                X_AXIS, ALU.max).then_inc(maxed, 1)

            def minus_maxima(u, banks, mx, e, maxed, done):
                dve.wait_ge(maxed, u + 1)
                V.tensor_tensor(e[0:S, u % 4], heads(banks[u % len(banks)][0:S, 0:QH * S]),
                                mx[0:S, QH * u:QH * (u + 1)].unsqueeze(2).broadcast_to([S, QH, S]),
                                ALU.subtract).then_inc(done, 1)

            def inverse_sums(n, ps, rs, dim, ps_ready, inverted):
                dve.wait_ge(ps_ready, n + 1)
                V.reciprocal(rs.unsqueeze(2), ps[:, :, dim:dim + 1]).then_inc(inverted, 1)

            def scaled_values(n, ps, rs, dst, dim, inverted, done):
                dve.wait_ge(inverted, n + 1)
                V.tensor_tensor(dst, ps[:, :, 0:dim],
                                rs.unsqueeze(2).broadcast_to([S, ps.shape[1], dim]), ALU.mult).then_inc(done, 1)

            def out1(b):
                ps = PB[b % 2][0:S, 0:H0 * (D0 + 1)].rearrange("p (h d) -> p h d", d=D0 + 1)
                inverse_sums(b, ps, rs1[0:S, b], D0, c1_ps, c1_rs)
                scaled_values(b, ps, rs1[0:S, b], ctxn[0:S, b].rearrange("p (h d) -> p h d", d=D0), D0, c1_rs, c1_ready)

            def add2(b):
                dve.wait_ge(y2_ps, b + 1)
                dve.wait_ge(resid, B + b + 1)
                V.tensor_tensor(RES[0:S, b], PB[3][0:S, 0:D], RES[0:S, b], ALU.add).then_inc(summed, 1)
                dve.wait_ge(summed, b + 1)
                norm_stats(2, b)

            x2_lower = lower_part(T0, [PB[3]], x2T_hi, x2T_ready)
            for u in range(QH * (B - 1) + X2T_LO + 1):
                if u in (UN // 2 + 1, UN // 2 + 5):
                    s = (u - UN // 2) // 4
                    dve.wait_ge(w_hi_ready, s + 1)
                    weights_lo(s)
                if u < UN:
                    maxima(u, s1_ps, SB1, max1, eT1_ps, s1_max)
                    minus_maxima(u, SB1, max1, e1, s1_max, s1_sub)
                for first, step in ((OUT, out1), (PROJECT, add2), (NORMED, lambda b: normalize(2, b, X)), (X2T_LO, x2_lower)):
                    b = turn_of(u, first)
                    if b is not None:
                        step(b)
            logits = PB[2][0:S, 0:B * NG].rearrange("p (b e) -> p b e", e=NG)
            ge, sc8 = gexp[0:S, :, 0:E], score[0:S, :, 0:E]
            dve.wait_ge(g_ps, B)
            V.reduce_max(gmax[0:S], logits[:, :, 0:E], X_AXIS).then_inc(g_step, 1)
            dve.wait_ge(g_step, 1)
            V.tensor_tensor(ge, logits[:, :, 0:E], gmax[0:S].unsqueeze(2).broadcast_to([S, B, E]), ALU.subtract).then_inc(g_step, 1)
            dve.wait_ge(g_exp, 2)
            V.reduce_sum(gsum[0:S], ge, X_AXIS).then_inc(g_step, 1)
            V.tensor_scalar_add(sig1[0:S].unsqueeze(2), gexp[0:S, :, E:E + 1], 1.0).then_inc(g_step, 1)
            dve.wait_ge(g_step, 4)
            V.reciprocal(grs[0:S], gsum[0:S]).then_inc(g_step, 1)
            V.reciprocal(wtm[0:S, :, E:E + 1], sig1[0:S].unsqueeze(2)).then_inc(g_step, 1)
            dve.wait_ge(g_step, 6)
            V.tensor_tensor(sc8, ge, grs[0:S].unsqueeze(2).broadcast_to([S, B, E]), ALU.mult).then_inc(g_step, 1)
            dve.wait_ge(g_step, 7)
            dve.wait_ge(sent_set, 1)
            for b in range(B):
                last = V.max(out=top[0:S, b], in_=score[0:S, b])
            last.then_inc(g_step, 1)
            dve.wait_ge(g_step, 8)
            V.memset(top[0:S, :, TOPK:8], -1.0).then_inc(g_step, 1)
            dve.wait_ge(g_step, 9)
            for b in range(B):
                last = V.match_replace(picked[0:S, b], top[0:S, b], score[0:S, b], -2.0)
            last.then_inc(g_step, 1)
            dve.wait_ge(g_step, 10)
            V.scalar_tensor_tensor(out=wtm[0:S, :, 0:E], in0=picked[0:S, :, 0:E], scalar=-1.5, in1=sc8,
                                   op0=ALU.is_lt, op1=ALU.mult).then_inc(wtm_ready, 1)

            for n in range(1, 3 * B, 2):
                dve.wait_ge(wb_ps, n + 1)
                V.tensor_copy(*wb_tile(n)).then_inc(wb_ready[1], 1)

            def multiply(j, n):
                dve.wait_ge(silu_ready, n + 1)
                V.tensor_tensor(hu[:, j % 2], sg[:, j % 2], PB[5 + 2 * (j % 2)][:, 0:HN], ALU.mult).then_inc(hu_ready, 1)

            def weigh(j, n):
                dve.wait_ge(hu_ready, n + 1 + 2)
                dve.wait_ge(hlo_ready, n + 1)
                V.tensor_tensor(hw[:, j % 2], hu[:, j % 2], wrow[:, j // 2 % 2, half(j % 2)], ALU.mult).then_inc(hw_ready, 1)

            def hidden_lo(j, n):
                dve.wait_ge(hhi_ready, n + 1)
                V.tensor_tensor(hid[j % 4][1][:], hw[:, j % 2], hid[j % 4][0][:].bitcast(F32), ALU.subtract).then_inc(hlo_ready, 1)

            def turn(i, last_turn):
                for j in range(WT):
                    multiply(j, i * WT + j)
                    if j % 2 == 0:
                        dve.wait_ge(wrow_ready, i * TURN + (j // 2 + 1))
                    weigh(j, i * WT + j)
                    hidden_lo(j, i * WT + j)
                    if j % 2 == 0 and not (last_turn and j // 2 + 2 >= TURN):
                        dve.wait_ge(w_hi_ready, i * TURN + (j // 2 + 3))
                        weights_lo((j // 2 + 2) % TURN)

            with dve.Fori(0, NC // TURN - 1) as i:
                turn(i, False)
            turn(NC // TURN - 1, True)

            norm_of_bank(3, XN, y3_ps)
            for h in range(2):
                dve.wait_ge(lat_hi, h + 1)
                V.tensor_tensor(latT[1][:, half(h)], PB[2 + h][:, 0:HN], latT[0][:, half(h)].bitcast(F32), ALU.subtract).then_inc(lat_ready, 1)
            for u in range(U2 + 6):
                n = u - 6
                ps = PB[2 + n % 2][0:S, 0:QH * (D1 + 1)].rearrange("p (h d) -> p h d", d=D1 + 1)
                rs = rs2[0:S, QH * max(n, 0):QH * (max(n, 0) + 1)]
                if u < U2:
                    maxima(u, s2_ps, SB2, max2, eT2_ps, s2_max)
                if n >= 0:
                    inverse_sums(n, ps, rs, D1, c2_ps, c2_rs)
                if u < U2:
                    minus_maxima(u, SB2, max2, e2, s2_max, s2_sub)
                if n >= 0:
                    scaled_values(n, ps, rs, a1[n % 2][0:S, n // 2].rearrange("p (h d) -> p h d", d=D1), D1, c2_rs, c2_ready)

            def add4(b):
                dve.wait_ge(y4_ps, b + 1)
                V.tensor_tensor(RES[0:S, b], PB[4 + b % 2][0:S, 0:D], XN[0:S, b], ALU.add).then_inc(summed, 1)

            add_and_norm(4, B, X, add4)

            def add5(b):
                dve.wait_ge(y5_ps, b + 1)
                V.tensor_tensor(RES[0:S, b], PB[2 + b % 2][0:S, 0:D], X[0:S, b], ALU.add).then_inc(summed, 1)

            add_and_norm(5, 2 * B, XN, add5)
            dve.wait_ge(omm_ready, 1)
            dve.wait_ge(pad_zero, 1)
            n = 0
            for a in (0, 1):
                for h in range(2):
                    for k in range(KC):
                        dve.wait_ge(mixt_ready, n + 1)
                        V.scalar_tensor_tensor(out=mix[:, a, k, half(h)].rearrange("p (b s) -> p b s", s=S),
                                               in0=pad[:, k, h * HB:(h + 1) * HB, 0:S], scalar=omm[:, a, k:k + 1],
                                               in1=mixt[:, n % 4].rearrange("p (b s) -> p b s", s=S),
                                               op0=ALU.mult, op1=ALU.add).then_inc(mix_ready, 1)
                        n += 1
            dve.wait_ge(rg_ready, B)
            for b in range(B + 3):
                if b < B:
                    dve.wait_ge(y6_ps, b + 1)
                    V.tensor_tensor(RES[0:S, b], PB[2 + b % 2][0:S, 0:D], rg[0:S, b], ALU.mult).then_inc(gated, 1)
                if 1 <= b < B + 1:
                    dve.wait_ge(summed_last, b)
                    norm_stats(6, b - 1)
                if b >= 3:
                    normalize(6, b - 3, X)


def _constants():
    half = D0 // 2
    pos = np.arange(S, dtype=np.float32)
    freqs = (np.float32(1.0) / np.float32(10000.0) ** (np.arange(half, dtype=np.float32) / np.float32(half))).astype(np.float32)
    ang = pos[:, None] * freqs[None, :]
    cos, sin = np.cos(ang).astype(np.float32), np.sin(ang).astype(np.float32)
    cc = np.concatenate([cos, cos], 1).T
    ss = np.concatenate([-sin, sin], 1).T
    rope = np.stack([np.tile(cc, (HC, 1)), np.tile(ss, (HC, 1))], 1)
    bf16 = mybir.dt.np(BF16)
    q, k = np.arange(S)[:, None], np.arange(S)[None, :]
    masked = (k > q) | (k < q - WINDOW)
    mask = np.tile(np.where(masked, np.float32(MASKED), np.float32(0)), (1, QH))
    return {
        "ident": np.eye(P, dtype=np.float32), "identb": np.eye(P).astype(bf16), "maskb": mask.astype(bf16),
        "rope": np.ascontiguousarray(rope, np.float32),
        "hmask": (np.arange(P)[:, None] // D0 == np.arange(HC)[None, :]).astype(np.float32),
    }


def _laid_out(a):
    def swapped(w):
        return w.reshape(H0, 2, D0 // 2, *w.shape[1:])[:, ::-1].reshape(w.shape)

    def cols(v):
        return v.reshape(KC, P).T

    ctx = a["ctx_1024"]
    gu, dn = a["L0_ffn_experts_gate_up"], a["L0_ffn_experts_down"]
    sg, su, sd = a["L0_ffn_shared_gate_w"], a["L0_ffn_shared_up_w"], a["L0_ffn_shared_down_w"]

    def hidden(experts, shared):
        rows = np.concatenate([experts.reshape(-1, D), shared], 0)
        return np.concatenate([rows, np.zeros((NC * P - HID, D), rows.dtype)], 0).reshape(NC, P, D)

    qb, kb = a["L0_xattn_q_b"], a["L0_xattn_k_b"]
    qw, kw = a["L0_xattn_q_w"], a["L0_xattn_k_w"]
    out = {
        "x": a["x"],
        "cA": ctx[:, :S].transpose(2, 0, 1).reshape(D, N),
        "cT": ctx.transpose(2, 0, 1), "cN": ctx,
        "qkvT": a["L0_attn_qkv_w"].T, "qk_b": a["L0_attn_qkv_b"][:2 * D],
        "projT": a["L0_attn_proj_w"].T, "proj_b": a["L0_attn_proj_b"],
        "xqT": qw.T, "xkT": kw.T,
        "xvT": a["L0_xattn_v_w"].T, "xv_b": a["L0_xattn_v_b"],
        "xoT": a["L0_xattn_o_w"].T, "xo_b": a["L0_xattn_o_b"],
        "colb": np.concatenate([cols(v) for v in (
            a["L0_attn_norm_w"], a["L0_attn_norm_b"], a["L0_attn_qkv_b"][2 * D:],
            qb, swapped(qb), kb, swapped(kb))], 1),
        "gateT": np.concatenate([a["L0_ffn_gate_w"], a["L0_ffn_shared_expert_gate_w"], np.zeros((1, D), np.float32)], 0).T,
        "guT": np.concatenate([hidden(gu[:, :I], sg), hidden(gu[:, I:], su)], 1).transpose(0, 2, 1),
        "dnT": hidden(dn.transpose(0, 2, 1), sd.T),
        "wqT": a["L1_attn_Wq"].T, "wkdT": a["L1_attn_Wkv_down"].T, "wkuT": a["L1_attn_Wk_up"].T,
        "wvuT": a["L1_attn_Wv_up"].T,
        "woT": a["L1_attn_Wo"].T.reshape(H1 // 2, 2, D1, D).transpose(1, 0, 2, 3).reshape(H1 * D1, D),
        "wrT": a["L1_ffn_W_r"].T, "wkT": a["L1_ffn_W_k"].T, "wvT": a["L1_ffn_W_v"].T,
        "mu": np.concatenate([cols(a["L1_ffn_mu_r"]), cols(a["L1_ffn_mu_k"])], 1),
    }
    return {**out, **_constants()}


def kernel(**inputs):
    import concourse.bacc as bacc
    from concourse.bass_utils import run_bass_kernel_spmd

    nc = bacc.Bacc("TRN2", target_bir_lowering=False, num_devices=1)
    arrays, aps = {}, {}
    for name, a in _laid_out({k: np.asarray(v) for k, v in inputs.items()}).items():
        a = np.ascontiguousarray(a)
        arrays[f"in_{name}"] = a
        aps[name] = nc.dram_tensor(f"in_{name}", a.shape, mybir.dt.from_np(a.dtype), kind="ExternalInput").ap()
    out = nc.dram_tensor("out_x", (B, S, D), F32, kind="ExternalOutput").ap()
    build(nc, aps, out)
    r = run_bass_kernel_spmd(nc, [arrays], core_ids=[0])
    return r.results[0]["out_x"]
```
